# Optimizing a Trainium2 kernel written in Bass

```python
import numpy as np
import jax
import jax.numpy as jnp

def _softmax(x, axis=-1):
    return jax.nn.softmax(x, axis=axis)

def _gelu(x):
    return jax.nn.gelu(x, approximate=True)

def _silu(x):
    return jax.nn.silu(x)

def _sigmoid(x):
    return jax.nn.sigmoid(x)

def _layernorm(x, axis=-1, eps=1e-05):
    m = jnp.mean(x, axis=axis, keepdims=True)
    v = jnp.var(x, axis=axis, keepdims=True)
    return (x - m) / jnp.sqrt(v + eps)

def _scatter_add(tgt, idx, src, axis=0):
    return tgt.at[idx].add(src)

def _segment_sum(src, seg, n):
    return jax.ops.segment_sum(src, seg, n)
kernel_name = 'mk_early_fusion_d2_tok_img256_r4_e532ba'

def setup_inputs(seed: int=0):
    np.random.seed(seed)
    _w = jnp.asarray

    def _rec_inputs():
        import jax
        import jax.numpy as jnp
        _rk = jax.random.key(seed)
        x = -7.10856e-05 + 0.999911 * jax.random.normal(jax.random.fold_in(_rk, 1), (4, 64, 128, 64), jnp.float32)
        txt = -0.000161634 + 0.479995 * jax.random.normal(jax.random.fold_in(_rk, 2), (4, 77, 64), jnp.float32)
        return (x, txt)
    x, txt = _rec_inputs()

    def _L0_tok_setup():
        import jax, jax.numpy as jnp
        import numpy as np
        PATCH_LEN = 16
        STRIDE = 8
        PAD = 8
        key = jax.random.key(seed)
        k1, k2 = jax.random.split(key)
        x = jax.random.normal(k1, (32, 64, 128, 64), dtype=jnp.float32)
        in_feat = 64 * (PATCH_LEN // 2 + 1) * 2
        W = jax.random.normal(k2, (64, in_feat), dtype=jnp.float32) * 0.02
        return {'x': x, 'W': W}
    _L0_tok_all = _L0_tok_setup()
    _L0_tok_in = {k: v for k, v in _L0_tok_all.items() if k in ('W',)}
    del _L0_tok_all

    def _L0_attn_setup():
        import jax, jax.numpy as jnp
        import numpy as np

        def softcap(x, a=10.0):
            return a * jnp.tanh(x / a)
        key = jax.random.key(seed)
        B, T, D = (4, 512, 64)
        ks = jax.random.split(key, 5)
        w = lambda k, s: jax.random.normal(k, s, dtype=jnp.float32) * 0.02
        return {'x': jax.random.normal(ks[0], (B, T, D), dtype=jnp.float32), 'Wq': w(ks[1], (D, D)), 'bq': jnp.zeros((D,), jnp.float32), 'Wk': w(ks[2], (D, D)), 'bk': jnp.zeros((D,), jnp.float32), 'Wv': w(ks[3], (D, D)), 'bv': jnp.zeros((D,), jnp.float32), 'Wg': w(ks[4], (D, 3 * D)), 'bg': jnp.zeros((3 * D,), jnp.float32), 'input_bias': -jnp.ones((D,), jnp.float32), 'norm_scale': jnp.ones((D,), jnp.float32)}
    _L0_attn_all = _L0_attn_setup()
    _L0_attn_in = {k: v for k, v in _L0_attn_all.items() if k in ('Wq', 'bq', 'Wk', 'bk', 'Wv', 'bv', 'Wg', 'bg', 'input_bias', 'norm_scale')}
    del _L0_attn_all

    def _L0_ffn_setup():
        import jax, jax.numpy as jnp
        import numpy as np
        BN_EPS = 0.001

        def _bn(h, g, b, m, v):
            return g * (h - m) * jax.lax.rsqrt(v + BN_EPS) + b
        key = jax.random.key(seed)
        ks = jax.random.split(key, 8)
        B, F, Df = (64, 64, 64)
        E, H, D = (8, 64, 64)
        s1 = 1.0 / np.sqrt(Df)
        s2 = 1.0 / np.sqrt(H)
        return {'x': jax.random.normal(ks[0], (B, F, Df), jnp.float32), 'Wr': jax.random.normal(ks[1], (Df, E), jnp.float32) * s1, 'br': jnp.zeros((E,), jnp.float32), 'W1': jax.random.normal(ks[2], (E, Df, H), jnp.float32) * s1, 'b1': jnp.zeros((E, H), jnp.float32), 'g1': jnp.ones((E, H), jnp.float32), 'be1': jnp.zeros((E, H), jnp.float32), 'm1': jnp.zeros((E, H), jnp.float32), 'v1': jnp.ones((E, H), jnp.float32), 'W2': jax.random.normal(ks[3], (E, H, H), jnp.float32) * s2, 'b2': jnp.zeros((E, H), jnp.float32), 'g2': jnp.ones((E, H), jnp.float32), 'be2': jnp.zeros((E, H), jnp.float32), 'm2': jnp.zeros((E, H), jnp.float32), 'v2': jnp.ones((E, H), jnp.float32), 'Wo': jax.random.normal(ks[4], (E, H, D), jnp.float32) * s2, 'bo': jnp.zeros((E, D), jnp.float32)}
    _L0_ffn_all = _L0_ffn_setup()
    _L0_ffn_in = {k: v for k, v in _L0_ffn_all.items() if k in ('Wr', 'br', 'W1', 'b1', 'g1', 'be1', 'm1', 'v1', 'W2', 'b2', 'g2', 'be2', 'm2', 'v2', 'Wo', 'bo')}
    del _L0_ffn_all

    def _L1_attn_setup():
        import jax, jax.numpy as jnp
        import numpy as np
        D_MODEL = 64
        D_INNER = 128
        D_STATE = 32
        D_CONV = 4
        DT_RANK = 16
        H_MLP = 32
        BINS = 64
        B, L = (16, 512)

        def _mamba(x, W_in, conv_w, conv_b, W_xproj, W_dt, b_dt, A_log, D, W_out):
            Bsz, Ls, _ = x.shape
            xz = jnp.einsum('bld,ed->ble', x, W_in)
            xc, z = jnp.split(xz, 2, axis=-1)
            xp = jnp.pad(xc, ((0, 0), (D_CONV - 1, 0), (0, 0)))
            xconv = sum((xp[:, k:k + Ls, :] * conv_w[:, k] for k in range(D_CONV))) + conv_b
            u = jax.nn.silu(xconv)
            dbc = jnp.einsum('bld,ed->ble', u, W_xproj)
            dt_lo = dbc[..., :DT_RANK]
            Bm = dbc[..., DT_RANK:DT_RANK + D_STATE]
            Cm = dbc[..., DT_RANK + D_STATE:]
            dt = jax.nn.softplus(jnp.einsum('blr,dr->bld', dt_lo, W_dt) + b_dt)
            A = -jnp.exp(A_log)

            def step(h, t):
                dt_t, B_t, C_t, u_t = t
                h = h * jnp.exp(dt_t[:, :, None] * A) + (dt_t * u_t)[:, :, None] * B_t[:, None, :]
                y = jnp.einsum('bds,bs->bd', h, C_t)
                return (h, y)
            h0 = jnp.zeros((Bsz, D_INNER, D_STATE), x.dtype)
            xs = (dt.transpose(1, 0, 2), Bm.transpose(1, 0, 2), Cm.transpose(1, 0, 2), u.transpose(1, 0, 2))
            _, ys = jax.lax.scan(step, h0, xs)
            y = ys.transpose(1, 0, 2) + u * D
            y = y * jax.nn.silu(z)
            return jnp.einsum('bld,ed->ble', y, W_out)
        key = jax.random.key(seed)
        ks = jax.random.split(key, 10)
        n = lambda k, sh, s=0.02: jax.random.normal(k, sh, dtype=jnp.float32) * s
        return {'x': jax.random.normal(ks[0], (B, L, D_MODEL), dtype=jnp.float32), 'W_in': n(ks[1], (2 * D_INNER, D_MODEL)), 'conv_w': n(ks[2], (D_INNER, D_CONV), 0.1), 'conv_b': jnp.zeros((D_INNER,), jnp.float32), 'W_xproj': n(ks[3], (DT_RANK + 2 * D_STATE, D_INNER)), 'W_dt': n(ks[4], (D_INNER, DT_RANK), 0.1), 'b_dt': n(ks[5], (D_INNER,), 0.5), 'A_log': jnp.log(jnp.tile(jnp.arange(1, D_STATE + 1, dtype=jnp.float32), (D_INNER, 1))), 'D': jnp.ones((D_INNER,), jnp.float32), 'W_out': n(ks[6], (D_MODEL, D_INNER)), 'W_ff1': n(ks[7], (H_MLP, D_MODEL), 0.05), 'b_ff1': jnp.zeros((H_MLP,), jnp.float32), 'W_ff2': n(ks[8], (BINS, H_MLP), 0.05), 'b_ff2': jnp.zeros((BINS,), jnp.float32)}
    _L1_attn_all = _L1_attn_setup()
    _L1_attn_in = {k: v for k, v in _L1_attn_all.items() if k in ('W_in', 'conv_w', 'conv_b', 'W_xproj', 'W_dt', 'b_dt', 'A_log', 'D', 'W_out', 'W_ff1', 'b_ff1', 'W_ff2', 'b_ff2')}
    del _L1_attn_all

    def _L1_ffn_setup():
        import jax, jax.numpy as jnp
        import numpy as np
        B, S, D = (8, 1024, 64)
        H = 4 * D
        CAPACITY = 0.5
        key = jax.random.key(seed)
        ks = jax.random.split(key, 6)
        x = jax.random.normal(ks[0], (B, S, D), dtype=jnp.float32)
        attention_mask = jnp.zeros((B, 1, 1, S), dtype=jnp.float32)
        wr = jax.random.normal(ks[1], (D, 1), dtype=jnp.float32) * 0.02
        br = jnp.zeros((1,), dtype=jnp.float32)
        w1 = jax.random.normal(ks[2], (D, H), dtype=jnp.float32) * 0.02
        b1 = jnp.zeros((H,), dtype=jnp.float32)
        w2 = jax.random.normal(ks[3], (H, D), dtype=jnp.float32) * 0.02
        b2 = jnp.zeros((D,), dtype=jnp.float32)
        return {'x': x, 'attention_mask': attention_mask, 'wr': wr, 'br': br, 'w1': w1, 'b1': b1, 'w2': w2, 'b2': b2}
    _L1_ffn_all = _L1_ffn_setup()
    _L1_ffn_in = {k: v for k, v in _L1_ffn_all.items() if k in ('attention_mask', 'wr', 'br', 'w1', 'b1', 'w2', 'b2')}
    del _L1_ffn_all
    return {'x': x, 'txt': txt, 'L0_tok_W': _L0_tok_in['W'], 'L0_attn_Wq': _L0_attn_in['Wq'], 'L0_attn_bq': _L0_attn_in['bq'], 'L0_attn_Wk': _L0_attn_in['Wk'], 'L0_attn_bk': _L0_attn_in['bk'], 'L0_attn_Wv': _L0_attn_in['Wv'], 'L0_attn_bv': _L0_attn_in['bv'], 'L0_attn_Wg': _L0_attn_in['Wg'], 'L0_attn_bg': _L0_attn_in['bg'], 'L0_attn_input_bias': _L0_attn_in['input_bias'], 'L0_attn_norm_scale': _L0_attn_in['norm_scale'], 'L0_ffn_Wr': _L0_ffn_in['Wr'], 'L0_ffn_br': _L0_ffn_in['br'], 'L0_ffn_W1': _L0_ffn_in['W1'], 'L0_ffn_b1': _L0_ffn_in['b1'], 'L0_ffn_g1': _L0_ffn_in['g1'], 'L0_ffn_be1': _L0_ffn_in['be1'], 'L0_ffn_m1': _L0_ffn_in['m1'], 'L0_ffn_v1': _L0_ffn_in['v1'], 'L0_ffn_W2': _L0_ffn_in['W2'], 'L0_ffn_b2': _L0_ffn_in['b2'], 'L0_ffn_g2': _L0_ffn_in['g2'], 'L0_ffn_be2': _L0_ffn_in['be2'], 'L0_ffn_m2': _L0_ffn_in['m2'], 'L0_ffn_v2': _L0_ffn_in['v2'], 'L0_ffn_Wo': _L0_ffn_in['Wo'], 'L0_ffn_bo': _L0_ffn_in['bo'], 'L1_attn_W_in': _L1_attn_in['W_in'], 'L1_attn_conv_w': _L1_attn_in['conv_w'], 'L1_attn_conv_b': _L1_attn_in['conv_b'], 'L1_attn_W_xproj': _L1_attn_in['W_xproj'], 'L1_attn_W_dt': _L1_attn_in['W_dt'], 'L1_attn_b_dt': _L1_attn_in['b_dt'], 'L1_attn_A_log': _L1_attn_in['A_log'], 'L1_attn_D': _L1_attn_in['D'], 'L1_attn_W_out': _L1_attn_in['W_out'], 'L1_attn_W_ff1': _L1_attn_in['W_ff1'], 'L1_attn_b_ff1': _L1_attn_in['b_ff1'], 'L1_attn_W_ff2': _L1_attn_in['W_ff2'], 'L1_attn_b_ff2': _L1_attn_in['b_ff2'], 'L1_ffn_attention_mask': _L1_ffn_in['attention_mask'], 'L1_ffn_wr': _L1_ffn_in['wr'], 'L1_ffn_br': _L1_ffn_in['br'], 'L1_ffn_w1': _L1_ffn_in['w1'], 'L1_ffn_b1': _L1_ffn_in['b1'], 'L1_ffn_w2': _L1_ffn_in['w2'], 'L1_ffn_b2': _L1_ffn_in['b2']}

def reference(x, txt, L0_tok_W, L0_attn_Wq, L0_attn_bq, L0_attn_Wk, L0_attn_bk, L0_attn_Wv, L0_attn_bv, L0_attn_Wg, L0_attn_bg, L0_attn_input_bias, L0_attn_norm_scale, L0_ffn_Wr, L0_ffn_br, L0_ffn_W1, L0_ffn_b1, L0_ffn_g1, L0_ffn_be1, L0_ffn_m1, L0_ffn_v1, L0_ffn_W2, L0_ffn_b2, L0_ffn_g2, L0_ffn_be2, L0_ffn_m2, L0_ffn_v2, L0_ffn_Wo, L0_ffn_bo, L1_attn_W_in, L1_attn_conv_w, L1_attn_conv_b, L1_attn_W_xproj, L1_attn_W_dt, L1_attn_b_dt, L1_attn_A_log, L1_attn_D, L1_attn_W_out, L1_attn_W_ff1, L1_attn_b_ff1, L1_attn_W_ff2, L1_attn_b_ff2, L1_ffn_attention_mask, L1_ffn_wr, L1_ffn_br, L1_ffn_w1, L1_ffn_b1, L1_ffn_w2, L1_ffn_b2):
    import jax
    import jax.numpy as jnp

    def _L0_tok_ref(x, W):
        import jax, jax.numpy as jnp
        import numpy as np
        PATCH_LEN = 16
        STRIDE = 8
        PAD = 8
        B, C, T, V = x.shape
        xp = jnp.pad(x, ((0, 0), (0, 0), (0, PAD), (0, 0)), mode='edge')
        Tp = T + PAD
        N = (Tp - PATCH_LEN) // STRIDE + 1
        idx = jnp.arange(N)[:, None] * STRIDE + jnp.arange(PATCH_LEN)[None, :]
        patches = xp[:, :, idx, :]
        patches = jnp.transpose(patches, (0, 4, 2, 3, 1))
        xf = jnp.fft.rfft(patches, axis=-2, norm='ortho')
        F = xf.shape[-2]
        x_real = xf.real.reshape(B, V, N, F * C)
        x_imag = xf.imag.reshape(B, V, N, F * C)
        x_emb = jnp.concatenate([x_real, x_imag], axis=-1)
        x_emb = x_emb @ W.T
        return x_emb.reshape(B, V * N, -1)

    def _L0_attn_ref(x, Wq, bq, Wk, bk, Wv, bv, Wg, bg, input_bias, norm_scale):
        import jax, jax.numpy as jnp
        import numpy as np

        def softcap(x, a=10.0):
            return a * jnp.tanh(x / a)
        B, T, D = x.shape
        inv_sqrt_d = 1.0 / jnp.sqrt(jnp.asarray(D, jnp.float32))
        q = x @ Wq + bq
        k = (x @ Wk + bk) * inv_sqrt_d
        v = x @ Wv + bv
        gates = x @ Wg + bg
        i_pre, f_pre, o_pre = jnp.split(gates, 3, axis=-1)
        log_i = softcap(i_pre + input_bias)
        log_f = -jax.nn.softplus(f_pre)

        def step(carry, inp):
            M, n, m = carry
            qt, kt, vt, li, lf, op = inp
            m_next = jnp.maximum(lf + m, li)
            i_s = jnp.exp(li - m_next)
            f_s = jnp.exp(lf + m - m_next)
            M = f_s[:, :, None] * M + i_s[:, :, None] * (vt[:, :, None] * kt[:, None, :])
            n = f_s * n + i_s * kt
            h_raw = jnp.einsum('bij,bj->bi', M, qt)
            denom = jnp.maximum(jnp.abs(jnp.einsum('bi,bi->b', n, qt))[:, None], 1e-06)
            h = jax.nn.sigmoid(op) * (h_raw / denom)
            return ((M, n, m_next), h)
        M0 = jnp.zeros((B, D, D), jnp.float32)
        n0 = jnp.zeros((B, D), jnp.float32)
        m0 = jnp.zeros((B, D), jnp.float32)
        xs = tuple((jnp.swapaxes(a, 0, 1) for a in (q, k, v, log_i, log_f, o_pre)))
        _, hs = jax.lax.scan(step, (M0, n0, m0), xs)
        out = jnp.swapaxes(hs, 0, 1)
        rms = jnp.sqrt(jnp.mean(out * out, axis=-1, keepdims=True) + 1e-08)
        return out / rms * norm_scale

    def _L0_ffn_ref(x, Wr, br, W1, b1, g1, be1, m1, v1, W2, b2, g2, be2, m2, v2, Wo, bo):
        import jax, jax.numpy as jnp
        import numpy as np
        BN_EPS = 0.001

        def _bn(h, g, b, m, v):
            return g * (h - m) * jax.lax.rsqrt(v + BN_EPS) + b
        feat = jnp.mean(x, axis=0)
        w = jax.nn.softmax(feat @ Wr + br, axis=-1)
        h = jnp.einsum('bfd,edh->bfeh', x, W1) + b1
        h = jax.nn.relu(_bn(h, g1, be1, m1, v1))
        h = jnp.einsum('bfeh,ehk->bfek', h, W2) + b2
        h = jax.nn.relu(_bn(h, g2, be2, m2, v2))
        y = jnp.einsum('bfeh,ehd->bfed', h, Wo) + bo
        return jnp.einsum('bfed,fe->bfd', y, w)

    def _L1_attn_ref(x, W_in, conv_w, conv_b, W_xproj, W_dt, b_dt, A_log, D, W_out, W_ff1, b_ff1, W_ff2, b_ff2):
        import jax, jax.numpy as jnp
        import numpy as np
        D_MODEL = 64
        D_INNER = 128
        D_STATE = 32
        D_CONV = 4
        DT_RANK = 16
        H_MLP = 32
        BINS = 64
        B, L = (16, 512)

        def _mamba(x, W_in, conv_w, conv_b, W_xproj, W_dt, b_dt, A_log, D, W_out):
            Bsz, Ls, _ = x.shape
            xz = jnp.einsum('bld,ed->ble', x, W_in)
            xc, z = jnp.split(xz, 2, axis=-1)
            xp = jnp.pad(xc, ((0, 0), (D_CONV - 1, 0), (0, 0)))
            xconv = sum((xp[:, k:k + Ls, :] * conv_w[:, k] for k in range(D_CONV))) + conv_b
            u = jax.nn.silu(xconv)
            dbc = jnp.einsum('bld,ed->ble', u, W_xproj)
            dt_lo = dbc[..., :DT_RANK]
            Bm = dbc[..., DT_RANK:DT_RANK + D_STATE]
            Cm = dbc[..., DT_RANK + D_STATE:]
            dt = jax.nn.softplus(jnp.einsum('blr,dr->bld', dt_lo, W_dt) + b_dt)
            A = -jnp.exp(A_log)

            def step(h, t):
                dt_t, B_t, C_t, u_t = t
                h = h * jnp.exp(dt_t[:, :, None] * A) + (dt_t * u_t)[:, :, None] * B_t[:, None, :]
                y = jnp.einsum('bds,bs->bd', h, C_t)
                return (h, y)
            h0 = jnp.zeros((Bsz, D_INNER, D_STATE), x.dtype)
            xs = (dt.transpose(1, 0, 2), Bm.transpose(1, 0, 2), Cm.transpose(1, 0, 2), u.transpose(1, 0, 2))
            _, ys = jax.lax.scan(step, h0, xs)
            y = ys.transpose(1, 0, 2) + u * D
            y = y * jax.nn.silu(z)
            return jnp.einsum('bld,ed->ble', y, W_out)
        h = _mamba(x, W_in, conv_w, conv_b, W_xproj, W_dt, b_dt, A_log, D, W_out)
        h = jax.nn.leaky_relu(h @ W_ff1.T + b_ff1)
        return jax.nn.sigmoid(h @ W_ff2.T + b_ff2)

    def _L1_ffn_ref(x, attention_mask, wr, br, w1, b1, w2, b2):
        import jax, jax.numpy as jnp
        import numpy as np
        B, S, D = (8, 1024, 64)
        H = 4 * D
        CAPACITY = 0.5
        b, s, d = x.shape
        weights = (jnp.einsum('bsd,do->bso', x, wr) + br)[..., 0]
        k = max(1, int(CAPACITY * s))
        kk = k - 1 if k > 1 else 1
        _, idx = jax.lax.top_k(weights, k)
        sel_idx = idx[:, :kk]
        sel = jnp.take_along_axis(x, sel_idx[:, :, None], axis=1)
        h = jax.nn.gelu(jnp.einsum('bkd,dh->bkh', sel, w1) + b1)
        y = jnp.einsum('bkh,hd->bkd', h, w2) + b2
        w_sel = jnp.take_along_axis(weights, sel_idx, axis=1)
        y = y * w_sel[..., None]
        batch_idx = jnp.arange(b)[:, None]
        processed = jnp.zeros_like(x).at[batch_idx, sel_idx].set(y)
        return processed + x
    h = _L0_tok_ref(x, L0_tok_W)
    h = jnp.concatenate([h, txt], axis=1)
    h = h + _L0_attn_ref(_layernorm(h, axis=-1), L0_attn_Wq, L0_attn_bq, L0_attn_Wk, L0_attn_bk, L0_attn_Wv, L0_attn_bv, L0_attn_Wg, L0_attn_bg, L0_attn_input_bias, L0_attn_norm_scale)
    h = h + _L0_ffn_ref(_layernorm(h, axis=-1), L0_ffn_Wr, L0_ffn_br, L0_ffn_W1, L0_ffn_b1, L0_ffn_g1, L0_ffn_be1, L0_ffn_m1, L0_ffn_v1, L0_ffn_W2, L0_ffn_b2, L0_ffn_g2, L0_ffn_be2, L0_ffn_m2, L0_ffn_v2, L0_ffn_Wo, L0_ffn_bo)
    h = h + _L1_attn_ref(_layernorm(h, axis=-1), L1_attn_W_in, L1_attn_conv_w, L1_attn_conv_b, L1_attn_W_xproj, L1_attn_W_dt, L1_attn_b_dt, L1_attn_A_log, L1_attn_D, L1_attn_W_out, L1_attn_W_ff1, L1_attn_b_ff1, L1_attn_W_ff2, L1_attn_b_ff2)
    h = h + _L1_ffn_ref(_layernorm(h, axis=-1), L1_ffn_attention_mask, L1_ffn_wr, L1_ffn_br, L1_ffn_w1, L1_ffn_b1, L1_ffn_w2, L1_ffn_b2)
    return h

_drawn_inputs = setup_inputs


def setup_inputs(seed=0):
    import zlib

    import numpy as np

    out = dict(_drawn_inputs(seed))
    spreads = {'L0_attn_bq': (0.0, 0.1),
     'L0_attn_bk': (0.0, 0.1),
     'L0_attn_bv': (0.0, 0.1),
     'L0_attn_bg': (0.0, 0.1),
     'L0_attn_input_bias': (-1.0, 0.6),
     'L0_attn_norm_scale': (1.0, 0.2),
     'L0_ffn_br': (0.0, 0.335),
     'L0_ffn_b1': (0.0, 0.467),
     'L0_ffn_g1': (1.0, 0.2),
     'L0_ffn_be1': (0.0, 0.44),
     'L0_ffn_m1': (0.0, 0.482),
     'L0_ffn_v1': (1.0, 0.6),
     'L0_ffn_b2': (0.0, 0.332),
     'L0_ffn_g2': (1.0, 0.2),
     'L0_ffn_be2': (0.0, 0.372),
     'L0_ffn_m2': (0.0, 0.317),
     'L0_ffn_v2': (1.0, 0.6),
     'L0_ffn_bo': (0.0, 0.1),
     'L1_attn_conv_b': (0.0, 0.8),
     'L1_attn_D': (1.0, 0.6),
     'L1_attn_b_ff1': (0.0, 0.8),
     'L1_attn_b_ff2': (0.0, 0.409),
     'L1_ffn_b1': (0.0, 0.8),
     'L1_ffn_b2': (0.0, 0.8)}
    factors = {'L1_attn_W_in': 8.0,
     'L1_attn_conv_w': 8.0,
     'L1_attn_W_xproj': 8.0,
     'L1_attn_W_dt': 8.0,
     'L1_attn_b_dt': 8.0,
     'L1_attn_A_log': 8.0,
     'L1_attn_W_out': 8.0,
     'L1_attn_W_ff1': 8.0,
     'L1_attn_W_ff2': 8.0,
     'L1_ffn_wr': 8.0,
     'L1_ffn_w1': 8.0,
     'L1_ffn_w2': 8.0}
    for name, (base, spread) in spreads.items():
        noise = np.random.default_rng([zlib.crc32(name.encode()), seed]).standard_normal(out[name].shape)
        drawn = base * np.exp(spread * noise) if base else spread * noise
        out[name] = jnp.asarray(drawn.astype(out[name].dtype))
    for name, factor in factors.items():
        out[name] = (out[name] * factor).astype(out[name].dtype)
    return out
```

```python
import math
from contextlib import ExitStack

import numpy as np

import concourse.bass as bass
from concourse import mybir

F32 = mybir.dt.float32
BF16 = mybir.dt.bfloat16
ALU = mybir.AluOpType
ACT = mybir.ActivationFunctionType
AX_X = mybir.AxisListType.X

B, C, T, V = 4, 64, 128, 64
D = 64
PATCH, STRIDE, PAD = 16, 8, 8
NP_ = (T + PAD - PATCH) // STRIDE + 1
NF = PATCH // 2 + 1
TXT = 77
TOK = V * NP_
S = TOK + TXT
NPAIR = B // 2
L = 16
NC = -(-S // L)
SP = NC * L
NG = 3
G = SP // NG
CG = NC // NG
E = 8
DI, DS, DTR, KC = 128, 32, 16, 4
HM = 32
HF = 256
KEEP = max(1, int(0.5 * S)) - 1
NT = -(-S // 128)
LAST = S - 128 * (NT - 1)
LASTP = SP - 128 * (NT - 1)
RMS_SCALE = 2.0 ** -30
EDGE = 2.0 ** -7
assert G <= 512 and NC % NG == 0 and SP == NG * G


OG = 7
NOG = -(-D // OG)
WEIGHTS = [("Wq", 128), ("Wk", 128), ("Wv", 128), ("Wi", 128), ("Wf", 128), ("Wo", 128), ("Wr", E), ("ebias", 128),
           ("Win", 4 * DI), ("XB", 128), ("XC", 128), ("XD", 128), ("WdtT", DI), ("WoutT", 2 * 128), ("FF1", 128),
           ("FF2", 128), ("wr", 2 * 128), ("w1", 2 * HF), ("w2", 2 * D), ("ident", 128), ("ones", 128),
           ("cmask", 128 // L), ("eyes", DS), ("before", 128), ("after", 128), ("b2row", D), ("brow", E), ("A_log", DS),
           ("conv_w", KC), ("cols", 16)]
EXPERTS = [("E1", E * 128), ("E2", E * 128), ("E3", E * 128)]
COLS = ["bq", "bk", "bv", "bi", "bf", "bo", "ib", "ns", "br", "conv_b", "b_dt", "Dm", "ff1b", "ff2b", "b1a", "b1b"]
BN = ["b1", "b2", "g1", "g2", "be1", "be2", "m1", "m2", "v1", "v2"]


def places(sizes):
    at, out = 0, {}
    for name, n in sizes:
        out[name] = (at, n)
        at += n
    return out, at


def build(nc, x, txt, wdft, wts, wexp, bn, out, dbg=None):
    lay, nw = places(WEIGHTS)
    elay, ne = places(EXPERTS)
    with ExitStack() as ctx:
        def sb(name, shape, dt=F32):
            return ctx.enter_context(nc.sbuf_tensor(name, shape, dt))

        sems = {}

        def s(name):
            if name not in sems:
                sems[name] = ctx.enter_context(nc.semaphore(name))
            return sems[name]

        PS = ctx.enter_context(nc.psum_tensor("PS", [128, 8, 512], F32))
        W_ = sb("weights", [128, nw])

        def w(name):
            a, n = lay[name]
            return W_[:, a:a + n]

        def col(name):
            a = lay["cols"][0] + COLS.index(name)
            return W_[:, a:a + 1]

        H = sb("hidden", [128, NPAIR, SP])
        pool_ = sb("pair_arrays", [128, 10, NPAIR, SP])
        P1, P2, P3, P4, P5, P6, P7, P8, P9, P10 = (pool_[:, i] for i in range(10))
        big = sb("big", [128, 2 * NPAIR * D * NC])
        Wt = sb("token_weights", [128, PATCH * 128])
        bnw = sb("bn_params", [128, len(BN), E])
        bns = sb("bn_scale", [128, 2, E])
        bnb = sb("bn_shift", [128, 2, E])
        cst = sb("constants", [128, 6])
        EPS5, EPS8, ONE, EPS3, HALF_LN, LN_EDGE = (cst[:, i:i + 1] for i in range(6))
        gbias = sb("gate_bias", [128, 2])
        txt_sb = sb("txt_rows", [TXT, B * D])
        dend = sb("chunk_decay", [128, NPAIR, NC])
        aneg = sb("A_negative", [128, DS])
        wcol = sb("router_cols", [128, B, NT])
        one_bf = sb("ones_bf16", [128, 1], BF16)
        sel = sb("selected", [128, B * NT])
        ytmp = sb("y_rows", [128, 2, D])
        dram_decay = nc.dram_tensor("decay_rows", [NPAIR, 2, D * NC], F32, kind="Internal").ap()

        xs = big[:, 0:NPAIR * (T + PAD) * V].rearrange("p (a t v) -> p a t v", a=NPAIR, t=T + PAD)
        wd = P1.rearrange("p a t -> p (a t)")[:, 0:NOG * 128]
        dft = P1.rearrange("p a t -> p (a t)")[:, NOG * 128:NOG * 128 + OG * PATCH]
        q_, k_, v_, li, r_, so, lf, m_, fs = P2, P3, P4, P5, P6, P7, P8, P9, P10
        ik, n_, rden = P1, P6, P9
        WV = [P4, P8]
        ve, dfw, hr = P1, P5, P6
        DBC = big[:, 0:NPAIR * D * NC].rearrange("p (a n) -> p a n", a=NPAIR)
        UM = big[:, NPAIR * D * NC:].rearrange("p (a n) -> p a n", a=NPAIR)
        UMc = big[:, NPAIR * D * NC:].rearrange("p (a i c) -> p a i c", a=NPAIR, i=D)
        lagmem = big[:, NPAIR * D * NC:]
        prod = [lagmem[:, i * SP:(i + 1) * SP] for i in range(4)]
        term = [lagmem[:, (4 + i) * SP:(5 + i) * SP] for i in range(2)]
        rows_t = [Wt[:, i * 256:(i + 1) * 256] for i in range(2)]
        spread = [Wt[:, 512 + i * 512:1024 + i * 512] for i in range(2)]
        NL = NPAIR * L
        EW = big[:, 0:ne]

        def ew(name, e):
            a = elay[name][0] + e * 128
            return EW[:, a:a + 128]

        def twin(a, i):
            return a.rearrange("p a t -> p (a t)")[:, i * NPAIR * G:(i + 1) * NPAIR * G].rearrange("p (a t) -> p a t", a=NPAIR)

        h1b, h2b, hwb = P2, P3, P4
        gate = P6.rearrange("p a t -> p (a t)")
        lg = gate[:, 0:NT * E].rearrange("p (j e) -> p j e", e=E)
        gmax, gsum = gate[:, 128:128 + NT], gate[:, 160:160 + NT]
        wT = P5[:, 0, :]
        pick8 = big[:, ne:ne + E * 128]
        tstart = [min(128 * j, SP - 128) for j in range(NT)]
        def batch_array(i, b):
            return big[:, (4 * i + b) * SP:(4 * i + b + 1) * SP]

        assert 16 * SP <= 2 * NPAIR * D * NC
        SBC = [(P4, P5)[b // 2].rearrange("p a t -> p (a t)").bitcast(BF16)
               .rearrange("p (b h t) -> p b h t", b=2, h=2)[:, b % 2] for b in range(B)]
        pick = Wt[:, :].bitcast(BF16)
        diagD = sb("D_diagonal", [128, 128])
        dlo_sb = sb("dt_low_rank", [128, 2, G])
        xcp = [a.rearrange("p a t -> p (a t)") for a in (P6, P7)]
        conv = [P8[:, i] for i in range(2)]
        dlo = [dlo_sb[:, i, :] for i in range(2)]
        resid = [P6, P7]
        expo, frelu, logs = (P8, P9), (P1, P10), (P2, P3)
        hbuf, hcbuf, cbuf = ([a[:, i] for i in range(2)] for a in (P6, P7, P8))
        bx = [P9[:, 0, i * G:(i + 1) * G] for i in range(2)]
        wrow = [(P5, P6)[b // 2][:, b % 2] for b in range(B)]
        hid = [P7, P8]
        RES = big[:, 0:B * NT * D].rearrange("p (b j d) -> p b j d", b=B, j=NT)
        beats = [big[:, 4096 + i * 640:4096 + i * 640 + SP // 2].bitcast(BF16) for i in range(2)]
        beats_own = [big[:, 5400 + i * 64:5464 + i * 64].bitcast(BF16) for i in range(2)]
        rank_row = big[0:1, 6144:6144 + B * SP].rearrange("p (b t) -> p b t", b=B)
        BANKS = [(0, 512), (512, 1024), (1024, S)]

        groups = [(p, k) for p in range(NPAIR) for k in range(NG)]
        NGR = len(groups)

        def cols(k):
            return slice(k * G, (k + 1) * G)

        def half(b):
            return slice(64 * (b % 2), 64 * (b % 2) + 64)

        def chunks(a):
            return a.rearrange("p (c r) -> p c r", r=L)

        def stepper(eng, name):
            n = [0]

            def step(ins):
                n[0] += 1
                ins.then_inc(s(name), 1)
                eng.wait_ge(s(name), n[0])
            return step

        def seq_of(e):
            return e * 128, min(128, SP - e * 128)

        def ln_pe(pe, n, ready, sq):
            for g in range(NGR + 1):
                if g < NGR:
                    p, k = groups[g]
                    ready(g)
                    if g >= 2:
                        pe.wait_ge(s(f"ln{n}_centred"), g - 1)
                    nc.tensor.matmul(PS[:, g % 2, 0:G], w("ones"), H[:, p, cols(k)],
                                     start=True, stop=True).then_inc(s(f"ln{n}_mean"), 1)
                if g >= 1:
                    p, k = groups[g - 1]
                    pe.wait_ge(s(f"ln{n}_sq"), g)
                    if g >= 3:
                        pe.wait_ge(s(f"ln{n}_ln"), g - 2)
                    nc.tensor.matmul(PS[:, 2 + (g - 1) % 2, 0:G], w("ones"), sq[:, p, cols(k)],
                                     start=True, stop=True).then_inc(s(f"ln{n}_var"), 1)

        def ln_act(act, n, xc, sq, rs):
            for g in range(NGR + 1):
                if g < NGR:
                    p, k = groups[g]
                    act.wait_ge(s(f"ln{n}_centred"), g + 1)
                    nc.scalar.activation(sq[:, p, cols(k)], xc[:, p, cols(k)], ACT.Square).then_inc(s(f"ln{n}_sq"), 1)
                if g >= 1:
                    p, k = groups[g - 1]
                    act.wait_ge(s(f"ln{n}_var"), g)
                    nc.scalar.activation(rs[:, p, cols(k)], PS[:, 2 + (g - 1) % 2, 0:G], ACT.Ln, bias=EPS5,
                                         scale=1.0 / D).then_inc(s(f"ln{n}_ln"), 1)
            act.wait_ge(s(f"ln{n}_ln"), NGR)
            for p, k in groups:
                nc.scalar.activation(rs[:, p, cols(k)], rs[:, p, cols(k)], ACT.Exp,
                                     scale=-0.5).then_inc(s(f"ln{n}_rs"), 1)

        def ln_dve(dve, n, xc, rs):
            for g, (p, k) in enumerate(groups):
                dve.wait_ge(s(f"ln{n}_mean"), g + 1)
                nc.vector.scalar_tensor_tensor(xc[:, p, cols(k)], PS[:, g % 2, 0:G], -1.0 / D, H[:, p, cols(k)],
                                               ALU.mult, ALU.add).then_inc(s(f"ln{n}_centred"), 1)
            for g, (p, k) in enumerate(groups):
                dve.wait_ge(s(f"ln{n}_rs"), g + 1)
                nc.vector.tensor_tensor(xc[:, p, cols(k)], xc[:, p, cols(k)], rs[:, p, cols(k)],
                                        ALU.mult).then_inc(s(f"ln{n}_out"), 1)

        block = ctx.enter_context(nc.Block())

        @block.sync
        def _(sp):
            sp.dma_start(P1.rearrange("p a t -> p (a t)")[:, 0:NOG * 128 + OG * PATCH], wdft).then_inc(s("w_dft_in"), 16)
            xv = x.rearrange("(a b) c t v -> a (b c) t v", a=NPAIR)
            split = T // 2 + PAD
            for p in range(NPAIR):
                sp.dma_start(xs[:, p, 0:split, :], xv[p, :, 0:split, :]).then_inc(s(f"x_low{p}"), 16)
                sp.dma_start(xs[:, p, split:T, :], xv[p, :, split:, :]).then_inc(s(f"x_high{p}"), 16)
                if p == 0:
                    sp.dma_start(W_[:, :], wts).then_inc(s("w_in"), 16)
                    sp.dma_start(txt_sb[:, :].rearrange("t (b d) -> t b d", b=B),
                                 txt.rearrange("b t d -> t b d")).then_inc(s("txt_in"), 16)
            sp.dma_start(bnw[:, :, :].rearrange("p a b -> p (a b)"), bn).then_inc(s("bn_in"), 16)
            sp.wait_ge(s("dend_ready"), 1)
            for p in range(NPAIR):
                sp.dma_start(dram_decay[p].rearrange("b (i c) -> (b i) c", i=D),
                             dend[:, p, :]).then_inc(s("dend_out"), 16)
            sp.wait_ge(s("dend_out"), 16 * NPAIR)
            sp.wait_ge(s("tok_ps"), 4)
            for p in range(NPAIR):
                for b2 in range(2):
                    sp.dma_start(DBC[64 * b2:64 * b2 + 64, p, :],
                                 dram_decay[p, b2:b2 + 1, :].to_broadcast([64, D * NC])).then_inc(s("decay_in"), 16)
            sp.wait_ge(s("states"), NPAIR)
            sp.dma_start(EW, wexp).then_inc(s("experts_in"), 16)
            for b in range(B):
                sp.wait_ge(s("rows_ready"), (b + 1) * NT)
                sp.dma_start(out[b, 0:128 * (NT - 1), :].rearrange("(j p) d -> p j d", p=128),
                             RES[:, b, 0:NT - 1, :]).then_inc(s("out_done"), 16)
                sp.dma_start(out[b, 128 * (NT - 1):S, :], RES[0:LAST, b, NT - 1, :]).then_inc(s("out_done"), 16)
            sp.wait_ge(s("out_done"), 32 * B)

        @block.tensor
        def _(pe):
            pe.wait_ge(s("w_dft_in"), 16)
            for g in range(NOG):
                last = nc.tensor.matmul(PS[:, 4 + g // 4, (g % 4) * OG * PATCH:(g % 4 + 1) * OG * PATCH],
                                        wd[:, g * 128:(g + 1) * 128], dft, start=True, stop=True)
            last.then_inc(s("wtok_ps"), 1)
            pe.wait_ge(s("wtok_sb"), 6)
            for p in range(NPAIR):
                for hf in range(2):
                    pe.wait_ge(s(f"x_low{p}"), 16)
                    if hf:
                        pe.wait_ge(s(f"x_high{p}"), 16)
                        pe.wait_ge(s("x_pad"), p + 1)
                    for t in range(PATCH):
                        t0 = hf * 64 + t
                        last = nc.tensor.matmul(PS[:, 2 * p + hf, :], Wt[:, t * 128:(t + 1) * 128],
                                                xs[:, p, t0:t0 + 57:STRIDE, :], start=(t == 0), stop=(t == PATCH - 1))
                    last.then_inc(s("tok_ps"), 1)
            pe.wait_ge(s("w_in"), 16)
            pe.wait_ge(s("txt_in"), 16)
            for p in range(NPAIR):
                last = nc.tensor.transpose(PS[:, 7, p * TXT:(p + 1) * TXT], txt_sb[:, p * 128:(p + 1) * 128],
                                           w("ident")[0:TXT, 0:TXT])
            last.then_inc(s("txt_ps"), 1)

            def ready1(g):
                if g == 0:
                    pe.wait_ge(s("tok_ev"), 4)
                    pe.wait_ge(s("txt_ev"), 2)
            ln_pe(pe, 1, ready1, P2)

            for r, (wa, wv) in enumerate((("Wi", "Wq"), ("Wf", "Wk"), ("Wo", "Wv"))):
                for g, (p, k) in enumerate(groups):
                    m = r * NGR + g
                    pe.wait_ge(s("ln1_out"), g + 1)
                    if m >= 2:
                        pe.wait_ge(s("gates_ev"), m - 1)
                    nc.tensor.matmul(PS[:, 4 + m % 2, 0:G], w(wa), P1[:, p, cols(k)],
                                     start=True, stop=True).then_inc(s("gates_ps"), 1)
                    if m >= 2:
                        pe.wait_ge(s("qkv_ev"), m - 1)
                    nc.tensor.matmul(PS[:, 6 + m % 2, 0:G], w(wv), P1[:, p, cols(k)],
                                     start=True, stop=True).then_inc(s("qkv_ps"), 1)
            pe.wait_ge(s("qkv_ev"), 3 * NGR)
            for g, (p, k) in enumerate(groups):
                pe.wait_ge(s("nq_ready"), p + 1)
                if g >= 2:
                    pe.wait_ge(s("den_ev"), g - 1)
                nc.tensor.matmul(PS[:, 6 + g % 2, 0:G], w("ones"), ik[:, p, cols(k)],
                                 start=True, stop=True).then_inc(s("den_ps"), 1)
            pe.wait_ge(s("gates_ev"), 3 * NGR)
            for n in range(NL):
                lag, p = n // NPAIR, n % NPAIR
                size = CG * (L - lag)
                pe.wait_ge(s("lag_prod"), n + 1)
                if n >= NPAIR:
                    pe.wait_ge(s("lag_read"), n - 1)
                for k in range(NG):
                    last = nc.tensor.matmul(PS[:, NG * p + k, 0:size], w("ones"), prod[n % 4][:, k * size:(k + 1) * size],
                                            start=True, stop=True)
                last.then_inc(s("lag_ps"), 1)
            pe.wait_ge(s("lag_ve"), NL)
            pe.wait_ge(s("den_ev"), NGR)
            pe.wait_ge(s("lag_read"), NL)

            def turn(u):
                p, (t0, n) = u // NT, seq_of(u % NT)
                if u >= 2:
                    pe.wait_ge(s("rows_ev"), u - 1)
                nc.tensor.transpose(PS[0:n, 6 + u % 2, 0:128], ve[:, p, t0:t0 + n], w("ident"))
                nc.tensor.transpose(PS[0:n, 6 + u % 2, 128:256], k_[:, p, t0:t0 + n], w("ident")).then_inc(s("rows_ps"), 1)

            turn(0)
            for u in range(NPAIR * NT):
                n = seq_of(u % NT)[1]
                if u + 1 < NPAIR * NT:
                    turn(u + 1)
                for b2 in range(2):
                    y = 2 * u + b2
                    pe.wait_ge(s("spread_ready"), y + 1)
                    if y >= 4:
                        pe.wait_ge(s("u_ev"), y - 3)
                    nc.tensor.matmul(PS[:, y % 4, 0:n // L * D], rows_t[u % 2][0:n, 128:256], spread[b2][0:n, 0:n // L * D],
                                     start=True, stop=True).then_inc(s("u_mm"), 1)
            pe.wait_ge(s("u_ev"), 4 * NT)
            for p in range(NPAIR):
                pe.wait_ge(s("states"), p + 1)
                for c in range(1, NC):
                    for b2 in range(2):
                        h = half(b2)
                        last = nc.tensor.matmul(PS[h, NG * p + c // CG, (c % CG) * L:(c % CG + 1) * L],
                                                UMc[h, p, :, c - 1], q_[h, p, c * L:(c + 1) * L], start=True, stop=True)
                last.then_inc(s("inter_ps"), 1)
            for g, (p, k) in enumerate(groups):
                pe.wait_ge(s("msq_in"), p + 1)
                if g >= 2:
                    pe.wait_ge(s("rms_ev"), g - 1)
                nc.tensor.matmul(PS[:, 6 + g % 2, 0:G], w("ones"), WV[1][:, p, cols(k)],
                                 start=True, stop=True).then_inc(s("msq_ps"), 1)

            def ready2(g):
                pe.wait_ge(s("mlstm_out"), g + 1)
                if g == 0:
                    pe.wait_ge(s("inter_ev"), NPAIR)
            ln_pe(pe, 2, ready2, P2)

            pe.wait_ge(s("ln2_out"), NGR)
            for j in range(NT):
                for p in range(NPAIR):
                    last = nc.tensor.matmul(PS[:, 4, j * E:(j + 1) * E], P1[:, p, tstart[j]:tstart[j] + 128], w("Wr"),
                                            start=(p == 0), stop=(p == NPAIR - 1))
            last.then_inc(s("logit_ps"), 1)
            pe.wait_ge(s("gate_ready"), 1)
            for j in range(NT):
                last = nc.tensor.transpose(PS[0:E, 5 + j // 4, (j % 4) * 128:(j % 4 + 1) * 128], lg[:, j, :], w("ident"))
            last.then_inc(s("gateT_ps"), 1)
            pe.wait_ge(s("experts_in"), 16)
            pe.wait_ge(s("gateT"), 2)
            pe.wait_ge(s("ln2_ln"), NGR)
            NX = NG * E

            def layer1(n):
                if n >= 1:
                    pe.wait_ge(s("h1_ev"), n)
                for p in range(NPAIR):
                    last = nc.tensor.matmul(PS[:, 2 + p, 0:G], ew("E1", n % E), P1[:, p, cols(n // E)],
                                            start=True, stop=True)
                last.then_inc(s("l1_ps"), 1)

            def layer2(n):
                pe.wait_ge(s("h1_ev"), n + 1)
                if n >= 1:
                    pe.wait_ge(s("h2_ev"), n)
                for p in range(NPAIR):
                    last = nc.tensor.matmul(PS[:, 4 + p, 0:G], ew("E2", n % E), twin(h1b, n % 2)[:, p, :],
                                            start=True, stop=True)
                last.then_inc(s("l2_ps"), 1)

            def spread_weight(n):
                if n >= 2:
                    pe.wait_ge(s("hw_ready"), n - 1)
                nc.tensor.matmul(PS[:, 6 + n % 2, 0:G], pick8[:, (n % E) * 128:(n % E + 1) * 128], wT[:, cols(n // E)],
                                 start=True, stop=True).then_inc(s("spread_w"), 1)

            def layer3(n):
                k, e = n // E, n % E
                pe.wait_ge(s("hw_ready"), n + 1)
                if e == 0 and k >= 1:
                    pe.wait_ge(s("ffn_out"), k)
                for p in range(NPAIR):
                    last = nc.tensor.matmul(PS[:, p, 0:G], ew("E3", e), twin(hwb, n % 2)[:, p, :],
                                            start=(e == 0), stop=False)
                    if e == E - 1:
                        last = nc.tensor.matmul(PS[:, p, 0:G], w("ebias"), wT[:, cols(k)], start=False, stop=True)
                last.then_inc(s("l3_ps"), 1)

            layer1(0)
            spread_weight(0)
            for n in range(NX):
                layer2(n)
                if n + 1 < NX:
                    layer1(n + 1)
                    spread_weight(n + 1)
                if n >= 1:
                    layer3(n - 1)
            layer3(NX - 1)

            def ready3(g):
                pe.wait_ge(s("ffn_out"), g % NG + 1)
                if g == 0:
                    pe.wait_ge(s("ffn_out"), NG)
            ln_pe(pe, 3, ready3, P2)

            pe.wait_ge(s("ln3_out"), NGR)
            for m in range(B * NG):
                b, k = m // NG, m % NG
                xin = P1[:, b // 2, cols(k)]
                win = w("Win")[:, (b % 2) * 2 * DI:(b % 2 + 1) * 2 * DI]
                if m >= 2:
                    pe.wait_ge(s("xc_ev"), m - 1)
                nc.tensor.matmul(PS[:, m % 2, 0:G], win[:, 0:DI], xin, start=True, stop=True).then_inc(s("xc_ps"), 1)
                if m >= 2:
                    pe.wait_ge(s("z_ev"), m - 1)
                nc.tensor.matmul(PS[:, 2 + m % 2, 0:G], win[:, DI:2 * DI], xin,
                                 start=True, stop=True).then_inc(s("z_ps"), 1)
            pe.wait_ge(s("xc_ev"), B * NG)
            pe.wait_ge(s("z_ev"), B * NG)
            for m in range(B * NG + 1):
                if m < B * NG:
                    b, k = m // NG, m % NG
                    u = batch_array(0, b)[:, cols(k)]
                    pe.wait_ge(s("u_ready"), b + 1)
                    if m >= 2:
                        pe.wait_ge(s("bc_left"), m - 1)
                        pe.wait_ge(s("dlo_ev"), m - 1)
                    nc.tensor.matmul(PS[:, 4 + m % 2, 0:G], w("XD"), u, start=True, stop=True).then_inc(s("dlo_ps"), 1)
                    nc.tensor.matmul(PS[:, 2 * (m % 2), 0:G], w("XB"), u, start=True, stop=True)
                    nc.tensor.matmul(PS[:, 2 * (m % 2) + 1, 0:G], w("XC"), u, start=True, stop=True).then_inc(s("bc_ps"), 1)
                if m >= 1:
                    pe.wait_ge(s("dlo_ev"), m)
                    if m >= 3:
                        pe.wait_ge(s("dt_abs"), m - 2)
                        pe.wait_ge(s("dt_relu"), m - 2)
                    nc.tensor.matmul(PS[:, 6 + (m - 1) % 2, 0:G], w("WdtT"), dlo[(m - 1) % 2],
                                     start=True, stop=True).then_inc(s("dt_ps"), 1)
            pe.wait_ge(s("pick_ready"), 1)
            pe.wait_ge(s("bc_ready"), B)
            pe.wait_ge(s("dt_abs"), B * NG)
            pe.wait_ge(s("dt_relu"), B * NG)
            pe.wait_ge(s("diag_ready"), 1)

            def tile_work(b, i, half_, first, add=None):
                picked = pick[:, bass.ds((i * 2 + (half_ - DS * b)) * 128, 128)]
                for k in range(NG):
                    m = NG * half_ + k
                    early = first and b == 0
                    if not (early and m < 2):
                        pe.wait_ge(s("b_used"), i * (2 * NG) + (m - 1))
                    nc.tensor.matmul(PS[:, 3 + m % 2, 0:G], picked, SBC[b][:, 0, cols(k)],
                                     start=True, stop=True).then_inc(s("b_spread"), 1)
                    if not (early and m < 1):
                        pe.wait_ge(s("c_copied"), i * (2 * NG) + m)
                    nc.tensor.matmul(PS[:, 5, 0:G], picked, SBC[b][:, 1, cols(k)],
                                     start=True, stop=True).then_inc(s("c_spread"), 1)
                    if add is not None:
                        add_y(add, half_, k)

            def add_y(i, half_, k, stop=False):
                if k == 0:
                    pe.wait_ge(s("hc_ready"), i * 2 + (half_ + 1))
                last = nc.tensor.matmul(PS[:, k, 0:G], w("ident"), hcbuf[half_][:, cols(k)], start=False, stop=stop,
                                        skip_group_check=True)
                if k == NG - 1:
                    last.then_inc(s("y_added"), 1)

            for b in range(B):
                i0 = b * DS // 2
                if b >= 1:
                    for half_ in range(2):
                        tile_work(b, i0, half_, True, None)
                        for k in range(NG):
                            add_y(i0 - 1, half_, k, stop=(half_ == 1))
                    pe.wait_ge(s("ys_ready"), b)
                else:
                    tile_work(b, i0, 0, True)
                    tile_work(b, i0, 1, True)
                for k in range(NG):
                    nc.tensor.matmul(PS[:, k, 0:G], diagD[:, :], batch_array(0, b)[:, cols(k)], start=True, stop=False,
                                     skip_group_check=True)
                with pe.Fori(i0 + 1, i0 + DS // 2) as i:
                    tile_work(b, i, 0, False, i - 1)
                    tile_work(b, i, 1, False, i - 1)
            for half_ in range(2):
                for k in range(NG):
                    add_y(B * DS // 2 - 1, half_, k, stop=(half_ == 1))
            pe.wait_ge(s("ys_ready"), B)
            for g in range(NGR + 2):
                if g < NGR:
                    p, k = groups[g]
                    if g >= 2:
                        pe.wait_ge(s("mo_ev"), g - 1)
                    for b2 in range(2):
                        last = nc.tensor.matmul(PS[:, g % 2, 0:G], w("WoutT")[:, b2 * 128:(b2 + 1) * 128],
                                                batch_array(3, 2 * p + b2)[:, cols(k)], start=(b2 == 0), stop=(b2 == 1))
                    last.then_inc(s("mo_ps"), 1)
                if 1 <= g <= NGR:
                    p, k = groups[g - 1]
                    pe.wait_ge(s("mo_ev"), g)
                    if g >= 3:
                        pe.wait_ge(s("ff1_ev"), g - 2)
                    nc.tensor.matmul(PS[:, 2 + (g - 1) % 2, 0:G], w("FF1"), P1[:, p, cols(k)],
                                     start=True, stop=True).then_inc(s("ff1_ps"), 1)
                if g >= 2:
                    p, k = groups[g - 2]
                    pe.wait_ge(s("ff1_out"), g - 1)
                    if g >= 4:
                        pe.wait_ge(s("ff2_ev"), g - 3)
                    nc.tensor.matmul(PS[:, 4 + g % 2, 0:G], w("FF2"), P3[:, p, cols(k)],
                                     start=True, stop=True).then_inc(s("ff2_ps"), 1)

            def ready4(g):
                pe.wait_ge(s("mamba_out"), g + 1)
            ln_pe(pe, 4, ready4, P2)

            pe.wait_ge(s("ln4_out"), NGR)
            for m in range(B * NG):
                b, k = m // NG, m % NG
                if m >= 2:
                    pe.wait_ge(s("wrow_ev"), m - 1)
                nc.tensor.matmul(PS[:, m % 2, 0:G], w("wr")[:, (b % 2) * 128:(b % 2 + 1) * 128], P1[:, b // 2, cols(k)],
                                 start=True, stop=True).then_inc(s("wrow_ps"), 1)
            pe.wait_ge(s("wrow_ev"), B * NG)
            for b in range(B):
                for j in range(NT):
                    t0, n = j * 128, (128 if j < NT - 1 else LAST)
                    last = nc.tensor.transpose(PS[0:n, 2, b * NT + j:b * NT + j + 1], wrow[b][0:1, t0:t0 + n],
                                               w("ident")[0:1, 0:1])
            last.then_inc(s("wcol_ps"), 1)
            def rank_bank(b, i):
                return (3 + i) if b % 2 == 0 else (6, 7, 0)[i]

            def own_first(x_, b, n):
                return nc.tensor.matmul(PS[0:1, rank_bank(b, 0), 0:n], one_bf[0:n, :], beats_own[x_ % 2][0:n, 0:n],
                                        start=False, stop=False)

            for b in range(B):
                for j in range(NT):
                    x_ = b * NT + j
                    n = 128 if j < NT - 1 else LAST
                    pe.wait_ge(s("beats_ready"), x_ + 1)
                    if b >= 2 and j == 0:
                        pe.wait_ge(s("rank_ev"), b - 1)

                    def own():
                        nc.tensor.matmul(PS[0:1, rank_bank(b, j // 4), (j % 4) * 128:(j % 4) * 128 + n], one_bf[0:n, :],
                                         beats_own[x_ % 2][0:n, 0:n], start=False, stop=False)
                    if j:
                        own()
                    for i, (a, z) in enumerate(BANKS):
                        last = nc.tensor.matmul(PS[0:1, rank_bank(b, i), 0:z - a], one_bf[0:n, :], beats[x_ % 2][0:n, a:z],
                                                start=(j == 0), stop=(j == NT - 1))
                    if j == 0:
                        last = own_first(x_, b, n)
                    last.then_inc(s("rank_ps"), 1)
            pe.wait_ge(s("rank_ev"), B)
            for b in range(B):
                for j in range(NT):
                    t0, n = j * 128, (128 if j < NT - 1 else LAST)
                    last = nc.tensor.transpose(PS[0:n, 1, b * NT + j:b * NT + j + 1], rank_row[:, b, t0:t0 + n],
                                               w("ident")[0:1, 0:1])
            last.then_inc(s("rank_cols"), 1)
            pe.wait_ge(s("residual"), 1)
            for b in range(B):
                for y in range(2 * NG):
                    m = b * 2 * NG + y
                    if m >= 2:
                        pe.wait_ge(s("hid_ready"), m - 1)
                    nc.tensor.matmul(PS[:, 4 + m % 2, 0:G], w("w1")[:, (b % 2) * HF + (y // NG) * 128:(b % 2) * HF + (y // NG + 1) * 128],
                                     P1[:, b // 2, cols(y % NG)], start=True, stop=True).then_inc(s("hid_ps"), 1)
                pe.wait_ge(s("hid_ready"), (b + 1) * 2 * NG)
                for j in range(NT):
                    x_ = b * NT + j
                    t0, n = j * 128, (128 if j < NT - 1 else LAST)
                    if x_ >= 2:
                        pe.wait_ge(s("rows_ready"), x_ - 1)
                    for hh in range(2):
                        nc.tensor.matmul(PS[0:n, 6 + x_ % 2, 0:D], hid[b % 2][:, hh, t0:t0 + n],
                                         w("w2")[:, hh * D:(hh + 1) * D], start=(hh == 0), stop=(hh == 1))
                    nc.tensor.transpose(PS[0:n, 6 + x_ % 2, D:2 * D], P4[half(b), b // 2, t0:t0 + n],
                                        w("ident")[half(b), half(b)]).then_inc(s("rows_out_ps"), 1)

        @block.scalar
        def _(act):
            step = stepper(act, "act_step")

            def f(o, i, fn, **kw):
                return nc.scalar.activation(o, i, fn, **kw)

            act.wait_ge(s("const_ready"), 1)
            for p in range(NPAIR):
                act.wait_ge(s(f"x_high{p}"), 16)
                f(xs[:, p, T:T + PAD, :], xs[:, p, T - 1:T, :].to_broadcast([128, PAD, V]), ACT.Copy).then_inc(s("x_pad"), 1)
                for hf in range(2):
                    act.wait_ge(s("tok_ps"), 2 * p + hf + 1)
                    f(H[:, p, 0:TOK].rearrange("q (v n) -> q n v", n=NP_)[:, 8 * hf:8 * hf + 8, :],
                      PS[:, 2 * p + hf, :].rearrange("q (n v) -> q n v", n=8), ACT.Copy).then_inc(s("tok_ev"), 1)
            ln_act(act, 1, P1, P2, P3)
            act.wait_ge(s("gbias_ready"), 1)
            act.wait_ge(s("ln1_out"), NGR)
            for g, (p, k) in enumerate(groups):
                act.wait_ge(s("gates_ps"), g + 1)
                f(li[:, p, cols(k)], PS[:, 4 + g % 2, 0:G], ACT.Tanh, bias=gbias[:, 0:1], scale=0.1).then_inc(s("gates_ev"), 1)
            for g, (p, k) in enumerate(groups):
                m = NGR + g
                act.wait_ge(s("gates_ps"), m + 1)
                f(fs[:, p, cols(k)], PS[:, 4 + m % 2, 0:G], ACT.Abs, bias=col("bf"))
                f(r_[:, p, cols(k)], PS[:, 4 + m % 2, 0:G], ACT.Relu, bias=col("bf")).then_inc(s("gates_ev"), 1)
            act.wait_ge(s("gates_ev"), 2 * NGR)
            step(f(fs, fs, ACT.Exp, scale=-1.0))
            f(lf, fs, ACT.Ln, bias=ONE).then_inc(s("softplus"), 1)
            for g, (p, k) in enumerate(groups):
                m = 2 * NGR + g
                act.wait_ge(s("gates_ps"), m + 1)
                f(so[:, p, cols(k)], PS[:, 4 + m % 2, 0:G], ACT.Sigmoid, bias=col("bo")).then_inc(s("gates_ev"), 1)
            act.wait_ge(s("exponents"), 1)
            f(fs, fs, ACT.Exp).then_inc(s("factors"), 1)
            act.wait_ge(s("exponents"), 2)
            f(li, li, ACT.Exp).then_inc(s("factors"), 1)
            for g, (p, k) in enumerate(groups):
                act.wait_ge(s("den_ps"), g + 1)
                f(rden[:, p, cols(k)], PS[:, 6 + g % 2, 0:G], ACT.Abs).then_inc(s("den_ev"), 1)
            act.wait_ge(s("den_max"), 1)
            step(f(rden, rden, ACT.Ln))
            f(rden, rden, ACT.Exp, scale=-1.0).then_inc(s("rden_ready"), 1)
            act.wait_ge(s("iv_ready"), 1)
            for n in range(NL):
                lag, p = n // NPAIR, n % NPAIR
                if lag:
                    act.wait_ge(s("lag_w"), n - 1)
                f(chunks(ve[:, p, :])[:, :, L - 1 - lag], chunks(WV[lag % 2][:, p, :])[:, :, L - 1],
                  ACT.Copy).then_inc(s("lag_ve"), 1)
            act.wait_ge(s("lag_sum"), NL - NPAIR)
            act.wait_ge(s("lag_ps"), NL)
            for u in range(NPAIR * NT + 1):
                if u < NPAIR * NT:
                    n = seq_of(u % NT)[1]
                    act.wait_ge(s("rows_ps"), u + 1)
                    if u >= 2:
                        act.wait_ge(s("u_mm"), 2 * (u - 1))
                    f(rows_t[u % 2][0:n, :], PS[0:n, 6 + u % 2, 0:256], ACT.Copy).then_inc(s("rows_ev"), 1)
                if u >= 1:
                    p, j = (u - 1) // NT, (u - 1) % NT
                    ncs = seq_of(j)[1] // L
                    for b2 in range(2):
                        y = 2 * (u - 1) + b2
                        act.wait_ge(s("u_mm"), y + 1)
                        f(UMc[half(b2), p, :, 8 * j:8 * j + ncs],
                          PS[half(b2), y % 4, 0:ncs * D].rearrange("q (c i) -> q i c", i=D), ACT.Copy).then_inc(s("u_ev"), 1)
            for p in range(NPAIR):
                act.wait_ge(s("gated"), p + 1)
                f(WV[1][:, p, :], hr[:, p, :], ACT.Square).then_inc(s("msq_in"), 1)
            for g, (p, k) in enumerate(groups):
                act.wait_ge(s("msq_ps"), g + 1)
                f(fs[:, p, cols(k)], PS[:, 6 + g % 2, 0:G], ACT.Ln, bias=EPS8, scale=RMS_SCALE / D).then_inc(s("rms_ev"), 1)
            act.wait_ge(s("rms_ev"), NGR)
            for p, k in groups:
                f(fs[:, p, cols(k)], fs[:, p, cols(k)], ACT.Exp, bias=HALF_LN, scale=-0.5).then_inc(s("rms_ready"), 1)
            ln_act(act, 2, P1, P2, P3)
            act.wait_ge(s("bn_in"), 16)
            f(bns[:, :, :], bnw[:, 8:10, :], ACT.Sqrt, bias=EPS3).then_inc(s("bn_sd"), 1)
            act.wait_ge(s("logits"), 1)
            f(lg, lg, ACT.Exp).then_inc(s("gate_exp"), 1)
            act.wait_ge(s("bn_ready"), 1)
            act.wait_ge(s("ln2_out"), NGR)

            def hidden1(n):
                act.wait_ge(s("l1_ps"), n + 1)
                if n >= 2:
                    act.wait_ge(s("l2_ps"), n - 1)
                e = n % E
                f(twin(h1b, n % 2), PS[:, 2:4, 0:G], ACT.Relu, bias=bnb[:, 0, e:e + 1],
                  scale=bns[:, 0, e:e + 1]).then_inc(s("h1_ev"), 1)

            def hidden2(n):
                act.wait_ge(s("l2_ps"), n + 1)
                if n >= 2:
                    act.wait_ge(s("hw_ready"), n - 1)
                e = n % E
                f(twin(h2b, n % 2), PS[:, 4:6, 0:G], ACT.Relu, bias=bnb[:, 1, e:e + 1],
                  scale=bns[:, 1, e:e + 1]).then_inc(s("h2_ev"), 1)

            hidden1(0)
            for n in range(NG * E):
                hidden2(n)
                if n + 1 < NG * E:
                    hidden1(n + 1)
            f(aneg[:, :], w("A_log"), ACT.Exp).then_inc(s("a_exp"), 1)
            ln_act(act, 3, P1, P2, P3)
            for b in range(B):
                for k in range(NG):
                    m = b * NG + k
                    act.wait_ge(s("z_ps"), m + 1)
                    f(batch_array(3, b)[:, cols(k)], PS[:, 2 + m % 2, 0:G], ACT.Silu).then_inc(s("z_ev"), 1)
                act.wait_ge(s("conv_ready"), b + 1)
                f(batch_array(0, b), conv[b % 2], ACT.Silu, bias=col("conv_b")).then_inc(s("u_ready"), 1)

            def mid_part(b):
                act.wait_ge(s("bc_left"), NG * (b + 1))
                f(SBC[b][64:128], resid[b % 2][64:128], ACT.Copy).then_inc(s("bc_mid"), 1)

            for m in range(B * NG + 1):
                if m < B * NG:
                    b, k = m // NG, m % NG
                    act.wait_ge(s("dlo_ps"), m + 1)
                    if m >= 2:
                        act.wait_ge(s("dt_ps"), m - 1)
                    f(dlo[m % 2], PS[:, 4 + m % 2, 0:G], ACT.Copy).then_inc(s("dlo_ev"), 1)
                    act.wait_ge(s("bc_ps"), m + 1)
                    f(SBC[b][:, :, cols(k)], PS[:, 2 * (m % 2):2 * (m % 2) + 2, 0:G], ACT.Copy).then_inc(s("bc_high"), 1)
                if m >= 1:
                    b, k = (m - 1) // NG, (m - 1) % NG
                    act.wait_ge(s("dt_ps"), m)
                    f(expo[b // 2][:, b % 2, cols(k)], PS[:, 6 + (m - 1) % 2, 0:G], ACT.Abs,
                      bias=col("b_dt")).then_inc(s("dt_abs"), 1)
                if m >= NG and m % NG == 1:
                    mid_part((m - 1) // NG - 1)
            act.wait_ge(s("dt_abs"), B * NG)
            for p in range(NPAIR):
                f(expo[p], expo[p], ACT.Exp, scale=-1.0).then_inc(s("dt_exp"), 1)
            mid_part(B - 1)
            act.wait_ge(s("dt_exp"), NPAIR)
            for p in range(NPAIR):
                f(logs[p], expo[p], ACT.Ln, bias=ONE).then_inc(s("dt_log"), 1)
            act.wait_ge(s("a_ready"), 1)
            act.wait_ge(s("dt_ready"), NPAIR)
            act.wait_ge(s("bc_ready"), B)

            def decay_and_c(b, i, half_, first):
                at = i * 2 + (half_ - DS * b)
                early = first and b == 0
                for k in range(NG):
                    m = NG * half_ + k
                    act.wait_ge(s("a_ready"), 1)
                    if not (early and m < 2):
                        act.wait_ge(s("scanned"), i * (2 * NG) + (m - 1))
                    f(PS[:, 6 + m % 2, 0:G], batch_array(1, b)[:, cols(k)], ACT.Exp,
                      scale=aneg[:, bass.ds(at, 1)]).then_inc(s("decay"), 1)
                    act.wait_ge(s("c_spread"), i * (2 * NG) + (m + 1))
                    if k == 0 and not early:
                        act.wait_ge(s("hc_ready"), i * 2 + (half_ - 1))
                    f(cbuf[half_][:, cols(k)], PS[:, 5, 0:G], ACT.Copy).then_inc(s("c_copied"), 1)

            for b in range(B):
                i0 = b * DS // 2
                decay_and_c(b, i0, 0, True)
                decay_and_c(b, i0, 1, True)
                with act.Fori(i0 + 1, i0 + DS // 2) as i:
                    decay_and_c(b, i, 0, False)
                    decay_and_c(b, i, 1, False)
            for g in range(NGR + 2):
                if g < NGR:
                    p, k = groups[g]
                    act.wait_ge(s("mo_ps"), g + 1)
                    f(P1[:, p, cols(k)], PS[:, g % 2, 0:G], ACT.Copy).then_inc(s("mo_ev"), 1)
                if g >= 2:
                    p, k = groups[g - 2]
                    act.wait_ge(s("ff2_ps"), g - 1)
                    f(P4[:, p, cols(k)], PS[:, 4 + g % 2, 0:G], ACT.Sigmoid, bias=col("ff2b")).then_inc(s("ff2_ev"), 1)
            ln_act(act, 4, P1, P2, P3)
            for m in range(B * NG):
                b, k = m // NG, m % NG
                act.wait_ge(s("wrow_ps"), m + 1)
                f(wrow[b][:, cols(k)], PS[:, m % 2, 0:G], ACT.Identity, bias=col("br")).then_inc(s("wrow_ev"), 1)
            for b in range(B):
                act.wait_ge(s("rank_ps"), NT * (b + 1))
                banks = (3, 4, 5) if b % 2 == 0 else (6, 7, 0)
                for i, (a, z) in enumerate(BANKS):
                    ins = f(rank_row[:, b, a:z], PS[0:1, banks[i], 0:z - a], ACT.Copy)
                ins.then_inc(s("rank_ev"), 1)
            for m in range(B * 2 * NG):
                b, y = m // (2 * NG), m % (2 * NG)
                act.wait_ge(s("hid_ps"), m + 1)
                if b >= 2 and y == 0:
                    act.wait_ge(s("rows_out_ps"), (b - 1) * NT)
                f(hid[b % 2][:, y // NG, cols(y % NG)], PS[:, 4 + m % 2, 0:G], ACT.Gelu_apprx_tanh,
                  bias=col("b1a" if y < NG else "b1b")).then_inc(s("hid_ready"), 1)

        @block.gpsimd
        def _(pool):
            step = stepper(pool, "pool_step")

            def forward_decays():
                pool.wait_ge(s("ik_ready"), 1)
                pool.wait_ge(s("iv_ready"), 1)
                pool.wait_ge(s("lag_prod"), NL // 2 + 1)
                fc, dc = (a.rearrange("p a (c r) -> p a c r", r=L) for a in (fs, dfw))
                step(nc.gpsimd.tensor_copy(dc[:, :, :, 0], fc[:, :, :, 0]))
                for r in range(1, L):
                    step(nc.gpsimd.tensor_tensor(dc[:, :, :, r], dc[:, :, :, r - 1], fc[:, :, :, r], ALU.mult))
                step(nc.gpsimd.tensor_copy(dend[:, :, :], dc[:, :, :, L - 1]))
                nc.gpsimd.memset(dend[:, :, 0:1], 0.0).then_inc(s("dend_ready"), 1)
                pool.wait_ge(s("dend_ready"), 1)

            pool.wait_ge(s("qkv_ev"), 3 * NGR)
            pool.wait_ge(s("tok_ps"), 4)
            for n in range(NL):
                lag, p = n // NPAIR, n % NPAIR
                if n >= 4:
                    pool.wait_ge(s("lag_ps"), n - 3)
                nc.gpsimd.tensor_tensor(prod[n % 4][:, 0:NC * (L - lag)].rearrange("p (c r) -> p c r", r=L - lag),
                                        chunks(q_[:, p, :])[:, :, lag:L], chunks(k_[:, p, :])[:, :, 0:L - lag],
                                        ALU.mult).then_inc(s("lag_prod"), 1)
                if n == NL // 2:
                    forward_decays()
            pool.wait_ge(s("states"), NPAIR)
            nc.gpsimd.tensor_copy(pick8.rearrange("p (e m) -> p e m", e=E),
                                  w("ident")[:, 0:E].unsqueeze(2).to_broadcast([128, E, 128])).then_inc(s("experts_zero"), 1)
            pool.wait_ge(s("gated"), NPAIR)
            pool.wait_ge(s("experts_zero"), 1)
            nc.gpsimd.memset(wT, 0.0).then_inc(s("experts_zero"), 1)
            pool.wait_ge(s("u_mm"), 4 * NT)
            pool.wait_ge(s("experts_zero"), 2)
            nc.gpsimd.tensor_copy(pick.rearrange("p (e m) -> p e m", e=DS),
                                  w("eyes").unsqueeze(2).to_broadcast([128, DS, 128])).then_inc(s("pick_ready"), 1)
            pool.wait_ge(s("pick_ready"), 1)
            for b in range(B):
                pool.wait_ge(s("bc_mid"), b + 1)
                nc.gpsimd.tensor_tensor(resid[b % 2][96:128], resid[b % 2][96:128], SBC[b][96:128],
                                        ALU.subtract).then_inc(s("bc_low"), 1)
            pool.wait_ge(s("bc_ready"), B)

            def times_c(i, half_, early):
                pool.wait_ge(s("scanned"), i * (2 * NG) + NG * (half_ + 1))
                pool.wait_ge(s("c_copied"), i * (2 * NG) + NG * (half_ + 1))
                if not early:
                    pool.wait_ge(s("y_added"), i * 2 + (half_ - 1))
                nc.gpsimd.tensor_tensor(hcbuf[half_], hbuf[half_], cbuf[half_], ALU.mult).then_inc(s("hc_ready"), 1)

            times_c(0, 0, True)
            times_c(0, 1, True)
            with pool.Fori(1, B * DS // 2) as i:
                times_c(i, 0, False)
                times_c(i, 1, False)

        @block.vector
        def _(dve):
            step = stepper(dve, "dve_step")
            tt = nc.vector.tensor_tensor
            stt = nc.vector.scalar_tensor_tensor
            ts = nc.vector.tensor_scalar

            for c_, v in zip((EPS5, EPS8, ONE, HALF_LN, LN_EDGE),
                             (1e-5, 1e-8 * RMS_SCALE, 1.0, 0.5 * math.log(RMS_SCALE), -math.log1p(EDGE))):
                nc.vector.memset(c_, v)
            nc.vector.memset(one_bf[:, :], 1.0)
            nc.vector.memset(EPS3, 1e-3).then_inc(s("const_ready"), 1)
            step(nc.vector.memset(Wt[:, :], 0.0))
            nc.vector.memset(H[:, :, S:SP], 0.0).then_inc(s("txt_ev"), 1)
            dve.wait_ge(s("wtok_ps"), 1)
            for b2 in range(2):
                h = half(b2)
                for bank in range(-(-NOG // 4)):
                    o0 = bank * 4 * OG
                    no = min(4 * OG, D - o0)
                    nc.vector.tensor_copy(
                        Wt[h, :].rearrange("p (t m) -> p m t", t=PATCH)[:, 64 * b2 + o0:64 * b2 + o0 + no, :],
                        PS[h, 4 + bank, 0:no * PATCH].rearrange("p (o t) -> p o t", t=PATCH)).then_inc(s("wtok_sb"), 1)
            dve.wait_ge(s("w_in"), 16)
            step(tt(gbias[:, 0:1], col("bi"), col("ib"), ALU.add))
            ts(gbias[:, 0:1], gbias[:, 0:1], 0.1, None, ALU.mult).then_inc(s("gbias_ready"), 1)
            dve.wait_ge(s("txt_ps"), 1)
            nc.vector.tensor_copy(H[:, :, TOK:S], PS[:, 7, 0:NPAIR * TXT].rearrange("q (a t) -> q a t", a=NPAIR)
                                  ).then_inc(s("txt_ev"), 1)
            dve.wait_ge(s("tok_ev"), 4)
            dve.wait_ge(s("txt_ev"), 2)
            ln_dve(dve, 1, P1, P3)
            for r, (dst, bias, scale) in enumerate(((q_, "bq", 1.0), (k_, "bk", float(D) ** -0.5), (v_, "bv", 1.0))):
                for g, (p, k) in enumerate(groups):
                    m = r * NGR + g
                    dve.wait_ge(s("qkv_ps"), m + 1)
                    if m == 0:
                        dve.wait_ge(s("ln1_out"), NGR)
                        dve.wait_ge(s("ln1_var"), NGR)
                    ts(dst[:, p, cols(k)], PS[:, 6 + m % 2, 0:G], col(bias), scale, ALU.add, ALU.mult).then_inc(s("qkv_ev"), 1)
            dve.wait_ge(s("gates_ev"), 2 * NGR)
            step(ts(li, li, 10.0, None, ALU.mult))
            dve.wait_ge(s("softplus"), 1)
            step(stt(lf, lf, -1.0, r_, ALU.mult, ALU.subtract))
            for p in range(NPAIR):
                step(nc.vector.tensor_tensor_scan(m_[:, p, :], lf[:, p, :], li[:, p, :], 0.0, ALU.add, ALU.max))
            nc.vector.tensor_copy(fs[:, :, 0:1], lf[:, :, 0:1])
            step(tt(fs[:, :, 1:], lf[:, :, 1:], m_[:, :, 0:SP - 1], ALU.add))
            tt(fs, fs, m_, ALU.subtract).then_inc(s("exponents"), 1)
            tt(li, li, m_, ALU.subtract).then_inc(s("exponents"), 1)
            dve.wait_ge(s("factors"), 2)
            tt(ik, li, k_, ALU.mult).then_inc(s("ik_ready"), 1)
            dve.wait_ge(s("ik_ready"), 1)
            for p in range(NPAIR):
                step(nc.vector.tensor_tensor_scan(n_[:, p, :], fs[:, p, :], ik[:, p, :], 0.0, ALU.mult, ALU.add))
                tt(ik[:, p, :], n_[:, p, :], q_[:, p, :], ALU.mult).then_inc(s("nq_ready"), 1)
            tt(v_, v_, li, ALU.mult).then_inc(s("iv_ready"), 1)
            dve.wait_ge(s("den_ev"), NGR)
            ts(rden, rden, 1e-6, None, ALU.max).then_inc(s("den_max"), 1)
            dve.wait_ge(s("iv_ready"), 1)
            for n in range(NL):
                lag, p = n // NPAIR, n % NPAIR
                now, was = (chunks(WV[(lag + d) % 2][:, p, :]) for d in (0, 1))
                if lag:
                    if lag >= 2:
                        dve.wait_ge(s("lag_ve"), n - 3)
                    tt(now[:, :, lag:L], was[:, :, lag - 1:L - 1], chunks(fs[:, p, :])[:, :, lag:L],
                       ALU.mult).then_inc(s("lag_w"), 1)
                    dve.wait_ge(s("lag_w"), n - 1)
                dve.wait_ge(s("lag_ps"), n + 1)
                qk = PS[:, NG * p:NG * p + NG, 0:CG * (L - lag)].rearrange("q k (c r) -> q k c r", r=L - lag)
                wv = now[:, :, lag:L].rearrange("q (k c) r -> q k c r", k=NG)
                if lag == 0:
                    tt(chunks(hr[:, p, :]).rearrange("q (k c) r -> q k c r", k=NG), wv, qk, ALU.mult).then_inc(s("lag_read"), 1)
                    dve.wait_ge(s("lag_read"), n + 1)
                    continue
                tm = term[n % 2][:, 0:NC * (L - lag)]
                tt(tm.rearrange("q (k c r) -> q k c r", k=NG, r=L - lag), wv, qk, ALU.mult).then_inc(s("lag_read"), 1)
                dve.wait_ge(s("lag_read"), n + 1)
                if n >= 2 * NPAIR:
                    dve.wait_ge(s("lag_sum"), n - 2 * NPAIR + 1)
                tt(chunks(hr[:, p, :])[:, :, lag:L], chunks(hr[:, p, :])[:, :, lag:L],
                   tm.rearrange("q (c r) -> q c r", r=L - lag), ALU.add).then_inc(s("lag_sum"), 1)

            def state_scan(p):
                dve.wait_ge(s("decay_in"), 64)
                dve.wait_ge(s("u_ev"), 2 * NT * (p + 1))
                nc.vector.tensor_tensor_scan(UM[:, p, :], DBC[:, p, :], UM[:, p, :], 0.0, ALU.mult,
                                             ALU.add).then_inc(s("states"), 1)

            for u in range(NPAIR * NT):
                n = seq_of(u % NT)[1]
                for b2 in range(2):
                    y = 2 * u + b2
                    dve.wait_ge(s("rows_ev"), u + 1)
                    if y >= 2:
                        dve.wait_ge(s("u_mm"), y - 1)
                    shape = [n, n // L, D]
                    tt(spread[b2][0:n, 0:n // L * D].rearrange("q (c i) -> q c i", i=D),
                       rows_t[u % 2][0:n, 64 * b2:64 * b2 + 64].unsqueeze(1).to_broadcast(shape),
                       w("cmask")[0:n, 0:n // L].unsqueeze(2).to_broadcast(shape), ALU.mult).then_inc(s("spread_ready"), 1)
                if u == NT + 2:
                    state_scan(0)
            state_scan(1)
            dve.wait_ge(s("lag_sum"), NL - NPAIR)
            dve.wait_ge(s("rden_ready"), 1)
            for p in range(NPAIR):
                dve.wait_ge(s("inter_ps"), p + 1)
                tt(WV[0][:, p, L:G], dfw[:, p, L:G], PS[:, NG * p, L:G], ALU.mult)
                tt(WV[0][:, p, G:SP].rearrange("q (k t) -> q k t", k=NG - 1), dfw[:, p, G:SP].rearrange("q (k t) -> q k t", k=NG - 1),
                   PS[:, NG * p + 1:NG * p + NG, 0:G], ALU.mult).then_inc(s("inter_ev"), 1)
                dve.wait_ge(s("inter_ev"), p + 1)
                step(tt(hr[:, p, L:], hr[:, p, L:], WV[0][:, p, L:], ALU.add))
                step(tt(hr[:, p, :], hr[:, p, :], rden[:, p, :], ALU.mult))
                tt(hr[:, p, :], hr[:, p, :], so[:, p, :], ALU.mult).then_inc(s("gated"), 1)
            dve.wait_ge(s("gated"), NPAIR)
            for g, (p, k) in enumerate(groups):
                dve.wait_ge(s("rms_ready"), g + 1)
                step(tt(hr[:, p, cols(k)], hr[:, p, cols(k)], fs[:, p, cols(k)], ALU.mult))
                stt(H[:, p, cols(k)], hr[:, p, cols(k)], col("ns"), H[:, p, cols(k)], ALU.mult, ALU.add
                    ).then_inc(s("mlstm_out"), 1)
            dve.wait_ge(s("mlstm_out"), NGR)
            ln_dve(dve, 2, P1, P3)
            dve.wait_ge(s("bn_sd"), 1)
            step(nc.vector.reciprocal(bns[:, :, :], bns[:, :, :]))
            step(tt(bns[:, :, :], bns[:, :, :], bnw[:, 2:4, :], ALU.mult))
            step(tt(bnb[:, :, :], bnw[:, 0:2, :], bnw[:, 6:8, :], ALU.subtract))
            step(tt(bnb[:, :, :], bnb[:, :, :], bns[:, :, :], ALU.mult))
            tt(bnb[:, :, :], bnb[:, :, :], bnw[:, 4:6, :], ALU.add).then_inc(s("bn_ready"), 1)
            wide = [128, NT, E]
            dve.wait_ge(s("logit_ps"), 1)
            step(stt(lg, PS[:, 4, 0:NT * E].rearrange("q (j e) -> q j e", e=E), 1.0 / B,
                     w("brow").unsqueeze(1).to_broadcast(wide), ALU.mult, ALU.add))
            step(nc.vector.tensor_reduce(gmax, lg, AX_X, ALU.max))
            tt(lg, lg, gmax.unsqueeze(2).to_broadcast(wide), ALU.subtract).then_inc(s("logits"), 1)
            dve.wait_ge(s("gate_exp"), 1)
            step(nc.vector.tensor_reduce(gsum, lg, AX_X, ALU.add))
            step(nc.vector.reciprocal(gsum, gsum))
            tt(lg, lg, gsum.unsqueeze(2).to_broadcast(wide), ALU.mult).then_inc(s("gate_ready"), 1)
            dve.wait_ge(s("gateT_ps"), 1)
            dve.wait_ge(s("experts_zero"), 2)
            nc.vector.tensor_copy(wT[0:E, 0:1024].rearrange("q (a t) -> q a t", a=2), PS[0:E, 5:7, :]).then_inc(s("gateT"), 1)
            dve.wait_ge(s("gateT"), 1)
            nc.vector.tensor_copy(wT[0:E, SP - 128:SP], PS[0:E, 7, 0:128]).then_inc(s("gateT"), 1)
            dve.wait_ge(s("ln2_out"), NGR)
            for n in range(NG * E + 1):
                if n < NG * E:
                    dve.wait_ge(s("h2_ev"), n + 1)
                    dve.wait_ge(s("spread_w"), n + 1)
                    if n >= 2:
                        dve.wait_ge(s("l3_ps"), n - 1)
                    tt(twin(hwb, n % 2), twin(h2b, n % 2), PS[:, 6 + n % 2:7 + n % 2, 0:G].to_broadcast([128, NPAIR, G]),
                       ALU.mult).then_inc(s("hw_ready"), 1)
                if n and n % E == 0:
                    k = n // E - 1
                    dve.wait_ge(s("l3_ps"), n)
                    tt(H[:, :, cols(k)], PS[:, 0:2, 0:G], H[:, :, cols(k)], ALU.add).then_inc(s("ffn_out"), 1)
            dve.wait_ge(s("ffn_out"), NG)
            ln_dve(dve, 3, P1, P3)
            dve.wait_ge(s("a_exp"), 1)
            ts(aneg[:, :], aneg[:, :], -1.0, None, ALU.mult).then_inc(s("a_ready"), 1)
            dve.wait_ge(s("ln3_out"), NGR)
            ts(diagD[:, :], w("ident"), col("Dm"), None, ALU.mult).then_inc(s("diag_ready"), 1)
            for i in range(2):
                step(nc.vector.memset(xcp[i][:, 0:KC - 1], 0.0))
            for b in range(B):
                xp = xcp[b % 2]
                for k in range(NG):
                    m = b * NG + k
                    dve.wait_ge(s("xc_ps"), m + 1)
                    nc.vector.tensor_copy(xp[:, KC - 1 + k * G:KC - 1 + (k + 1) * G], PS[:, m % 2, 0:G]).then_inc(s("xc_ev"), 1)
                dve.wait_ge(s("xc_ev"), NG * (b + 1))
                if b >= 2:
                    dve.wait_ge(s("u_ready"), b - 1)
                cw = w("conv_w")
                step(ts(conv[b % 2], xp[:, 0:SP], cw[:, 0:1], None, ALU.mult))
                for j in range(1, KC):
                    ins = stt(conv[b % 2], xp[:, j:j + SP], cw[:, j:j + 1], conv[b % 2], ALU.mult, ALU.add)
                    if j < KC - 1:
                        step(ins)
                ins.then_inc(s("conv_ready"), 1)
            dve.wait_ge(s("z_ps"), B * NG)
            dve.wait_ge(s("u_ready"), B)

            def low_part(b):
                dve.wait_ge(s("bc_low"), b + 1)
                nc.vector.tensor_copy(SBC[b][96:128], resid[b % 2][96:128]).then_inc(s("bc_ready"), 1)

            def softplus(p):
                both = slice(2 * p * SP, (2 * p + 2) * SP)
                u, dt, low = (big[:, 4 * i * SP:4 * (i + 1) * SP][:, both].rearrange("q (b t) -> q b t", b=2) for i in range(3))
                dve.wait_ge(s("dt_exp"), p + 1)
                step(ts(low, expo[p], EDGE, None, ALU.min))
                step(ts(dt, low, 1.0 / 3.0, -0.5, ALU.mult, ALU.add))
                step(tt(dt, dt, low, ALU.mult))
                step(stt(dt, dt, 1.0, low, ALU.add, ALU.mult))
                step(tt(dt, dt, frelu[p], ALU.add))
                dve.wait_ge(s("dt_log"), p + 1)
                step(ts(logs[p], logs[p], -math.log1p(EDGE), 0.0, ALU.add, ALU.max))
                step(tt(dt, dt, logs[p], ALU.add))
                tt(low, dt, u, ALU.mult).then_inc(s("dt_ready"), 1)

            for m in range(B * NG + 1):
                if m < B * NG:
                    b, k = m // NG, m % NG
                    if b >= 2 and k == 0:
                        low_part(b - 2)
                        dve.wait_ge(s("bc_ready"), b - 1)
                    dve.wait_ge(s("bc_high"), m + 1)
                    tt(resid[b % 2][:, :, cols(k)], PS[:, 2 * (m % 2):2 * (m % 2) + 2, 0:G], SBC[b][:, :, cols(k)],
                       ALU.subtract).then_inc(s("bc_left"), 1)
                if m >= 1:
                    b, k = (m - 1) // NG, (m - 1) % NG
                    dve.wait_ge(s("dt_abs"), m)
                    ts(frelu[b // 2][:, b % 2, cols(k)], PS[:, 6 + (m - 1) % 2, 0:G], col("b_dt"), 0.0,
                       ALU.add, ALU.max).then_inc(s("dt_relu"), 1)
            dve.wait_ge(s("dt_relu"), B * NG)
            softplus(0)
            for b in range(2, B):
                low_part(b)
            softplus(1)
            dve.wait_ge(s("bc_ready"), B)
            dve.wait_ge(s("dt_ready"), NPAIR)

            def input_term(b, i, m, early):
                if not (early and m < 2):
                    dve.wait_ge(s("scanned"), i * (2 * NG) + (m - 1))
                dve.wait_ge(s("b_spread"), i * (2 * NG) + (m + 1))
                tt(bx[m % 2], batch_array(2, b)[:, cols(m % NG)], PS[:, 3 + m % 2, 0:G], ALU.mult).then_inc(s("b_used"), 1)

            def scan_tiles(b, i, first):
                early = first and b == 0
                input_term(b, i, 0, early)
                for m in range(2 * NG):
                    half_, k = m // NG, m % NG
                    if m + 1 < 2 * NG:
                        input_term(b, i, m + 1, early)
                    dve.wait_ge(s("b_used"), i * (2 * NG) + (m + 1))
                    dve.wait_ge(s("decay"), i * (2 * NG) + (m + 1))
                    if k == 0 and not early:
                        dve.wait_ge(s("hc_ready"), i * 2 + (half_ - 1))
                    if k:
                        dve.wait_ge(s("scanned"), i * (2 * NG) + m)
                    h = hbuf[half_]
                    nc.vector.tensor_tensor_scan(h[:, cols(k)], PS[:, 6 + m % 2, 0:G], bx[m % 2],
                                                 h[:, k * G - 1:k * G] if k else 0.0, ALU.mult, ALU.add).then_inc(s("scanned"), 1)

            def finish_y(b):
                dve.wait_ge(s("y_added"), DS * (b + 1))
                z = batch_array(3, b).rearrange("q (k t) -> q k t", k=NG)
                tt(z, z, PS[:, 0:NG, 0:G], ALU.mult).then_inc(s("ys_ready"), 1)

            for b in range(B):
                i0 = b * DS // 2
                scan_tiles(b, i0, True)
                if b >= 1:
                    finish_y(b - 1)
                with dve.Fori(i0 + 1, i0 + DS // 2) as i:
                    scan_tiles(b, i, False)
            finish_y(B - 1)
            for g in range(NGR + 2):
                if 1 <= g <= NGR:
                    p, k = groups[g - 1]
                    dve.wait_ge(s("ff1_ps"), g)
                    ts(P2[:, p, cols(k)], PS[:, 2 + (g - 1) % 2, 0:G], col("ff1b"), None,
                       ALU.add).then_inc(s("ff1_ev"), 1)
                    dve.wait_ge(s("ff1_ev"), g)
                    stt(P3[:, p, cols(k)], P2[:, p, cols(k)], 0.01, P2[:, p, cols(k)],
                        ALU.mult, ALU.max).then_inc(s("ff1_out"), 1)
                if g >= 2:
                    p, k = groups[g - 2]
                    dve.wait_ge(s("ff2_ev"), g - 1)
                    tt(H[:, p, cols(k)], H[:, p, cols(k)], P4[:, p, cols(k)], ALU.add).then_inc(s("mamba_out"), 1)
            dve.wait_ge(s("mamba_out"), NGR)
            dve.wait_ge(s("mo_ev"), NGR)
            dve.wait_ge(s("ff1_ps"), NGR)
            dve.wait_ge(s("ff2_ps"), NGR)
            ln_dve(dve, 4, P1, P3)
            dve.wait_ge(s("ln4_out"), NGR)
            tt(P4, H[:, :, :], P1, ALU.add).then_inc(s("residual"), 1)
            dve.wait_ge(s("wcol_ps"), 1)
            pcol = PS[:, 2, 0:B * NT].rearrange("q (b j) -> q b j", b=B)
            step(nc.vector.tensor_copy(wcol[:, :, 0:NT - 1], pcol[:, :, 0:NT - 1]))
            step(nc.vector.tensor_copy(wcol[0:LAST, :, NT - 1:NT], pcol[0:LAST, :, NT - 1:NT]))
            for b in range(B):
                for j in range(NT):
                    t0, n = j * 128, (128 if j < NT - 1 else LAST)
                    x_ = b * NT + j
                    own, row, bt = wcol[0:n, b, j:j + 1], wrow[b][0:n], beats[x_ % 2][0:n]
                    if x_ >= 2:
                        dve.wait_ge(s("rank_ps"), x_ - 1)
                    if j:
                        ts(bt[:, 0:t0], row[:, 0:t0], own, None, ALU.is_lt)
                    if t0 + n < S:
                        ts(bt[:, t0 + n:S], row[:, t0 + n:S], own, None, ALU.is_le)
                    stt(bt[:, t0:t0 + n], row[:, t0:t0 + n], own, w("after")[0:n, 0:n], ALU.is_le, ALU.mult)
                    stt(beats_own[x_ % 2][0:n, 0:n], row[:, t0:t0 + n], own, w("before")[0:n, 0:n], ALU.is_lt,
                        ALU.mult).then_inc(s("beats_ready"), 1)
            dve.wait_ge(s("rank_cols"), 1)
            for a, n in ((slice(0, NT - 1), 128), (slice(NT - 1, NT), LAST)):
                sv = sel[0:n, :].rearrange("q (b j) -> q b j", b=B)[:, :, a]
                rc = PS[0:n, 1, 0:B * NT].rearrange("q (b j) -> q b j", b=B)[:, :, a]
                step(ts(sv, rc, float(KEEP), None, ALU.is_lt))
                step(tt(sv, sv, wcol[0:n, :, a], ALU.mult))
            for y in range(B * NT):
                b, j = y // NT, y % NT
                n = 128 if j < NT - 1 else LAST
                dve.wait_ge(s("rows_out_ps"), y + 1)
                step(tt(ytmp[0:n, y % 2, :], PS[0:n, 6 + y % 2, 0:D], w("b2row")[0:n, :], ALU.add))
                stt(RES[0:n, b, j, :], ytmp[0:n, y % 2, :], sel[0:n, y:y + 1], PS[0:n, 6 + y % 2, D:2 * D],
                    ALU.mult, ALU.add).then_inc(s("rows_ready"), 1)


def pack(inputs):
    f = {k: np.asarray(v) for k, v in inputs.items()}
    z = np.float32

    def diag2(a):
        o = np.zeros((2 * a.shape[0], 2 * a.shape[1]), z)
        o[:a.shape[0], :a.shape[1]] = a
        o[a.shape[0]:, a.shape[1]:] = a
        return o

    def twice(a):
        return np.concatenate([a, a], 0)

    def rows(a):
        o = np.zeros((128, a.shape[1]), z)
        o[:a.shape[0]] = a
        return o

    def wide(a):
        return np.ascontiguousarray(rows(a.T).T)

    def column(v):
        return rows(v.reshape(-1, 1))

    wg, bg = f["L0_attn_Wg"], f["L0_attn_bg"]
    xp = f["L1_attn_W_xproj"]
    xB, xC = xp[DTR:DTR + DS].T, xp[DTR + DS:].T
    wout = np.zeros((128, 2, 2, 64), z)
    wr = np.zeros((2, 64, 2, 128), z)
    for i in range(2):
        wout[:, i, i, :] = f["L1_attn_W_out"].T
        wr[i, :, i, :] = f["L1_ffn_wr"]
    idx = np.arange(128)
    w2 = f["L1_ffn_w2"]
    parts = {
        "Wq": diag2(f["L0_attn_Wq"]), "Wk": diag2(f["L0_attn_Wk"]), "Wv": diag2(f["L0_attn_Wv"]),
        "Wi": diag2(wg[:, 0:D]), "Wf": diag2(wg[:, D:2 * D]), "Wo": diag2(wg[:, 2 * D:]),
        "Wr": twice(f["L0_ffn_Wr"]), "ebias": rows(np.concatenate([f["L0_ffn_bo"]] * 2, 1)),
        "Win": diag2(f["L1_attn_W_in"].T), "XB": np.concatenate([xB] * 4, 1), "XC": np.concatenate([xC] * 4, 1),
        "XD": wide(xp[0:DTR].T), "WdtT": rows(f["L1_attn_W_dt"].T), "WoutT": wout.reshape(128, 256),
        "FF1": wide(diag2(f["L1_attn_W_ff1"].T)), "FF2": rows(diag2(f["L1_attn_W_ff2"].T)),
        "wr": wr.reshape(128, 256), "w1": diag2(f["L1_ffn_w1"]), "w2": np.concatenate([w2[0:128], w2[128:]], 1),
        "ident": np.eye(128, dtype=z), "ones": diag2(np.ones((64, 64), z)),
        "cmask": (idx[:, None] // L == np.arange(128 // L)[None]).astype(z),
        "eyes": np.concatenate([np.eye(DS, dtype=z) * (i != 1) for i in range(4)], 0),
        "before": (idx[None] < idx[:, None]).astype(z), "after": (idx[None] > idx[:, None]).astype(z),
        "b2row": np.tile(f["L1_ffn_b2"], (128, 1)), "brow": np.tile(f["L0_ffn_br"], (128, 1)),
        "A_log": f["L1_attn_A_log"], "conv_w": f["L1_attn_conv_w"],
    }
    two = {"bq": f["L0_attn_bq"], "bk": f["L0_attn_bk"], "bv": f["L0_attn_bv"], "bi": bg[0:D], "bf": bg[D:2 * D],
           "bo": bg[2 * D:], "ib": f["L0_attn_input_bias"], "ns": f["L0_attn_norm_scale"],
           "ff1b": f["L1_attn_b_ff1"], "ff2b": f["L1_attn_b_ff2"], "br": np.tile(f["L1_ffn_br"], 64)}
    one = {"conv_b": f["L1_attn_conv_b"], "b_dt": f["L1_attn_b_dt"], "Dm": f["L1_attn_D"],
           "b1a": f["L1_ffn_b1"][0:128], "b1b": f["L1_ffn_b1"][128:]}
    parts["cols"] = np.concatenate([column(np.concatenate([two[n]] * 2) if n in two else one[n]) for n in COLS], 1)
    wts = np.concatenate([parts[n] for n, _ in WEIGHTS], 1)
    wexp = np.concatenate([diag2(f[f"L0_ffn_{n}"][e]) for n in ("W1", "W2", "Wo") for e in range(E)], 1)
    bn = np.concatenate([twice(f[f"L0_ffn_{n}"].T) for n in BN], 1)
    t, fr = np.arange(PATCH), np.arange(NF)
    ang = 2 * np.pi * np.outer(fr, t) / PATCH
    dft = (np.concatenate([np.cos(ang), -np.sin(ang)], 0) / np.sqrt(PATCH)).astype(z)
    wo = np.zeros((NOG * OG, 2 * NF, 2, C), z)
    wo[0:D] = f["L0_tok_W"].reshape(D, 2 * NF, 1, C)
    wd = np.zeros((128, NOG * 128 + OG * PATCH), z)
    wd[0:OG * 2 * NF, 0:NOG * 128] = wo.reshape(NOG, OG * 2 * NF, 128).transpose(1, 0, 2).reshape(OG * 2 * NF, NOG * 128)
    for i in range(OG):
        wd[i * 2 * NF:(i + 1) * 2 * NF, NOG * 128 + i * PATCH:NOG * 128 + (i + 1) * PATCH] = dft
    return {"x": f["x"], "txt": f["txt"], "wdft": wd, "wts": wts, "wexp": wexp, "bn": bn}


def kernel(**inputs):
    import concourse.bacc as bacc
    from concourse.bass_utils import run_bass_kernel_spmd

    nc = bacc.Bacc("TRN2", target_bir_lowering=False, num_devices=1)
    arrays = {k: np.ascontiguousarray(v) for k, v in pack(inputs).items()}
    args = {k: nc.dram_tensor(f"in_{k}", a.shape, mybir.dt.from_np(a.dtype), kind="ExternalInput").ap()
            for k, a in arrays.items()}
    out = nc.dram_tensor("out_h", (B, S, D), F32, kind="ExternalOutput").ap()
    build(nc, out=out, **args)
    r = run_bass_kernel_spmd(nc, [{f"in_{k}": a for k, a in arrays.items()}], core_ids=[0])
    return r.results[0]["out_h"]
```

```python
import math
from contextlib import ExitStack

import numpy as np

import concourse.bass as bass
from concourse import mybir

F32 = mybir.dt.float32
BF16 = mybir.dt.bfloat16
ALU = mybir.AluOpType
ACT = mybir.ActivationFunctionType
AX_X = mybir.AxisListType.X

B, C, T, V = 4, 64, 128, 64
D = 64
PATCH, STRIDE, PAD = 16, 8, 8
NP_ = (T + PAD - PATCH) // STRIDE + 1
NF = PATCH // 2 + 1
TXT = 77
TOK = V * NP_
S = TOK + TXT
NPAIR = B // 2
L = 16
NC = -(-S // L)
SP = NC * L
NG = 3
G = SP // NG
CG = NC // NG
E = 8
DI, DS, DTR, KC = 128, 32, 16, 4
NPS = 4
NS = DS // (2 * NPS)
NSEG = B * NG
HM = 32
HF = 256
KEEP = max(1, int(0.5 * S)) - 1
NT = -(-S // 128)
LAST = S - 128 * (NT - 1)
LASTP = SP - 128 * (NT - 1)
RMS_SCALE = 2.0 ** -30
EDGE = 2.0 ** -7
assert G <= 512 and NC % NG == 0 and SP == NG * G


OG = 7
NOG = -(-D // OG)
WEIGHTS = [("Wq", 128), ("Wk", 128), ("Wv", 128), ("Wi", 128), ("Wf", 128), ("Wo", 128), ("Wr", E), ("ebias", 128),
           ("Win", 4 * DI), ("XB", 128), ("XC", 128), ("XD", 128), ("WdtT", DI), ("WoutT", 2 * 128), ("FF1", 128),
           ("FF2", 128), ("wr", 2 * 128), ("w1", 2 * HF), ("w2", 2 * D), ("ident", 128), ("ones", 128),
           ("cmask", 128 // L), ("eyes", DS), ("before", 128), ("after", 128), ("b2row", D), ("brow", E), ("A_log", DS),
           ("conv_w", KC), ("cols", 16)]
EXPERTS = [("E1", E * 128), ("E2", E * 128), ("E3", E * 128)]
COLS = ["bq", "bk", "bv", "bi", "bf", "bo", "ib", "ns", "br", "conv_b", "b_dt", "Dm", "ff1b", "ff2b", "b1a", "b1b"]
BN = ["b1", "b2", "g1", "g2", "be1", "be2", "m1", "m2", "v1", "v2"]


def places(sizes):
    at, out = 0, {}
    for name, n in sizes:
        out[name] = (at, n)
        at += n
    return out, at


def build(nc, x, txt, wdft, wts, wexp, bn, out, dbg=None):
    lay, nw = places(WEIGHTS)
    elay, ne = places(EXPERTS)
    with ExitStack() as ctx:
        def sb(name, shape, dt=F32):
            return ctx.enter_context(nc.sbuf_tensor(name, shape, dt))

        sems = {}

        def s(name):
            if name not in sems:
                sems[name] = ctx.enter_context(nc.semaphore(name))
            return sems[name]

        PS = ctx.enter_context(nc.psum_tensor("PS", [128, 8, 512], F32))
        W_ = sb("weights", [128, nw])

        def w(name):
            a, n = lay[name]
            return W_[:, a:a + n]

        def col(name):
            a = lay["cols"][0] + COLS.index(name)
            return W_[:, a:a + 1]

        H = sb("hidden", [128, NPAIR, SP])
        pool_ = sb("pair_arrays", [128, 10, NPAIR, SP])
        P1, P2, P3, P4, P5, P6, P7, P8, P9, P10 = (pool_[:, i] for i in range(10))
        big = sb("big", [128, 2 * NPAIR * D * NC])
        Wt = sb("token_weights", [128, PATCH * 128])
        bnw = sb("bn_params", [128, len(BN), E])
        bns = sb("bn_scale", [128, 2, E])
        bnb = sb("bn_shift", [128, 2, E])
        cst = sb("constants", [128, 6])
        EPS5, EPS8, ONE, EPS3, HALF_LN, LN_EDGE = (cst[:, i:i + 1] for i in range(6))
        gbias = sb("gate_bias", [128, 2])
        txt_sb = sb("txt_rows", [TXT, B * D])
        dend = sb("chunk_decay", [128, NPAIR, NC])
        aneg = sb("A_negative", [128, DS])
        wcol = sb("router_cols", [128, B, NT])
        one_bf = sb("ones_bf16", [128, 1], BF16)
        sel = sb("selected", [128, B * NT])
        ytmp = sb("y_rows", [128, 2, 4, D])
        dram_decay = nc.dram_tensor("decay_rows", [NPAIR, 2, D * NC], F32, kind="Internal").ap()

        xs = big[:, 0:NPAIR * (T + PAD) * V].rearrange("p (a t v) -> p a t v", a=NPAIR, t=T + PAD)
        wd = P1.rearrange("p a t -> p (a t)")[:, 0:NOG * 128]
        dft = P1.rearrange("p a t -> p (a t)")[:, NOG * 128:NOG * 128 + OG * PATCH]
        q_, k_, v_, li, r_, so, lf, m_, fs = P2, P3, P4, P5, P6, P7, P8, P9, P10
        ik, n_, rden = P1, P6, P9
        WV = [P4, P8]
        ve, dfw, hr = P1, P5, P6
        DBC = big[:, 0:NPAIR * D * NC].rearrange("p (a n) -> p a n", a=NPAIR)
        UM = big[:, NPAIR * D * NC:].rearrange("p (a n) -> p a n", a=NPAIR)
        UMc = big[:, NPAIR * D * NC:].rearrange("p (a i c) -> p a i c", a=NPAIR, i=D)
        lagmem = big[:, NPAIR * D * NC:]
        prod = [lagmem[:, i * SP:(i + 1) * SP] for i in range(4)]
        term = [lagmem[:, (4 + i) * SP:(5 + i) * SP] for i in range(2)]
        rows_t = [Wt[:, i * 256:(i + 1) * 256] for i in range(2)]
        spread = [Wt[:, 512 + i * 512:1024 + i * 512] for i in range(2)]
        NL = NPAIR * L
        EW = big[:, 0:ne]

        def ew(name, e):
            a = elay[name][0] + e * 128
            return EW[:, a:a + 128]

        def twin(a, i):
            return a.rearrange("p a t -> p (a t)")[:, i * NPAIR * G:(i + 1) * NPAIR * G].rearrange("p (a t) -> p a t", a=NPAIR)

        h1b, h2b, hwb = P2, P3, P4
        gate = P6.rearrange("p a t -> p (a t)")
        lg = gate[:, 0:NT * E].rearrange("p (j e) -> p j e", e=E)
        gmax, gsum = gate[:, 128:128 + NT], gate[:, 160:160 + NT]
        wT = P5[:, 0, :]
        pick8 = big[:, ne:ne + E * 128]
        tstart = [min(128 * j, SP - 128) for j in range(NT)]
        def batch_array(i, b):
            return big[:, (4 * i + b) * SP:(4 * i + b + 1) * SP]

        assert 16 * SP <= 2 * NPAIR * D * NC
        SBC = pool_[:, 3:5].rearrange("p s a t -> p s (a t)").bitcast(BF16)

        def bc(b):
            return SBC[:, :, b * SP:(b + 1) * SP]

        pick = Wt[:, :].bitcast(BF16)
        diagD = sb("D_diagonal", [128, 128])
        dlo_sb = sb("dt_low_rank", [128, 2, G])
        dlo_low = sb("low_parts", [128, 2, SP])
        xcp = [a.rearrange("p a t -> p (a t)") for a in (P6, P7)]
        conv = [P8[:, i] for i in range(2)]
        dlo = [dlo_sb[:, i, :] for i in range(2)]
        resid = [P6, P7]
        expo, frelu, logs = (P8, P9), (P1, P10), (P2, P3)

        def pair_of(i, p):
            return big[:, (4 * i + 2 * p) * SP:(4 * i + 2 * p + 2) * SP].rearrange("q (b t) -> q b t", b=2)

        ring_mem = [pool_[:, a:b].rearrange("p s a t -> p (s a t)") for a, b in ((5, 9), (0, 3))]

        def ring(mem, i):
            n = 2 * NPS * G
            return [ring_mem[mem][:, i * n:(i + 1) * n].rearrange("p (c h t) -> p c h t", c=NPS, h=2)[:, c] for c in range(NPS)]

        hbuf, hcbuf, cbuf, decays, bx = ring(0, 0), ring(0, 1), ring(0, 2), ring(1, 0), ring(1, 1)
        B_BANKS = (2, 6)
        low_tmp = dlo_low[96:128]
        carry = sb("scan_carry", [128, DS])

        def at(i, seg):
            return big[:, 4 * i * SP + seg * G:4 * i * SP + (seg + 1) * G]

        wrow = [(P5, P6)[b // 2][:, b % 2] for b in range(B)]
        hid = [P7, P8, P9, P10]
        RES = big[:, 0:B * NT * D].rearrange("p (b j d) -> p b j d", b=B, j=NT)
        beats = [big[:, 4096 + i * 640:4096 + i * 640 + SP // 2].bitcast(BF16) for i in range(2)]
        beats_own = [big[:, 5400 + i * 64:5464 + i * 64].bitcast(BF16) for i in range(2)]
        rank_row = big[0:1, 6144:6144 + B * SP].rearrange("p (b t) -> p b t", b=B)
        ROWS = [(128, [(b, 4 * i + j) for j in range(4)]) for b in range(B) for i in range(2)] + \
               [(LAST, [(b, NT - 1) for b in range(B)])]
        BANKS = [(0, 512), (512, 1024), (1024, S)]

        groups = [(p, k) for p in range(NPAIR) for k in range(NG)]
        NGR = len(groups)

        def cols(k):
            return slice(k * G, (k + 1) * G)

        def half(b):
            return slice(64 * (b % 2), 64 * (b % 2) + 64)

        def chunks(a):
            return a.rearrange("p (c r) -> p c r", r=L)

        def stepper(eng, name):
            n = [0]

            def step(ins):
                n[0] += 1
                ins.then_inc(s(name), 1)
                eng.wait_ge(s(name), n[0])
            return step

        def seq_of(e):
            return e * 128, min(128, SP - e * 128)

        def ln_pe(pe, n, ready, sq):
            for g in range(NGR + 1):
                if g < NGR:
                    p, k = groups[g]
                    ready(g)
                    if g >= 2:
                        pe.wait_ge(s("ln_centred"), NGR * (n - 1) + g - 1)
                    nc.tensor.matmul(PS[:, g % 2, 0:G], w("ones"), H[:, p, cols(k)],
                                     start=True, stop=True).then_inc(s("ln_mean"), 1)
                if g >= 1:
                    p, k = groups[g - 1]
                    pe.wait_ge(s("ln_sq"), NGR * (n - 1) + g)
                    if g >= 3:
                        pe.wait_ge(s("ln_ln"), NGR * (n - 1) + g - 2)
                    nc.tensor.matmul(PS[:, 2 + (g - 1) % 2, 0:G], w("ones"), sq[:, p, cols(k)],
                                     start=True, stop=True).then_inc(s("ln_var"), 1)

        def ln_act(act, n, xc, sq, rs):
            for g in range(NGR + 1):
                if g < NGR:
                    p, k = groups[g]
                    act.wait_ge(s("ln_centred"), NGR * (n - 1) + g + 1)
                    nc.scalar.activation(sq[:, p, cols(k)], xc[:, p, cols(k)], ACT.Square).then_inc(s("ln_sq"), 1)
                if g >= 1:
                    p, k = groups[g - 1]
                    act.wait_ge(s("ln_var"), NGR * (n - 1) + g)
                    nc.scalar.activation(rs[:, p, cols(k)], PS[:, 2 + (g - 1) % 2, 0:G], ACT.Ln, bias=EPS5,
                                         scale=1.0 / D).then_inc(s("ln_ln"), 1)
            act.wait_ge(s("ln_ln"), NGR * n)
            for p, k in groups:
                nc.scalar.activation(rs[:, p, cols(k)], rs[:, p, cols(k)], ACT.Exp,
                                     scale=-0.5).then_inc(s("ln_rs"), 1)

        def ln_dve(dve, n, xc, rs):
            for g, (p, k) in enumerate(groups):
                dve.wait_ge(s("ln_mean"), NGR * (n - 1) + g + 1)
                nc.vector.scalar_tensor_tensor(xc[:, p, cols(k)], PS[:, g % 2, 0:G], -1.0 / D, H[:, p, cols(k)],
                                               ALU.mult, ALU.add).then_inc(s("ln_centred"), 1)
            for g, (p, k) in enumerate(groups):
                dve.wait_ge(s("ln_rs"), NGR * (n - 1) + g + 1)
                nc.vector.tensor_tensor(xc[:, p, cols(k)], xc[:, p, cols(k)], rs[:, p, cols(k)],
                                        ALU.mult).then_inc(s("ln_out"), 1)

        block = ctx.enter_context(nc.Block())

        @block.sync
        def _(sp):
            sp.dma_start(P1.rearrange("p a t -> p (a t)")[:, 0:NOG * 128 + OG * PATCH], wdft).then_inc(s("w_dft_in"), 16)
            xv = x.rearrange("(a b) c t v -> a (b c) t v", a=NPAIR)
            split = T // 2 + PAD
            for p in range(NPAIR):
                sp.dma_start(xs[:, p, 0:split, :], xv[p, :, 0:split, :]).then_inc(s(f"x_low{p}"), 16)
                sp.dma_start(xs[:, p, split:T, :], xv[p, :, split:, :]).then_inc(s(f"x_high{p}"), 16)
                if p == 0:
                    sp.dma_start(W_[:, :], wts).then_inc(s("w_in"), 16)
                    sp.dma_start(txt_sb[:, :].rearrange("t (b d) -> t b d", b=B),
                                 txt.rearrange("b t d -> t b d")).then_inc(s("txt_in"), 16)
            sp.dma_start(bnw[:, :, :].rearrange("p a b -> p (a b)"), bn).then_inc(s("bn_in"), 16)
            sp.wait_ge(s("dend_ready"), 1)
            for p in range(NPAIR):
                sp.dma_start(dram_decay[p].rearrange("b (i c) -> (b i) c", i=D),
                             dend[:, p, :]).then_inc(s("dend_out"), 16)
            sp.wait_ge(s("dend_out"), 16 * NPAIR)
            sp.wait_ge(s("tok_ps"), 4)
            for p in range(NPAIR):
                for b2 in range(2):
                    sp.dma_start(DBC[64 * b2:64 * b2 + 64, p, :],
                                 dram_decay[p, b2:b2 + 1, :].to_broadcast([64, D * NC])).then_inc(s("decay_in"), 16)
            sp.wait_ge(s("states"), NPAIR)
            sp.dma_start(EW, wexp).then_inc(s("experts_in"), 16)
            for x_, (n, members) in enumerate(ROWS):
                b, j = members[0]
                sp.wait_ge(s("rows_ready"), x_ + 1)
                if n == 128:
                    sp.dma_start(out[b, 128 * j:128 * (j + 4), :].rearrange("(j p) d -> p j d", p=128),
                                 RES[:, b, j:j + 4, :]).then_inc(s("out_done"), 16)
                else:
                    sp.dma_start(out[:, 128 * j:S, :].rearrange("b p d -> p b d"), RES[0:n, :, j, :]).then_inc(s("out_done"), 16)
            sp.wait_ge(s("out_done"), 16 * len(ROWS))

        @block.tensor
        def _(pe):
            pe.wait_ge(s("w_dft_in"), 16)
            for g in range(NOG):
                last = nc.tensor.matmul(PS[:, 4 + g // 4, (g % 4) * OG * PATCH:(g % 4 + 1) * OG * PATCH],
                                        wd[:, g * 128:(g + 1) * 128], dft, start=True, stop=True)
            last.then_inc(s("wtok_ps"), 1)
            pe.wait_ge(s("wtok_sb"), 6)
            for p in range(NPAIR):
                for hf in range(2):
                    pe.wait_ge(s(f"x_low{p}"), 16)
                    if hf:
                        pe.wait_ge(s(f"x_high{p}"), 16)
                        pe.wait_ge(s("x_pad"), p + 1)
                    for t in range(PATCH):
                        t0 = hf * 64 + t
                        last = nc.tensor.matmul(PS[:, 2 * p + hf, :], Wt[:, t * 128:(t + 1) * 128],
                                                xs[:, p, t0:t0 + 57:STRIDE, :], start=(t == 0), stop=(t == PATCH - 1))
                    last.then_inc(s("tok_ps"), 1)
            pe.wait_ge(s("w_in"), 16)
            pe.wait_ge(s("txt_in"), 16)
            for p in range(NPAIR):
                last = nc.tensor.transpose(PS[:, 7, p * TXT:(p + 1) * TXT], txt_sb[:, p * 128:(p + 1) * 128],
                                           w("ident")[0:TXT, 0:TXT])
            last.then_inc(s("txt_ps"), 1)

            def ready1(g):
                if g == 0:
                    pe.wait_ge(s("tok_ev"), 4)
                    pe.wait_ge(s("txt_ev"), 2)
            ln_pe(pe, 1, ready1, P2)

            for r, (wa, wv) in enumerate((("Wi", "Wq"), ("Wf", "Wk"), ("Wo", "Wv"))):
                for g, (p, k) in enumerate(groups):
                    m = r * NGR + g
                    pe.wait_ge(s("ln_out"), g + 1)
                    if m >= 2:
                        pe.wait_ge(s("gates_ev"), m - 1)
                    nc.tensor.matmul(PS[:, 4 + m % 2, 0:G], w(wa), P1[:, p, cols(k)],
                                     start=True, stop=True).then_inc(s("gates_ps"), 1)
                    if m >= 2:
                        pe.wait_ge(s("qkv_ev"), m - 1)
                    nc.tensor.matmul(PS[:, 6 + m % 2, 0:G], w(wv), P1[:, p, cols(k)],
                                     start=True, stop=True).then_inc(s("qkv_ps"), 1)
            pe.wait_ge(s("qkv_ev"), 3 * NGR)
            for g, (p, k) in enumerate(groups):
                pe.wait_ge(s("nq_ready"), p + 1)
                if g >= 2:
                    pe.wait_ge(s("den_ev"), g - 1)
                nc.tensor.matmul(PS[:, 6 + g % 2, 0:G], w("ones"), ik[:, p, cols(k)],
                                 start=True, stop=True).then_inc(s("den_ps"), 1)
            pe.wait_ge(s("gates_ev"), 3 * NGR)
            for n in range(NL):
                lag, p = n // NPAIR, n % NPAIR
                size = CG * (L - lag)
                pe.wait_ge(s("lag_prod"), n + 1)
                if n >= NPAIR:
                    pe.wait_ge(s("lag_read"), n - 1)
                for k in range(NG):
                    last = nc.tensor.matmul(PS[:, NG * p + k, 0:size], w("ones"), prod[n % 4][:, k * size:(k + 1) * size],
                                            start=True, stop=True)
                last.then_inc(s("lag_ps"), 1)
            pe.wait_ge(s("lag_ve"), NL)
            pe.wait_ge(s("den_ev"), NGR)
            pe.wait_ge(s("lag_read"), NL)

            def turn(u):
                p, (t0, n) = u // NT, seq_of(u % NT)
                if u >= 2:
                    pe.wait_ge(s("rows_ev"), u - 1)
                nc.tensor.transpose(PS[0:n, 6 + u % 2, 0:128], ve[:, p, t0:t0 + n], w("ident"))
                nc.tensor.transpose(PS[0:n, 6 + u % 2, 128:256], k_[:, p, t0:t0 + n], w("ident")).then_inc(s("rows_ps"), 1)

            turn(0)
            for u in range(NPAIR * NT):
                n = seq_of(u % NT)[1]
                if u + 1 < NPAIR * NT:
                    turn(u + 1)
                for b2 in range(2):
                    y = 2 * u + b2
                    pe.wait_ge(s("spread_ready"), y + 1)
                    if y >= 4:
                        pe.wait_ge(s("u_ev"), y - 3)
                    nc.tensor.matmul(PS[:, y % 4, 0:n // L * D], rows_t[u % 2][0:n, 128:256], spread[b2][0:n, 0:n // L * D],
                                     start=True, stop=True).then_inc(s("u_mm"), 1)
            pe.wait_ge(s("u_ev"), 4 * NT)
            for p in range(NPAIR):
                pe.wait_ge(s("states"), p + 1)
                for c in range(1, NC):
                    for b2 in range(2):
                        h = half(b2)
                        last = nc.tensor.matmul(PS[h, NG * p + c // CG, (c % CG) * L:(c % CG + 1) * L],
                                                UMc[h, p, :, c - 1], q_[h, p, c * L:(c + 1) * L], start=True, stop=True)
                last.then_inc(s("inter_ps"), 1)
            for g, (p, k) in enumerate(groups):
                pe.wait_ge(s("msq_in"), p + 1)
                if g >= 2:
                    pe.wait_ge(s("rms_ev"), g - 1)
                nc.tensor.matmul(PS[:, 6 + g % 2, 0:G], w("ones"), WV[1][:, p, cols(k)],
                                 start=True, stop=True).then_inc(s("msq_ps"), 1)

            def ready2(g):
                pe.wait_ge(s("mlstm_out"), g + 1)
                if g == 0:
                    pe.wait_ge(s("inter_ev"), NPAIR)
            ln_pe(pe, 2, ready2, P2)

            pe.wait_ge(s("ln_out"), 2 * NGR)
            for j in range(NT):
                for p in range(NPAIR):
                    last = nc.tensor.matmul(PS[:, 4, j * E:(j + 1) * E], P1[:, p, tstart[j]:tstart[j] + 128], w("Wr"),
                                            start=(p == 0), stop=(p == NPAIR - 1))
            last.then_inc(s("logit_ps"), 1)
            pe.wait_ge(s("gate_ready"), 1)
            for j in range(NT):
                last = nc.tensor.transpose(PS[0:E, 5 + j // 4, (j % 4) * 128:(j % 4 + 1) * 128], lg[:, j, :], w("ident"))
            last.then_inc(s("gateT_ps"), 1)
            pe.wait_ge(s("experts_in"), 16)
            pe.wait_ge(s("gateT"), 2)
            pe.wait_ge(s("ln_ln"), 2 * NGR)
            NX = NG * E

            def layer1(n):
                if n >= 1:
                    pe.wait_ge(s("h1_ev"), n)
                for p in range(NPAIR):
                    last = nc.tensor.matmul(PS[:, 2 + p, 0:G], ew("E1", n % E), P1[:, p, cols(n // E)],
                                            start=True, stop=True)
                last.then_inc(s("l1_ps"), 1)

            def layer2(n):
                pe.wait_ge(s("h1_ev"), n + 1)
                if n >= 1:
                    pe.wait_ge(s("h2_ev"), n)
                for p in range(NPAIR):
                    last = nc.tensor.matmul(PS[:, 4 + p, 0:G], ew("E2", n % E), twin(h1b, n % 2)[:, p, :],
                                            start=True, stop=True)
                last.then_inc(s("l2_ps"), 1)

            def spread_weight(n):
                if n >= 2:
                    pe.wait_ge(s("hw_ready"), n - 1)
                nc.tensor.matmul(PS[:, 6 + n % 2, 0:G], pick8[:, (n % E) * 128:(n % E + 1) * 128], wT[:, cols(n // E)],
                                 start=True, stop=True).then_inc(s("spread_w"), 1)

            def layer3(n):
                k, e = n // E, n % E
                pe.wait_ge(s("hw_ready"), n + 1)
                if e == 0 and k >= 1:
                    pe.wait_ge(s("ffn_out"), k)
                for p in range(NPAIR):
                    last = nc.tensor.matmul(PS[:, p, 0:G], ew("E3", e), twin(hwb, n % 2)[:, p, :],
                                            start=(e == 0), stop=False)
                    if e == E - 1:
                        last = nc.tensor.matmul(PS[:, p, 0:G], w("ebias"), wT[:, cols(k)], start=False, stop=True)
                last.then_inc(s("l3_ps"), 1)

            layer1(0)
            spread_weight(0)
            for n in range(NX):
                layer2(n)
                if n + 1 < NX:
                    layer1(n + 1)
                    spread_weight(n + 1)
                if n >= 1:
                    layer3(n - 1)
            layer3(NX - 1)

            def ready3(g):
                pe.wait_ge(s("ffn_out"), g % NG + 1)
                if g == 0:
                    pe.wait_ge(s("ffn_out"), NG)
            ln_pe(pe, 3, ready3, P2)

            pe.wait_ge(s("ln_out"), 3 * NGR)
            for m in range(B * NG):
                b, k = m // NG, m % NG
                xin = P1[:, b // 2, cols(k)]
                win = w("Win")[:, (b % 2) * 2 * DI:(b % 2 + 1) * 2 * DI]
                if m >= 2:
                    pe.wait_ge(s("xc_ev"), m - 1)
                nc.tensor.matmul(PS[:, m % 2, 0:G], win[:, 0:DI], xin, start=True, stop=True).then_inc(s("xc_ps"), 1)
                if m >= 2:
                    pe.wait_ge(s("z_ev"), m - 1)
                nc.tensor.matmul(PS[:, 2 + m % 2, 0:G], win[:, DI:2 * DI], xin,
                                 start=True, stop=True).then_inc(s("z_ps"), 1)
            pe.wait_ge(s("xc_ev"), B * NG)
            pe.wait_ge(s("z_ev"), B * NG)
            for m in range(B * NG + 1):
                if m < B * NG:
                    b, k = m // NG, m % NG
                    u = batch_array(0, b)[:, cols(k)]
                    pe.wait_ge(s("u_ready"), b + 1)
                    if m >= 2:
                        pe.wait_ge(s("bc_left"), m - 1)
                        pe.wait_ge(s("dlo_ev"), m - 1)
                    nc.tensor.matmul(PS[:, 4 + m % 2, 0:G], w("XD"), u, start=True, stop=True).then_inc(s("dlo_ps"), 1)
                    nc.tensor.matmul(PS[:, 2 * (m % 2), 0:G], w("XB"), u, start=True, stop=True)
                    nc.tensor.matmul(PS[:, 2 * (m % 2) + 1, 0:G], w("XC"), u, start=True, stop=True).then_inc(s("bc_ps"), 1)
                if m >= 1:
                    pe.wait_ge(s("dlo_ev"), m)
                    if m >= 3:
                        pe.wait_ge(s("dt_abs"), m - 2)
                        pe.wait_ge(s("dt_relu"), m - 2)
                    nc.tensor.matmul(PS[:, 6 + (m - 1) % 2, 0:G], w("WdtT"), dlo[(m - 1) % 2],
                                     start=True, stop=True).then_inc(s("dt_ps"), 1)
            pe.wait_ge(s("pick_ready"), 1)
            pe.wait_ge(s("bc_ready"), B)
            pe.wait_ge(s("dt_abs"), B * NG)
            pe.wait_ge(s("dt_relu"), B * NG)
            pe.wait_ge(s("diag_ready"), 1)

            def spread_pair(kind, seg, n, c):
                bank = 4 if kind else B_BANKS[c % 2]
                for h in range(2):
                    last = nc.tensor.matmul(PS[:, bank + h, 0:G], pick[:, bass.ds((n * (2 * NPS) + (2 * c + h)) * 128, 128)],
                                            SBC[:, kind, seg * G:(seg + 1) * G], start=True, stop=True)
                return last

            def add_y(seg, n, c, h, stop):
                if h == 0:
                    pe.wait_ge(s("hc_ready"), n * NPS + (NPS * NS * seg + c + 1))
                last = nc.tensor.matmul(PS[:, seg % 2, 0:G], w("ident"), hcbuf[c][:, h, :],
                                        start=False, stop=stop, skip_group_check=True)
                if h:
                    last.then_inc(s("y_added"), 1)

            def step_pe(seg, n, add):
                first = seg == 0 and add is None
                for c in range(NPS):
                    if not (first and c < 2):
                        pe.wait_ge(s("b_used"), n * NPS + (NPS * NS * seg + c - 1))
                    spread_pair(0, seg, n, c).then_inc(s("b_spread"), 1)
                    if add is not None:
                        add_y(*add, c, 0, False)
                    if not (first and c == 0):
                        pe.wait_ge(s("c_copied"), n * NPS + (NPS * NS * seg + c))
                    spread_pair(1, seg, n, c).then_inc(s("c_spread"), 1)
                    if add is not None:
                        add_y(*add, c, 1, add[0] < seg and c == NPS - 1)

            for seg in range(NSEG):
                step_pe(seg, 0, (seg - 1, NS - 1) if seg else None)
                if seg >= 2:
                    pe.wait_ge(s("ys_ready"), seg - 1)
                nc.tensor.matmul(PS[:, seg % 2, 0:G], diagD[:, :], at(0, seg), start=True, stop=False,
                                 skip_group_check=True)
                with pe.Fori(1, NS) as n:
                    step_pe(seg, n, (seg, n - 1))
            for c in range(NPS):
                for h in range(2):
                    add_y(NSEG - 1, NS - 1, c, h, c == NPS - 1 and h == 1)
            pe.wait_ge(s("ys_ready"), NSEG)
            for g in range(NGR + 2):
                if g < NGR:
                    p, k = groups[g]
                    if g >= 2:
                        pe.wait_ge(s("mo_ev"), g - 1)
                    for b2 in range(2):
                        last = nc.tensor.matmul(PS[:, g % 2, 0:G], w("WoutT")[:, b2 * 128:(b2 + 1) * 128],
                                                batch_array(3, 2 * p + b2)[:, cols(k)], start=(b2 == 0), stop=(b2 == 1))
                    last.then_inc(s("mo_ps"), 1)
                if 1 <= g <= NGR:
                    p, k = groups[g - 1]
                    pe.wait_ge(s("mo_ev"), g)
                    if g >= 3:
                        pe.wait_ge(s("ff1_ev"), g - 2)
                    nc.tensor.matmul(PS[:, 2 + (g - 1) % 2, 0:G], w("FF1"), P1[:, p, cols(k)],
                                     start=True, stop=True).then_inc(s("ff1_ps"), 1)
                if g >= 2:
                    p, k = groups[g - 2]
                    pe.wait_ge(s("ff1_out"), g - 1)
                    if g >= 4:
                        pe.wait_ge(s("ff2_ev"), g - 3)
                    nc.tensor.matmul(PS[:, 4 + g % 2, 0:G], w("FF2"), P3[:, p, cols(k)],
                                     start=True, stop=True).then_inc(s("ff2_ps"), 1)

            def ready4(g):
                pe.wait_ge(s("mamba_out"), g + 1)
            ln_pe(pe, 4, ready4, P2)

            pe.wait_ge(s("ln_out"), 4 * NGR)
            for m in range(B * NG):
                b, k = m // NG, m % NG
                if m >= 2:
                    pe.wait_ge(s("wrow_ev"), m - 1)
                nc.tensor.matmul(PS[:, m % 2, 0:G], w("wr")[:, (b % 2) * 128:(b % 2 + 1) * 128], P1[:, b // 2, cols(k)],
                                 start=True, stop=True).then_inc(s("wrow_ps"), 1)
            pe.wait_ge(s("wrow_ev"), B * NG)
            for b in range(B):
                for j in range(NT):
                    t0, n = j * 128, (128 if j < NT - 1 else LAST)
                    last = nc.tensor.transpose(PS[0:n, 2, b * NT + j:b * NT + j + 1], wrow[b][0:1, t0:t0 + n],
                                               w("ident")[0:1, 0:1])
            last.then_inc(s("wcol_ps"), 1)
            RANK_BANKS = (3, 6, 7)

            def own_beats(x_, j, n):
                return nc.tensor.matmul(PS[0:1, RANK_BANKS[j // 4], (j % 4) * 128:(j % 4) * 128 + n], one_bf[0:n, :],
                                        beats_own[x_ % 2][0:n, 0:n], start=False, stop=False)

            def hidden(b):
                for y in range(2 * NG):
                    m = b * 2 * NG + y
                    if m >= 2:
                        pe.wait_ge(s("hid_ready"), m - 1)
                    nc.tensor.matmul(PS[:, 4 + m % 2, 0:G], w("w1")[:, (b % 2) * HF + (y // NG) * 128:(b % 2) * HF + (y // NG + 1) * 128],
                                     P1[:, b // 2, cols(y % NG)], start=True, stop=True).then_inc(s("hid_ps"), 1)

            hidden(0)
            for b in range(B):
                if b >= 1:
                    pe.wait_ge(s("rank_ev"), b)
                for j in range(NT):
                    x_ = b * NT + j
                    n = 128 if j < NT - 1 else LAST
                    pe.wait_ge(s("beats_ready"), x_ + 1)
                    for i, (a, z) in enumerate(BANKS):
                        if i == j // 4 and j:
                            own_beats(x_, j, n)
                        last = nc.tensor.matmul(PS[0:1, RANK_BANKS[i], 0:z - a], one_bf[0:n, :], beats[x_ % 2][0:n, a:z],
                                                start=(j == 0), stop=(j == NT - 1))
                        if i == j // 4 and not j:
                            last = own_beats(x_, j, n)
                    last.then_inc(s("rank_ps"), 1)
                if b + 1 < B:
                    hidden(b + 1)
            pe.wait_ge(s("rank_ev"), B)
            for b in range(B):
                for j in range(NT):
                    t0, n = j * 128, (128 if j < NT - 1 else LAST)
                    last = nc.tensor.transpose(PS[0:n, 1, b * NT + j:b * NT + j + 1], rank_row[:, b, t0:t0 + n],
                                               w("ident")[0:1, 0:1])
            last.then_inc(s("rank_cols"), 1)
            pe.wait_ge(s("residual"), 1)
            pe.wait_ge(s("hid_ready"), B * 2 * NG)
            for x_, (n, members) in enumerate(ROWS):
                if x_ >= 4:
                    pe.wait_ge(s("rows_ready"), x_ - 3)
                for i, (b, j) in enumerate(members):
                    t0 = j * 128
                    for hh in range(2):
                        nc.tensor.matmul(PS[0:n, 2 + x_ % 4, i * D:(i + 1) * D], hid[b][:, hh, t0:t0 + n],
                                         w("w2")[:, hh * D:(hh + 1) * D], start=(hh == 0), stop=(hh == 1))
                    if n == 128:
                        last = nc.tensor.transpose(PS[0:n, 2 + x_ % 4, (4 + i) * D:(5 + i) * D], P4[half(b), b // 2, t0:t0 + n],
                                                   w("ident")[half(b), half(b)])
                    elif b % 2:
                        last = nc.tensor.transpose(PS[0:n, 2 + x_ % 4, (3 + i) * D:(5 + i) * D], P4[:, b // 2, t0:t0 + n],
                                                   w("ident"))
                last.then_inc(s("rows_out_ps"), 1)

        @block.scalar
        def _(act):
            step = stepper(act, "act_step")

            def f(o, i, fn, **kw):
                return nc.scalar.activation(o, i, fn, **kw)

            act.wait_ge(s("const_ready"), 1)
            for p in range(NPAIR):
                act.wait_ge(s(f"x_high{p}"), 16)
                f(xs[:, p, T:T + PAD, :], xs[:, p, T - 1:T, :].to_broadcast([128, PAD, V]), ACT.Copy).then_inc(s("x_pad"), 1)
                for hf in range(2):
                    act.wait_ge(s("tok_ps"), 2 * p + hf + 1)
                    f(H[:, p, 0:TOK].rearrange("q (v n) -> q n v", n=NP_)[:, 8 * hf:8 * hf + 8, :],
                      PS[:, 2 * p + hf, :].rearrange("q (n v) -> q n v", n=8), ACT.Copy).then_inc(s("tok_ev"), 1)
            ln_act(act, 1, P1, P2, P3)
            act.wait_ge(s("gbias_ready"), 1)
            act.wait_ge(s("ln_out"), NGR)
            for g, (p, k) in enumerate(groups):
                act.wait_ge(s("gates_ps"), g + 1)
                f(li[:, p, cols(k)], PS[:, 4 + g % 2, 0:G], ACT.Tanh, bias=gbias[:, 0:1], scale=0.1).then_inc(s("gates_ev"), 1)
            for g, (p, k) in enumerate(groups):
                m = NGR + g
                act.wait_ge(s("gates_ps"), m + 1)
                f(fs[:, p, cols(k)], PS[:, 4 + m % 2, 0:G], ACT.Abs, bias=col("bf"))
                f(r_[:, p, cols(k)], PS[:, 4 + m % 2, 0:G], ACT.Relu, bias=col("bf")).then_inc(s("gates_ev"), 1)
            act.wait_ge(s("gates_ev"), 2 * NGR)
            step(f(fs, fs, ACT.Exp, scale=-1.0))
            f(lf, fs, ACT.Ln, bias=ONE).then_inc(s("softplus"), 1)
            for g, (p, k) in enumerate(groups):
                m = 2 * NGR + g
                act.wait_ge(s("gates_ps"), m + 1)
                f(so[:, p, cols(k)], PS[:, 4 + m % 2, 0:G], ACT.Sigmoid, bias=col("bo")).then_inc(s("gates_ev"), 1)
            act.wait_ge(s("exponents"), 1)
            f(fs, fs, ACT.Exp).then_inc(s("factors"), 1)
            act.wait_ge(s("exponents"), 2)
            f(li, li, ACT.Exp).then_inc(s("factors"), 1)
            for g, (p, k) in enumerate(groups):
                act.wait_ge(s("den_ps"), g + 1)
                f(rden[:, p, cols(k)], PS[:, 6 + g % 2, 0:G], ACT.Abs).then_inc(s("den_ev"), 1)
            act.wait_ge(s("den_max"), 1)
            step(f(rden, rden, ACT.Ln))
            f(rden, rden, ACT.Exp, scale=-1.0).then_inc(s("rden_ready"), 1)
            act.wait_ge(s("iv_ready"), 1)
            for n in range(NL):
                lag, p = n // NPAIR, n % NPAIR
                if lag:
                    act.wait_ge(s("lag_w"), n - 1)
                f(chunks(ve[:, p, :])[:, :, L - 1 - lag], chunks(WV[lag % 2][:, p, :])[:, :, L - 1],
                  ACT.Copy).then_inc(s("lag_ve"), 1)
            act.wait_ge(s("lag_sum"), NL - NPAIR)
            act.wait_ge(s("lag_ps"), NL)
            for u in range(NPAIR * NT + 1):
                if u < NPAIR * NT:
                    n = seq_of(u % NT)[1]
                    act.wait_ge(s("rows_ps"), u + 1)
                    if u >= 2:
                        act.wait_ge(s("u_mm"), 2 * (u - 1))
                    f(rows_t[u % 2][0:n, :], PS[0:n, 6 + u % 2, 0:256], ACT.Copy).then_inc(s("rows_ev"), 1)
                if u >= 1:
                    p, j = (u - 1) // NT, (u - 1) % NT
                    ncs = seq_of(j)[1] // L
                    for b2 in range(2):
                        y = 2 * (u - 1) + b2
                        act.wait_ge(s("u_mm"), y + 1)
                        f(UMc[half(b2), p, :, 8 * j:8 * j + ncs],
                          PS[half(b2), y % 4, 0:ncs * D].rearrange("q (c i) -> q i c", i=D), ACT.Copy).then_inc(s("u_ev"), 1)
            for p in range(NPAIR):
                act.wait_ge(s("gated"), p + 1)
                f(WV[1][:, p, :], hr[:, p, :], ACT.Square).then_inc(s("msq_in"), 1)
            for g, (p, k) in enumerate(groups):
                act.wait_ge(s("msq_ps"), g + 1)
                f(fs[:, p, cols(k)], PS[:, 6 + g % 2, 0:G], ACT.Ln, bias=EPS8, scale=RMS_SCALE / D).then_inc(s("rms_ev"), 1)
            act.wait_ge(s("rms_ev"), NGR)
            for p, k in groups:
                f(fs[:, p, cols(k)], fs[:, p, cols(k)], ACT.Exp, bias=HALF_LN, scale=-0.5).then_inc(s("rms_ready"), 1)
            ln_act(act, 2, P1, P2, P3)
            act.wait_ge(s("bn_in"), 16)
            f(bns[:, :, :], bnw[:, 8:10, :], ACT.Sqrt, bias=EPS3).then_inc(s("bn_sd"), 1)
            act.wait_ge(s("logits"), 1)
            f(lg, lg, ACT.Exp).then_inc(s("gate_exp"), 1)
            act.wait_ge(s("bn_ready"), 1)
            act.wait_ge(s("ln_out"), 2 * NGR)

            def hidden1(n):
                act.wait_ge(s("l1_ps"), n + 1)
                if n >= 2:
                    act.wait_ge(s("l2_ps"), n - 1)
                e = n % E
                f(twin(h1b, n % 2), PS[:, 2:4, 0:G], ACT.Relu, bias=bnb[:, 0, e:e + 1],
                  scale=bns[:, 0, e:e + 1]).then_inc(s("h1_ev"), 1)

            def hidden2(n):
                act.wait_ge(s("l2_ps"), n + 1)
                if n >= 2:
                    act.wait_ge(s("hw_ready"), n - 1)
                e = n % E
                f(twin(h2b, n % 2), PS[:, 4:6, 0:G], ACT.Relu, bias=bnb[:, 1, e:e + 1],
                  scale=bns[:, 1, e:e + 1]).then_inc(s("h2_ev"), 1)

            hidden1(0)
            for n in range(NG * E):
                hidden2(n)
                if n + 1 < NG * E:
                    hidden1(n + 1)
            f(aneg[:, :], w("A_log"), ACT.Exp).then_inc(s("a_exp"), 1)
            ln_act(act, 3, P1, P2, P3)
            for b in range(B):
                for k in range(NG):
                    m = b * NG + k
                    act.wait_ge(s("z_ps"), m + 1)
                    f(batch_array(3, b)[:, cols(k)], PS[:, 2 + m % 2, 0:G], ACT.Silu).then_inc(s("z_ev"), 1)
                act.wait_ge(s("conv_ready"), b + 1)
                f(batch_array(0, b), conv[b % 2], ACT.Silu, bias=col("conv_b")).then_inc(s("u_ready"), 1)

            def mid_part(b):
                act.wait_ge(s("bc_left"), NG * (b + 1))
                f(bc(b)[64:128], resid[b % 2][64:128], ACT.Copy).then_inc(s("bc_mid"), 1)

            def logarithms(p):
                act.wait_ge(s("dt_abs"), 2 * NG * (p + 1))
                f(expo[p], expo[p], ACT.Exp, scale=-1.0).then_inc(s("dt_exp"), 1)
                act.wait_ge(s("dt_exp"), p + 1)
                f(logs[p], expo[p], ACT.Ln, bias=ONE).then_inc(s("dt_log"), 1)

            for m in range(B * NG + 1):
                if m < B * NG:
                    b, k = m // NG, m % NG
                    act.wait_ge(s("dlo_ps"), m + 1)
                    if m >= 2:
                        act.wait_ge(s("dt_ps"), m - 1)
                    f(dlo[m % 2], PS[:, 4 + m % 2, 0:G], ACT.Copy).then_inc(s("dlo_ev"), 1)
                    act.wait_ge(s("bc_ps"), m + 1)
                    f(bc(b)[:, :, cols(k)], PS[:, 2 * (m % 2):2 * (m % 2) + 2, 0:G], ACT.Copy).then_inc(s("bc_high"), 1)
                if m >= 1:
                    b, k = (m - 1) // NG, (m - 1) % NG
                    act.wait_ge(s("dt_ps"), m)
                    f(expo[b // 2][:, b % 2, cols(k)], PS[:, 6 + (m - 1) % 2, 0:G], ACT.Abs,
                      bias=col("b_dt")).then_inc(s("dt_abs"), 1)
                if m >= NG and m % NG == 1:
                    mid_part((m - 1) // NG - 1)
                if m == 2 * NG:
                    logarithms(0)
            mid_part(B - 1)
            logarithms(1)
            act.wait_ge(s("a_ready"), 1)
            act.wait_ge(s("dt_ready"), NPAIR)
            act.wait_ge(s("bc_ready"), B)

            def step_act(seg, n, first):
                early = first and seg == 0
                for c in range(NPS):
                    for h in range(2):
                        act.wait_ge(s("a_ready"), 1)
                        if not early:
                            act.wait_ge(s("scanned"), n * 2 * NPS + (2 * NPS * (NS * seg - 1) + 2 * c + h + 1))
                        f(decays[c][:, h, :], at(1, seg), ACT.Exp,
                          scale=aneg[:, bass.ds(n * (2 * NPS) + (2 * c + h), 1)]).then_inc(s("decay"), 1)
                    if not early:
                        act.wait_ge(s("hc_ready"), n * NPS + (NPS * (NS * seg - 1) + c + 1))
                    act.wait_ge(s("c_spread"), n * NPS + (NPS * NS * seg + c + 1))
                    f(cbuf[c], PS[:, 4:6, 0:G], ACT.Copy).then_inc(s("c_copied"), 1)

            for seg in range(NSEG):
                step_act(seg, 0, True)
                with act.Fori(1, NS) as n:
                    step_act(seg, n, False)
            for g in range(NGR + 2):
                if g < NGR:
                    p, k = groups[g]
                    act.wait_ge(s("mo_ps"), g + 1)
                    f(P1[:, p, cols(k)], PS[:, g % 2, 0:G], ACT.Copy).then_inc(s("mo_ev"), 1)
                if g >= 2:
                    p, k = groups[g - 2]
                    act.wait_ge(s("ff2_ps"), g - 1)
                    f(P4[:, p, cols(k)], PS[:, 4 + g % 2, 0:G], ACT.Sigmoid, bias=col("ff2b")).then_inc(s("ff2_ev"), 1)
            ln_act(act, 4, P1, P2, P3)
            for m in range(B * NG):
                b, k = m // NG, m % NG
                act.wait_ge(s("wrow_ps"), m + 1)
                f(wrow[b][:, cols(k)], PS[:, m % 2, 0:G], ACT.Identity, bias=col("br")).then_inc(s("wrow_ev"), 1)
            for b in range(B):
                for y in range(2 * NG):
                    m = b * 2 * NG + y
                    act.wait_ge(s("hid_ps"), m + 1)
                    f(hid[b][:, y // NG, cols(y % NG)], PS[:, 4 + m % 2, 0:G], ACT.Gelu_apprx_tanh,
                      bias=col("b1a" if y < NG else "b1b")).then_inc(s("hid_ready"), 1)
                act.wait_ge(s("rank_ps"), NT * (b + 1))
                for i, (a, z) in enumerate(BANKS):
                    ins = f(rank_row[:, b, a:z], PS[0:1, (3, 6, 7)[i], 0:z - a], ACT.Copy)
                ins.then_inc(s("rank_ev"), 1)

        @block.gpsimd
        def _(pool):
            step = stepper(pool, "pool_step")

            def forward_decays():
                pool.wait_ge(s("ik_ready"), 1)
                pool.wait_ge(s("iv_ready"), 1)
                pool.wait_ge(s("lag_prod"), NL // 2 + 1)
                fc, dc = (a.rearrange("p a (c r) -> p a c r", r=L) for a in (fs, dfw))
                step(nc.gpsimd.tensor_copy(dc[:, :, :, 0], fc[:, :, :, 0]))
                for r in range(1, L):
                    step(nc.gpsimd.tensor_tensor(dc[:, :, :, r], dc[:, :, :, r - 1], fc[:, :, :, r], ALU.mult))
                step(nc.gpsimd.tensor_copy(dend[:, :, :], dc[:, :, :, L - 1]))
                nc.gpsimd.memset(dend[:, :, 0:1], 0.0).then_inc(s("dend_ready"), 1)
                pool.wait_ge(s("dend_ready"), 1)

            pool.wait_ge(s("qkv_ev"), 3 * NGR)
            pool.wait_ge(s("tok_ps"), 4)
            for n in range(NL):
                lag, p = n // NPAIR, n % NPAIR
                if n >= 4:
                    pool.wait_ge(s("lag_ps"), n - 3)
                nc.gpsimd.tensor_tensor(prod[n % 4][:, 0:NC * (L - lag)].rearrange("p (c r) -> p c r", r=L - lag),
                                        chunks(q_[:, p, :])[:, :, lag:L], chunks(k_[:, p, :])[:, :, 0:L - lag],
                                        ALU.mult).then_inc(s("lag_prod"), 1)
                if n == NL // 2:
                    forward_decays()
            pool.wait_ge(s("states"), NPAIR)
            nc.gpsimd.tensor_copy(pick8.rearrange("p (e m) -> p e m", e=E),
                                  w("ident")[:, 0:E].unsqueeze(2).to_broadcast([128, E, 128])).then_inc(s("experts_zero"), 1)
            pool.wait_ge(s("gated"), NPAIR)
            pool.wait_ge(s("experts_zero"), 1)
            nc.gpsimd.memset(wT, 0.0).then_inc(s("experts_zero"), 1)
            pool.wait_ge(s("u_mm"), 4 * NT)
            pool.wait_ge(s("experts_zero"), 2)
            nc.gpsimd.tensor_copy(pick.rearrange("p (e m) -> p e m", e=DS),
                                  w("eyes").unsqueeze(2).to_broadcast([128, DS, 128])).then_inc(s("pick_ready"), 1)
            pool.wait_ge(s("pick_ready"), 1)
            def low_of(b):
                pool.wait_ge(s("bc_mid"), b + 1)
                step(nc.gpsimd.tensor_tensor(low_tmp, resid[b % 2][96:128], bc(b)[96:128], ALU.subtract))
                nc.gpsimd.tensor_copy(bc(b)[96:128], low_tmp).then_inc(s("bc_ready"), 1)
                pool.wait_ge(s("bc_ready"), b + 1)

            def series_product(p):
                pool.wait_ge(s("series"), p + 1)
                nc.gpsimd.tensor_tensor(pair_of(1, p), pair_of(1, p), pair_of(2, p), ALU.mult).then_inc(s("series_mid"), 1)
                pool.wait_ge(s("series_mid"), p + 1)

            def dt_times_u(p):
                pool.wait_ge(s("dt_sum"), p + 1)
                nc.gpsimd.tensor_tensor(pair_of(2, p), pair_of(1, p), pair_of(0, p), ALU.mult).then_inc(s("dt_ready"), 1)
                pool.wait_ge(s("dt_ready"), p + 1)

            low_of(0)
            low_of(1)
            series_product(0)
            low_of(2)
            dt_times_u(0)
            low_of(3)
            series_product(1)
            dt_times_u(1)
            pool.wait_ge(s("bc_ready"), B)

            pool.wait_ge(s("dt_ready"), NPAIR)

            def step_pool(seg, n, first):
                early = first and seg == 0
                for c in range(NPS):
                    pool.wait_ge(s("scanned"), n * 2 * NPS + (2 * NPS * NS * seg + 2 * c + 2))
                    if seg % NG < NG - 1:
                        nc.gpsimd.tensor_copy(carry[:, bass.ds(n * (2 * NPS) + 2 * c, 2)], hbuf[c][:, :, G - 1]).then_inc(s("carried"), 1)
                    pool.wait_ge(s("c_copied"), n * NPS + (NPS * NS * seg + c + 1))
                    if not early:
                        pool.wait_ge(s("y_added"), n * NPS + (NPS * (NS * seg - 1) + c + 1))
                    nc.gpsimd.tensor_tensor(hcbuf[c], hbuf[c], cbuf[c], ALU.mult).then_inc(s("hc_ready"), 1)

            for seg in range(NSEG):
                step_pool(seg, 0, True)
                with pool.Fori(1, NS) as n:
                    step_pool(seg, n, False)

        @block.vector
        def _(dve):
            step = stepper(dve, "dve_step")
            tt = nc.vector.tensor_tensor
            stt = nc.vector.scalar_tensor_tensor
            ts = nc.vector.tensor_scalar

            for c_, v in zip((EPS5, EPS8, ONE, HALF_LN, LN_EDGE),
                             (1e-5, 1e-8 * RMS_SCALE, 1.0, 0.5 * math.log(RMS_SCALE), -math.log1p(EDGE))):
                nc.vector.memset(c_, v)
            nc.vector.memset(one_bf[:, :], 1.0)
            nc.vector.memset(EPS3, 1e-3).then_inc(s("const_ready"), 1)
            step(nc.vector.memset(Wt[:, :], 0.0))
            nc.vector.memset(H[:, :, S:SP], 0.0).then_inc(s("txt_ev"), 1)
            dve.wait_ge(s("wtok_ps"), 1)
            for b2 in range(2):
                h = half(b2)
                for bank in range(-(-NOG // 4)):
                    o0 = bank * 4 * OG
                    no = min(4 * OG, D - o0)
                    nc.vector.tensor_copy(
                        Wt[h, :].rearrange("p (t m) -> p m t", t=PATCH)[:, 64 * b2 + o0:64 * b2 + o0 + no, :],
                        PS[h, 4 + bank, 0:no * PATCH].rearrange("p (o t) -> p o t", t=PATCH)).then_inc(s("wtok_sb"), 1)
            dve.wait_ge(s("w_in"), 16)
            step(tt(gbias[:, 0:1], col("bi"), col("ib"), ALU.add))
            ts(gbias[:, 0:1], gbias[:, 0:1], 0.1, None, ALU.mult).then_inc(s("gbias_ready"), 1)
            dve.wait_ge(s("txt_ps"), 1)
            nc.vector.tensor_copy(H[:, :, TOK:S], PS[:, 7, 0:NPAIR * TXT].rearrange("q (a t) -> q a t", a=NPAIR)
                                  ).then_inc(s("txt_ev"), 1)
            dve.wait_ge(s("tok_ev"), 4)
            dve.wait_ge(s("txt_ev"), 2)
            ln_dve(dve, 1, P1, P3)
            for r, (dst, bias, scale) in enumerate(((q_, "bq", 1.0), (k_, "bk", float(D) ** -0.5), (v_, "bv", 1.0))):
                for g, (p, k) in enumerate(groups):
                    m = r * NGR + g
                    dve.wait_ge(s("qkv_ps"), m + 1)
                    if m == 0:
                        dve.wait_ge(s("ln_out"), NGR)
                        dve.wait_ge(s("ln_var"), NGR)
                    ts(dst[:, p, cols(k)], PS[:, 6 + m % 2, 0:G], col(bias), scale, ALU.add, ALU.mult).then_inc(s("qkv_ev"), 1)
            dve.wait_ge(s("gates_ev"), 2 * NGR)
            step(ts(li, li, 10.0, None, ALU.mult))
            dve.wait_ge(s("softplus"), 1)
            step(stt(lf, lf, -1.0, r_, ALU.mult, ALU.subtract))
            for p in range(NPAIR):
                step(nc.vector.tensor_tensor_scan(m_[:, p, :], lf[:, p, :], li[:, p, :], 0.0, ALU.add, ALU.max))
            nc.vector.tensor_copy(fs[:, :, 0:1], lf[:, :, 0:1])
            step(tt(fs[:, :, 1:], lf[:, :, 1:], m_[:, :, 0:SP - 1], ALU.add))
            tt(fs, fs, m_, ALU.subtract).then_inc(s("exponents"), 1)
            tt(li, li, m_, ALU.subtract).then_inc(s("exponents"), 1)
            dve.wait_ge(s("factors"), 2)
            tt(ik, li, k_, ALU.mult).then_inc(s("ik_ready"), 1)
            dve.wait_ge(s("ik_ready"), 1)
            for p in range(NPAIR):
                step(nc.vector.tensor_tensor_scan(n_[:, p, :], fs[:, p, :], ik[:, p, :], 0.0, ALU.mult, ALU.add))
                tt(ik[:, p, :], n_[:, p, :], q_[:, p, :], ALU.mult).then_inc(s("nq_ready"), 1)
            tt(v_, v_, li, ALU.mult).then_inc(s("iv_ready"), 1)
            dve.wait_ge(s("den_ev"), NGR)
            ts(rden, rden, 1e-6, None, ALU.max).then_inc(s("den_max"), 1)
            dve.wait_ge(s("iv_ready"), 1)
            for n in range(NL):
                lag, p = n // NPAIR, n % NPAIR
                now, was = (chunks(WV[(lag + d) % 2][:, p, :]) for d in (0, 1))
                if lag:
                    if lag >= 2:
                        dve.wait_ge(s("lag_ve"), n - 3)
                    tt(now[:, :, lag:L], was[:, :, lag - 1:L - 1], chunks(fs[:, p, :])[:, :, lag:L],
                       ALU.mult).then_inc(s("lag_w"), 1)
                    dve.wait_ge(s("lag_w"), n - 1)
                dve.wait_ge(s("lag_ps"), n + 1)
                qk = PS[:, NG * p:NG * p + NG, 0:CG * (L - lag)].rearrange("q k (c r) -> q k c r", r=L - lag)
                wv = now[:, :, lag:L].rearrange("q (k c) r -> q k c r", k=NG)
                if lag == 0:
                    tt(chunks(hr[:, p, :]).rearrange("q (k c) r -> q k c r", k=NG), wv, qk, ALU.mult).then_inc(s("lag_read"), 1)
                    dve.wait_ge(s("lag_read"), n + 1)
                    continue
                tm = term[n % 2][:, 0:NC * (L - lag)]
                tt(tm.rearrange("q (k c r) -> q k c r", k=NG, r=L - lag), wv, qk, ALU.mult).then_inc(s("lag_read"), 1)
                dve.wait_ge(s("lag_read"), n + 1)
                if n >= 2 * NPAIR:
                    dve.wait_ge(s("lag_sum"), n - 2 * NPAIR + 1)
                tt(chunks(hr[:, p, :])[:, :, lag:L], chunks(hr[:, p, :])[:, :, lag:L],
                   tm.rearrange("q (c r) -> q c r", r=L - lag), ALU.add).then_inc(s("lag_sum"), 1)

            def state_scan(p):
                dve.wait_ge(s("decay_in"), 64)
                dve.wait_ge(s("u_ev"), 2 * NT * (p + 1))
                nc.vector.tensor_tensor_scan(UM[:, p, :], DBC[:, p, :], UM[:, p, :], 0.0, ALU.mult,
                                             ALU.add).then_inc(s("states"), 1)

            for u in range(NPAIR * NT):
                n = seq_of(u % NT)[1]
                for b2 in range(2):
                    y = 2 * u + b2
                    dve.wait_ge(s("rows_ev"), u + 1)
                    if y >= 2:
                        dve.wait_ge(s("u_mm"), y - 1)
                    shape = [n, n // L, D]
                    tt(spread[b2][0:n, 0:n // L * D].rearrange("q (c i) -> q c i", i=D),
                       rows_t[u % 2][0:n, 64 * b2:64 * b2 + 64].unsqueeze(1).to_broadcast(shape),
                       w("cmask")[0:n, 0:n // L].unsqueeze(2).to_broadcast(shape), ALU.mult).then_inc(s("spread_ready"), 1)
                if u == NT + 2:
                    state_scan(0)
            state_scan(1)
            dve.wait_ge(s("lag_sum"), NL - NPAIR)
            dve.wait_ge(s("rden_ready"), 1)
            for p in range(NPAIR):
                dve.wait_ge(s("inter_ps"), p + 1)
                tt(WV[0][:, p, L:G], dfw[:, p, L:G], PS[:, NG * p, L:G], ALU.mult)
                tt(WV[0][:, p, G:SP].rearrange("q (k t) -> q k t", k=NG - 1), dfw[:, p, G:SP].rearrange("q (k t) -> q k t", k=NG - 1),
                   PS[:, NG * p + 1:NG * p + NG, 0:G], ALU.mult).then_inc(s("inter_ev"), 1)
                dve.wait_ge(s("inter_ev"), p + 1)
                step(tt(hr[:, p, L:], hr[:, p, L:], WV[0][:, p, L:], ALU.add))
                step(tt(hr[:, p, :], hr[:, p, :], rden[:, p, :], ALU.mult))
                tt(hr[:, p, :], hr[:, p, :], so[:, p, :], ALU.mult).then_inc(s("gated"), 1)
            dve.wait_ge(s("gated"), NPAIR)
            for g, (p, k) in enumerate(groups):
                dve.wait_ge(s("rms_ready"), g + 1)
                step(tt(hr[:, p, cols(k)], hr[:, p, cols(k)], fs[:, p, cols(k)], ALU.mult))
                stt(H[:, p, cols(k)], hr[:, p, cols(k)], col("ns"), H[:, p, cols(k)], ALU.mult, ALU.add
                    ).then_inc(s("mlstm_out"), 1)
            dve.wait_ge(s("mlstm_out"), NGR)
            ln_dve(dve, 2, P1, P3)
            dve.wait_ge(s("bn_sd"), 1)
            step(nc.vector.reciprocal(bns[:, :, :], bns[:, :, :]))
            step(tt(bns[:, :, :], bns[:, :, :], bnw[:, 2:4, :], ALU.mult))
            step(tt(bnb[:, :, :], bnw[:, 0:2, :], bnw[:, 6:8, :], ALU.subtract))
            step(tt(bnb[:, :, :], bnb[:, :, :], bns[:, :, :], ALU.mult))
            tt(bnb[:, :, :], bnb[:, :, :], bnw[:, 4:6, :], ALU.add).then_inc(s("bn_ready"), 1)
            wide = [128, NT, E]
            dve.wait_ge(s("logit_ps"), 1)
            step(stt(lg, PS[:, 4, 0:NT * E].rearrange("q (j e) -> q j e", e=E), 1.0 / B,
                     w("brow").unsqueeze(1).to_broadcast(wide), ALU.mult, ALU.add))
            step(nc.vector.tensor_reduce(gmax, lg, AX_X, ALU.max))
            tt(lg, lg, gmax.unsqueeze(2).to_broadcast(wide), ALU.subtract).then_inc(s("logits"), 1)
            dve.wait_ge(s("gate_exp"), 1)
            step(nc.vector.tensor_reduce(gsum, lg, AX_X, ALU.add))
            step(nc.vector.reciprocal(gsum, gsum))
            tt(lg, lg, gsum.unsqueeze(2).to_broadcast(wide), ALU.mult).then_inc(s("gate_ready"), 1)
            dve.wait_ge(s("gateT_ps"), 1)
            dve.wait_ge(s("experts_zero"), 2)
            nc.vector.tensor_copy(wT[0:E, 0:1024].rearrange("q (a t) -> q a t", a=2), PS[0:E, 5:7, :]).then_inc(s("gateT"), 1)
            dve.wait_ge(s("gateT"), 1)
            nc.vector.tensor_copy(wT[0:E, SP - 128:SP], PS[0:E, 7, 0:128]).then_inc(s("gateT"), 1)
            dve.wait_ge(s("ln_out"), 2 * NGR)
            for n in range(NG * E + 1):
                if n < NG * E:
                    dve.wait_ge(s("h2_ev"), n + 1)
                    dve.wait_ge(s("spread_w"), n + 1)
                    if n >= 2:
                        dve.wait_ge(s("l3_ps"), n - 1)
                    tt(twin(hwb, n % 2), twin(h2b, n % 2), PS[:, 6 + n % 2:7 + n % 2, 0:G].to_broadcast([128, NPAIR, G]),
                       ALU.mult).then_inc(s("hw_ready"), 1)
                if n and n % E == 0:
                    k = n // E - 1
                    dve.wait_ge(s("l3_ps"), n)
                    tt(H[:, :, cols(k)], PS[:, 0:2, 0:G], H[:, :, cols(k)], ALU.add).then_inc(s("ffn_out"), 1)
            dve.wait_ge(s("ffn_out"), NG)
            ln_dve(dve, 3, P1, P3)
            dve.wait_ge(s("a_exp"), 1)
            ts(aneg[:, :], aneg[:, :], -1.0, None, ALU.mult).then_inc(s("a_ready"), 1)
            dve.wait_ge(s("ln_out"), 3 * NGR)
            ts(diagD[:, :], w("ident"), col("Dm"), None, ALU.mult).then_inc(s("diag_ready"), 1)
            for i in range(2):
                step(nc.vector.memset(xcp[i][:, 0:KC - 1], 0.0))
            for b in range(B):
                xp = xcp[b % 2]
                for k in range(NG):
                    m = b * NG + k
                    dve.wait_ge(s("xc_ps"), m + 1)
                    nc.vector.tensor_copy(xp[:, KC - 1 + k * G:KC - 1 + (k + 1) * G], PS[:, m % 2, 0:G]).then_inc(s("xc_ev"), 1)
                dve.wait_ge(s("xc_ev"), NG * (b + 1))
                if b >= 2:
                    dve.wait_ge(s("u_ready"), b - 1)
                cw = w("conv_w")
                step(ts(conv[b % 2], xp[:, 0:SP], cw[:, 0:1], None, ALU.mult))
                for j in range(1, KC):
                    ins = stt(conv[b % 2], xp[:, j:j + SP], cw[:, j:j + 1], conv[b % 2], ALU.mult, ALU.add)
                    if j < KC - 1:
                        step(ins)
                ins.then_inc(s("conv_ready"), 1)
            dve.wait_ge(s("z_ps"), B * NG)
            dve.wait_ge(s("u_ready"), B)

            def softplus(p, part):
                dt, low = pair_of(1, p), pair_of(2, p)
                if part == 0:
                    dve.wait_ge(s("dt_exp"), p + 1)
                    step(ts(low, expo[p], EDGE, None, ALU.min))
                    ts(dt, low, 1.0 / 3.0, -0.5, ALU.mult, ALU.add).then_inc(s("series"), 1)
                    dve.wait_ge(s("dt_log"), p + 1)
                    step(ts(logs[p], logs[p], -math.log1p(EDGE), 0.0, ALU.add, ALU.max))
                    tt(frelu[p], frelu[p], logs[p], ALU.add).then_inc(s("dt_large"), 1)
                else:
                    dve.wait_ge(s("series_mid"), p + 1)
                    step(stt(dt, dt, 1.0, low, ALU.add, ALU.mult))
                    dve.wait_ge(s("dt_large"), p + 1)
                    tt(dt, dt, frelu[p], ALU.add).then_inc(s("dt_sum"), 1)

            for m in range(B * NG + 1):
                if m < B * NG:
                    b, k = m // NG, m % NG
                    if b >= 2 and k == 0:
                        dve.wait_ge(s("bc_ready"), b - 1)
                    dve.wait_ge(s("bc_high"), m + 1)
                    tt(resid[b % 2][:, :, cols(k)], PS[:, 2 * (m % 2):2 * (m % 2) + 2, 0:G], bc(b)[:, :, cols(k)],
                       ALU.subtract).then_inc(s("bc_left"), 1)
                if m >= 1:
                    b, k = (m - 1) // NG, (m - 1) % NG
                    dve.wait_ge(s("dt_abs"), m)
                    ts(frelu[b // 2][:, b % 2, cols(k)], PS[:, 6 + (m - 1) % 2, 0:G], col("b_dt"), 0.0,
                       ALU.add, ALU.max).then_inc(s("dt_relu"), 1)
                if m == 2 * NG + 2:
                    softplus(0, 0)
                if m == 3 * NG + 2:
                    softplus(0, 1)
            softplus(1, 0)
            softplus(1, 1)
            dve.wait_ge(s("bc_ready"), B)
            dve.wait_ge(s("dt_ready"), NPAIR)

            def input_term(seg, n, c, early):
                if not early:
                    dve.wait_ge(s("scanned"), n * 2 * NPS + (2 * NPS * (NS * seg - 1) + 2 * c + 2))
                dve.wait_ge(s("b_spread"), n * NPS + (NPS * NS * seg + c + 1))
                bank = B_BANKS[c % 2]
                tt(bx[c], at(2, seg).unsqueeze(1).to_broadcast([128, 2, G]), PS[:, bank:bank + 2, 0:G],
                   ALU.mult).then_inc(s("b_used"), 1)

            def scan_pair(seg, n, c, early):
                b, k = seg // NG, seg % NG
                dve.wait_ge(s("b_used"), n * NPS + (NPS * NS * seg + c + 1))
                if not early:
                    dve.wait_ge(s("hc_ready"), n * NPS + (NPS * (NS * seg - 1) + c + 1))
                if k:
                    dve.wait_ge(s("carried"), n * NPS + (NPS * NS * ((NG - 1) * b + k - 1) + c + 1))
                for h in range(2):
                    dve.wait_ge(s("decay"), n * 2 * NPS + (2 * NPS * NS * seg + 2 * c + h + 1))
                    nc.vector.tensor_tensor_scan(hbuf[c][:, h, :], decays[c][:, h, :], bx[c][:, h, :],
                                                 carry[:, bass.ds(n * (2 * NPS) + (2 * c + h), 1)] if k else 0.0, ALU.mult,
                                                 ALU.add).then_inc(s("scanned"), 1)

            def step_dve(seg, n, before, number=None):
                early = number == 0 and seg == 0
                for c in range(NPS):
                    input_term(seg, n, c, early)
                    if c:
                        scan_pair(seg, n, c - 1, early)
                    elif before is not None:
                        scan_pair(*before, NPS - 1, number == 1 and seg == 0)

            def finish_y(seg):
                dve.wait_ge(s("y_added"), NPS * NS * (seg + 1))
                tt(at(3, seg), at(3, seg), PS[:, seg % 2, 0:G], ALU.mult).then_inc(s("ys_ready"), 1)

            for seg in range(NSEG):
                step_dve(seg, 0, (seg - 1, NS - 1) if seg else None, 0)
                step_dve(seg, 1, (seg, 0), 1)
                if seg:
                    finish_y(seg - 1)
                with dve.Fori(2, NS) as n:
                    step_dve(seg, n, (seg, n - 1))
            scan_pair(NSEG - 1, NS - 1, NPS - 1, False)
            finish_y(NSEG - 1)
            for g in range(NGR + 2):
                if 1 <= g <= NGR:
                    p, k = groups[g - 1]
                    dve.wait_ge(s("ff1_ps"), g)
                    ts(P2[:, p, cols(k)], PS[:, 2 + (g - 1) % 2, 0:G], col("ff1b"), None,
                       ALU.add).then_inc(s("ff1_ev"), 1)
                    dve.wait_ge(s("ff1_ev"), g)
                    stt(P3[:, p, cols(k)], P2[:, p, cols(k)], 0.01, P2[:, p, cols(k)],
                        ALU.mult, ALU.max).then_inc(s("ff1_out"), 1)
                if g >= 2:
                    p, k = groups[g - 2]
                    dve.wait_ge(s("ff2_ev"), g - 1)
                    tt(H[:, p, cols(k)], H[:, p, cols(k)], P4[:, p, cols(k)], ALU.add).then_inc(s("mamba_out"), 1)
            dve.wait_ge(s("mamba_out"), NGR)
            dve.wait_ge(s("mo_ev"), NGR)
            dve.wait_ge(s("ff1_ps"), NGR)
            dve.wait_ge(s("ff2_ps"), NGR)
            ln_dve(dve, 4, P1, P3)
            dve.wait_ge(s("ln_out"), 4 * NGR)
            tt(P4, H[:, :, :], P1, ALU.add).then_inc(s("residual"), 1)
            dve.wait_ge(s("wcol_ps"), 1)
            pcol = PS[:, 2, 0:B * NT].rearrange("q (b j) -> q b j", b=B)
            step(nc.vector.tensor_copy(wcol[:, :, 0:NT - 1], pcol[:, :, 0:NT - 1]))
            step(nc.vector.tensor_copy(wcol[0:LAST, :, NT - 1:NT], pcol[0:LAST, :, NT - 1:NT]))
            for b in range(B):
                for j in range(NT):
                    t0, n = j * 128, (128 if j < NT - 1 else LAST)
                    x_ = b * NT + j
                    own, row, bt = wcol[0:n, b, j:j + 1], wrow[b][0:n], beats[x_ % 2][0:n]
                    if x_ >= 2:
                        dve.wait_ge(s("rank_ps"), x_ - 1)
                    if j:
                        ts(bt[:, 0:t0], row[:, 0:t0], own, None, ALU.is_lt)
                    if t0 + n < S:
                        ts(bt[:, t0 + n:S], row[:, t0 + n:S], own, None, ALU.is_le)
                    stt(bt[:, t0:t0 + n], row[:, t0:t0 + n], own, w("after")[0:n, 0:n], ALU.is_le, ALU.mult)
                    stt(beats_own[x_ % 2][0:n, 0:n], row[:, t0:t0 + n], own, w("before")[0:n, 0:n], ALU.is_lt,
                        ALU.mult).then_inc(s("beats_ready"), 1)
            dve.wait_ge(s("rank_cols"), 1)
            for a, n in ((slice(0, NT - 1), 128), (slice(NT - 1, NT), LAST)):
                sv = sel[0:n, :].rearrange("q (b j) -> q b j", b=B)[:, :, a]
                rc = PS[0:n, 1, 0:B * NT].rearrange("q (b j) -> q b j", b=B)[:, :, a]
                step(ts(sv, rc, float(KEEP), None, ALU.is_lt))
                step(tt(sv, sv, wcol[0:n, :, a], ALU.mult))
            sel3 = sel[:, :].rearrange("q (b j) -> q b j", b=B)
            for x_, (n, members) in enumerate(ROWS):
                b, j = members[0]
                if n == 128:
                    weight, rows = sel3[:, b, j:j + 4], RES[:, b, j:j + 4, :]
                else:
                    weight, rows = sel3[0:n, :, NT - 1], RES[0:n, :, NT - 1, :]
                y = ytmp[0:n, x_ % 2]
                both = PS[0:n, 2 + x_ % 4, :].rearrange("q (h i d) -> q h i d", h=2, i=4)
                dve.wait_ge(s("rows_out_ps"), x_ + 1)
                step(tt(y, both[:, 0], w("b2row")[0:n, :].unsqueeze(1).to_broadcast([n, 4, D]), ALU.add))
                step(tt(y, y, weight.unsqueeze(2).to_broadcast([n, 4, D]), ALU.mult))
                tt(rows, y, both[:, 1], ALU.add).then_inc(s("rows_ready"), 1)


def pack(inputs):
    f = {k: np.asarray(v) for k, v in inputs.items()}
    z = np.float32

    def diag2(a):
        o = np.zeros((2 * a.shape[0], 2 * a.shape[1]), z)
        o[:a.shape[0], :a.shape[1]] = a
        o[a.shape[0]:, a.shape[1]:] = a
        return o

    def twice(a):
        return np.concatenate([a, a], 0)

    def rows(a):
        o = np.zeros((128, a.shape[1]), z)
        o[:a.shape[0]] = a
        return o

    def wide(a):
        return np.ascontiguousarray(rows(a.T).T)

    def column(v):
        return rows(v.reshape(-1, 1))

    wg, bg = f["L0_attn_Wg"], f["L0_attn_bg"]
    xp = f["L1_attn_W_xproj"]
    xB, xC = xp[DTR:DTR + DS].T, xp[DTR + DS:].T
    wout = np.zeros((128, 2, 2, 64), z)
    wr = np.zeros((2, 64, 2, 128), z)
    for i in range(2):
        wout[:, i, i, :] = f["L1_attn_W_out"].T
        wr[i, :, i, :] = f["L1_ffn_wr"]
    idx = np.arange(128)
    w2 = f["L1_ffn_w2"]
    parts = {
        "Wq": diag2(f["L0_attn_Wq"]), "Wk": diag2(f["L0_attn_Wk"]), "Wv": diag2(f["L0_attn_Wv"]),
        "Wi": diag2(wg[:, 0:D]), "Wf": diag2(wg[:, D:2 * D]), "Wo": diag2(wg[:, 2 * D:]),
        "Wr": twice(f["L0_ffn_Wr"]), "ebias": rows(np.concatenate([f["L0_ffn_bo"]] * 2, 1)),
        "Win": diag2(f["L1_attn_W_in"].T), "XB": np.concatenate([xB] * 4, 1), "XC": np.concatenate([xC] * 4, 1),
        "XD": wide(xp[0:DTR].T), "WdtT": rows(f["L1_attn_W_dt"].T), "WoutT": wout.reshape(128, 256),
        "FF1": wide(diag2(f["L1_attn_W_ff1"].T)), "FF2": rows(diag2(f["L1_attn_W_ff2"].T)),
        "wr": wr.reshape(128, 256), "w1": diag2(f["L1_ffn_w1"]), "w2": np.concatenate([w2[0:128], w2[128:]], 1),
        "ident": np.eye(128, dtype=z), "ones": diag2(np.ones((64, 64), z)),
        "cmask": (idx[:, None] // L == np.arange(128 // L)[None]).astype(z),
        "eyes": np.concatenate([np.eye(DS, dtype=z) * (i != 1) for i in range(4)], 0),
        "before": (idx[None] < idx[:, None]).astype(z), "after": (idx[None] > idx[:, None]).astype(z),
        "b2row": np.tile(f["L1_ffn_b2"], (128, 1)), "brow": np.tile(f["L0_ffn_br"], (128, 1)),
        "A_log": f["L1_attn_A_log"], "conv_w": f["L1_attn_conv_w"],
    }
    two = {"bq": f["L0_attn_bq"], "bk": f["L0_attn_bk"], "bv": f["L0_attn_bv"], "bi": bg[0:D], "bf": bg[D:2 * D],
           "bo": bg[2 * D:], "ib": f["L0_attn_input_bias"], "ns": f["L0_attn_norm_scale"],
           "ff1b": f["L1_attn_b_ff1"], "ff2b": f["L1_attn_b_ff2"], "br": np.tile(f["L1_ffn_br"], 64)}
    one = {"conv_b": f["L1_attn_conv_b"], "b_dt": f["L1_attn_b_dt"], "Dm": f["L1_attn_D"],
           "b1a": f["L1_ffn_b1"][0:128], "b1b": f["L1_ffn_b1"][128:]}
    parts["cols"] = np.concatenate([column(np.concatenate([two[n]] * 2) if n in two else one[n]) for n in COLS], 1)
    wts = np.concatenate([parts[n] for n, _ in WEIGHTS], 1)
    wexp = np.concatenate([diag2(f[f"L0_ffn_{n}"][e]) for n in ("W1", "W2", "Wo") for e in range(E)], 1)
    bn = np.concatenate([twice(f[f"L0_ffn_{n}"].T) for n in BN], 1)
    t, fr = np.arange(PATCH), np.arange(NF)
    ang = 2 * np.pi * np.outer(fr, t) / PATCH
    dft = (np.concatenate([np.cos(ang), -np.sin(ang)], 0) / np.sqrt(PATCH)).astype(z)
    wo = np.zeros((NOG * OG, 2 * NF, 2, C), z)
    wo[0:D] = f["L0_tok_W"].reshape(D, 2 * NF, 1, C)
    wd = np.zeros((128, NOG * 128 + OG * PATCH), z)
    wd[0:OG * 2 * NF, 0:NOG * 128] = wo.reshape(NOG, OG * 2 * NF, 128).transpose(1, 0, 2).reshape(OG * 2 * NF, NOG * 128)
    for i in range(OG):
        wd[i * 2 * NF:(i + 1) * 2 * NF, NOG * 128 + i * PATCH:NOG * 128 + (i + 1) * PATCH] = dft
    return {"x": f["x"], "txt": f["txt"], "wdft": wd, "wts": wts, "wexp": wexp, "bn": bn}


def kernel(**inputs):
    import concourse.bacc as bacc
    from concourse.bass_utils import run_bass_kernel_spmd

    nc = bacc.Bacc("TRN2", target_bir_lowering=False, num_devices=1)
    arrays = {k: np.ascontiguousarray(v) for k, v in pack(inputs).items()}
    args = {k: nc.dram_tensor(f"in_{k}", a.shape, mybir.dt.from_np(a.dtype), kind="ExternalInput").ap()
            for k, a in arrays.items()}
    out = nc.dram_tensor("out_h", (B, S, D), F32, kind="ExternalOutput").ap()
    build(nc, out=out, **args)
    r = run_bass_kernel_spmd(nc, [{f"in_{k}": a for k, a in arrays.items()}], core_ids=[0])
    return r.results[0]["out_h"]
```

```python
import math
from contextlib import ExitStack

import numpy as np

import concourse.bass as bass
from concourse import mybir

F32 = mybir.dt.float32
BF16 = mybir.dt.bfloat16
ALU = mybir.AluOpType
ACT = mybir.ActivationFunctionType
AX_X = mybir.AxisListType.X

B, C, T, V = 4, 64, 128, 64
D = 64
PATCH, STRIDE, PAD = 16, 8, 8
NP_ = (T + PAD - PATCH) // STRIDE + 1
NF = PATCH // 2 + 1
assert PATCH == 2 * STRIDE and T == NP_ * STRIDE
RH = STRIDE // 2
TXT = 77
TOK = V * NP_
S = TOK + TXT
NPAIR = B // 2
L = 16
NC = -(-S // L)
SP = NC * L
NG = 3
G = SP // NG
CG = NC // NG
HC = 64 // L
E = 8
DI, DS, DTR, KC = 128, 32, 16, 4
NPS = 4
NS = DS // (2 * NPS)
NSEG = B * NG
HM = 32
HF = 256
KEEP = max(1, int(0.5 * S)) - 1
NT = -(-S // 128)
LAST = S - 128 * (NT - 1)
RMS_SCALE = 2.0 ** -30
EDGE = 2.0 ** -7
assert G <= 512 and NC % NG == 0 and SP == NG * G


OG = 7
NOG = -(-D // OG)
WEIGHTS = [("Wq", 128), ("Wk", 128), ("Wv", 128), ("Wi", 128), ("Wf", 128), ("Wo", 128), ("Wr", E), ("ebias", 128),
           ("Win", 4 * DI), ("XB", 128), ("XC", 128), ("XD", 128), ("WdtT", DI), ("WoutT", 2 * 128), ("FF1", 128),
           ("FF2", 128), ("wr", 2 * 128), ("w1", 2 * HF), ("w2", 2 * D), ("ident", 128), ("ones", 128),
           ("cmask", HC), ("hmask", 2), ("eyes", DS), ("eyes8", E), ("after", 128), ("order", NT), ("b2row", D), ("brow", E), ("A_log", DS),
           ("conv_w", KC), ("cols", 16)]
EXPERTS = [("E1", E * 128), ("E2", E * 128), ("E3", E * 128)]
COLS = ["bq", "bk", "bv", "bi", "bf", "bo", "ib", "ns", "br", "conv_b", "b_dt", "Dm", "ff1b", "ff2b", "b1a", "b1b"]
BN = ["b1", "b2", "g1", "g2", "be1", "be2", "m1", "m2", "v1", "v2"]


def places(sizes):
    at, out = 0, {}
    for name, n in sizes:
        out[name] = (at, n)
        at += n
    return out, at


def build(nc, x, txt, wdft, wts, wexp, bn, out):
    lay, nw = places(WEIGHTS)
    elay, ne = places(EXPERTS)
    with ExitStack() as ctx:
        def sb(name, shape, dt=F32):
            return ctx.enter_context(nc.sbuf_tensor(name, shape, dt))

        sems = {}

        def s(name):
            if name not in sems:
                sems[name] = ctx.enter_context(nc.semaphore(name))
            return sems[name]

        PS = ctx.enter_context(nc.psum_tensor("PS", [128, 8, 512], F32))
        W_ = sb("weights", [128, nw])

        def w(name):
            a, n = lay[name]
            return W_[:, a:a + n]

        def col(name):
            a = lay["cols"][0] + COLS.index(name)
            return W_[:, a:a + 1]

        H = sb("hidden", [128, NPAIR, SP])
        pool_ = sb("pair_arrays", [128, 10, NPAIR, SP])
        P1, P2, P3, P4, P5, P6, P7, P8, P9, P10 = (pool_[:, i] for i in range(10))
        big = sb("big", [128, 2 * NPAIR * D * NC])
        Wt = sb("token_weights", [128, PATCH * 128])
        bnw = sb("bn_params", [128, len(BN), E])
        bns = sb("bn_scale", [128, 2, E])
        bnb = sb("bn_shift", [128, 2, E])
        cst = sb("constants", [128, 5])
        EPS5, EPS8, ONE, EPS3, HALF_LN = (cst[:, i:i + 1] for i in range(5))
        gbias = sb("gate_bias", [128, 2])
        txt_sb = sb("txt_rows", [TXT, B * D])
        dend = sb("chunk_decay", [128, NPAIR, NC])
        aneg = sb("A_negative", [128, DS])
        wcol = sb("router_cols", [128, B, NT])
        one_bf = sb("ones_bf16", [128, 1], BF16)
        sel = sb("selected", [128, B * NT])
        lost = sb("later_beaten", [128, B * NT])
        ytmp = sb("y_rows", [128, 2, 4, D])
        dram_decay = nc.dram_tensor("decay_rows", [NPAIR, 2, D * NC], F32, kind="Internal").ap()

        xs = big[:, 0:B * (NP_ + 1) * RH * V].rearrange("p (b m r v) -> p b m r v", b=B, m=NP_ + 1, r=RH)
        Wtok = Wt[:, 0:RH * 128].rearrange("p (r h o) -> p r h o", r=RH, h=2)
        shifted = P2
        wd = P1.rearrange("p a t -> p (a t)")[:, 0:NOG * 128]
        dft = P1.rearrange("p a t -> p (a t)")[:, NOG * 128:NOG * 128 + OG * PATCH]
        q_, k_, v_, li, r_, so, lf, m_, fs = P2, P3, P4, P5, P6, P7, P8, P9, P10
        ik, n_, rden = P1, P6, P9
        WV = [P4, P8]
        ve, dfw, hr = P1, P5, P6
        DBC = big[:, 0:NPAIR * D * NC].rearrange("p (a n) -> p a n", a=NPAIR)
        UM = big[:, NPAIR * D * NC:].rearrange("p (a n) -> p a n", a=NPAIR)
        UMc = big[:, NPAIR * D * NC:].rearrange("p (a i c) -> p a i c", a=NPAIR, i=D)
        lagmem = big[:, NPAIR * D * NC:]
        prod = [lagmem[:, i * SP:(i + 1) * SP] for i in range(4)]
        term = [lagmem[:, (4 + i) * SP:(5 + i) * SP] for i in range(2)]
        rows_t = [Wt[:, i * 256:(i + 1) * 256] for i in range(2)]
        spread = [Wt[:, 512 + i * 256:768 + i * 256] for i in range(4)]
        khalf = [Wt[:, 1536 + i * 256:1792 + i * 256].rearrange("p (b h j) -> p b h j", b=2, h=2) for i in range(2)]
        qdiag = [a.rearrange("p a t -> p (a t)").rearrange("p (c b r) -> p c b r", b=2, r=L) for a in (P8, P10)]
        INTER_BANKS = (4, 5, 0, 1, 2, 3)
        CB = 512 // (2 * L)
        IB = -(-(NC - 1) // CB)
        NL = NPAIR * L
        EW = big[:, 0:ne]

        def ew(name, e):
            a = elay[name][0] + e * 128
            return EW[:, a:a + 128]

        def twin(a, i):
            return a.rearrange("p a t -> p (a t)")[:, i * NPAIR * G:(i + 1) * NPAIR * G].rearrange("p (a t) -> p a t", a=NPAIR)

        h1b, h2b, hwb = P2, P3, P4
        gate = P6.rearrange("p a t -> p (a t)")
        lg = gate[:, 0:NT * E].rearrange("p (j e) -> p j e", e=E)
        gmax, gsum = gate[:, 128:128 + NT], gate[:, 160:160 + NT]
        parts = gate[:, 256:256 + NT * 32].rearrange("p (j r) -> p j r", r=32)
        part_bf = [gate[:, 1024 + i * 64:1024 + i * 64 + NT * E // 2].bitcast(BF16).rearrange("p (j e) -> p j e", e=E)
                   for i in range(2)]
        wTb = P5[:, 1, 0:SP // 2].bitcast(BF16)
        wT = P5[:, 0, :]
        pick8 = big[:, ne:ne + E * 64].bitcast(BF16)
        tstart = [min(128 * j, SP - 128) for j in range(NT)]
        def batch_array(i, b):
            return big[:, (4 * i + b) * SP:(4 * i + b + 1) * SP]

        assert 16 * SP <= 2 * NPAIR * D * NC
        SBC = pool_[:, 3:5].rearrange("p s a t -> p s (a t)").bitcast(BF16)

        def bc(b):
            return SBC[:, :, b * SP:(b + 1) * SP]

        pick = Wt[:, :].bitcast(BF16)
        diagD = sb("D_diagonal", [128, 128])
        dlo_sb = sb("dt_low_rank", [128, 2, G])
        xcp = [a.rearrange("p a t -> p (a t)") for a in (P6, P7)]
        conv = [P8[:, i] for i in range(2)]
        dlo = [dlo_sb[:, i, :] for i in range(2)]
        resid = [P6, P7]
        expo, frelu, logs = (P8, P9), (P1, P10), (P2, P3)

        def pair_of(i, p):
            return big[:, (4 * i + 2 * p) * SP:(4 * i + 2 * p + 2) * SP].rearrange("q (b t) -> q b t", b=2)

        ring_mem = [pool_[:, a:b].rearrange("p s a t -> p (s a t)") for a, b in ((5, 9), (0, 3))]

        def ring(mem, i):
            n = 2 * NPS * G
            return [ring_mem[mem][:, i * n:(i + 1) * n].rearrange("p (c h t) -> p c h t", c=NPS, h=2)[:, c] for c in range(NPS)]

        hbuf, hcbuf, cbuf, decays, bx = ring(0, 0), ring(0, 1), ring(0, 2), ring(1, 0), ring(1, 1)
        B_BANKS = (2, 6)
        carry = sb("scan_carry", [128, DS])

        def at(i, seg):
            return big[:, 4 * i * SP + seg * G:4 * i * SP + (seg + 1) * G]

        TOK_BANKS = ((0, 1, 2), (3, 6, 7), (4, 5, 6), (7, 0, 1))
        wrow = [(P5, P6)[b // 2][:, b % 2] for b in range(B)]
        hid = [P7, P8, P9, P10]
        RES = big[:, 0:B * NT * D].rearrange("p (b j d) -> p b j d", b=B, j=NT)
        beats = [big[:, 4096 + i * 640:4096 + i * 640 + SP // 2].bitcast(BF16) for i in range(3)]
        later = Wt[:, 0:SP]
        ROWS = [(128, [(b, 4 * i + j) for j in range(4)]) for b in range(B) for i in range(2)] + \
               [(LAST, [(b, NT - 1) for b in range(B)])]
        RANK_BANKS = (3, 6)
        RESID = [(p, j, nj, n) for p in range(NPAIR) for j, nj, n in ((0, 4, 128), (4, 4, 128), (NT - 1, 1, LAST))]


        groups = [(p, k) for p in range(NPAIR) for k in range(NG)]
        NGR = len(groups)

        def cols(k):
            return slice(k * G, (k + 1) * G)

        def half(b):
            return slice(64 * (b % 2), 64 * (b % 2) + 64)

        def block_pieces(b, h):
            b0, b1, b2 = TOK_BANKS[b]
            return [(b0, 1, 0, 7), (b1, 0, 7, 8), (b2, 0, 15, 1)] if h else [(b0, 0, 0, 8), (b1, 0, 8, 8)]

        def chunks(a):
            return a.rearrange("p (c r) -> p c r", r=L)

        def stepper(eng, name):
            n = [0]

            def step(ins):
                n[0] += 1
                ins.then_inc(s(name), 1)
                eng.wait_ge(s(name), n[0])
            return step

        def seq_of(e):
            return e * 128, min(128, SP - e * 128)

        def ln_mean(pe, n, g):
            p, k = groups[g]
            if g >= 2:
                pe.wait_ge(s("ln_centred"), NGR * (n - 1) + g - 1)
            nc.tensor.matmul(PS[:, g % 2, 0:G], w("ones"), H[:, p, cols(k)], start=True, stop=True).then_inc(s("ln_mean"), 1)

        def ln_var(pe, n, g, sq):
            p, k = groups[g]
            pe.wait_ge(s("ln_sq"), NGR * (n - 1) + g + 1)
            if g >= 2:
                pe.wait_ge(s("ln_ln"), NGR * (n - 1) + g - 1)
            nc.tensor.matmul(PS[:, 2 + g % 2, 0:G], w("ones"), sq[:, p, cols(k)], start=True, stop=True).then_inc(s("ln_var"), 1)

        def ln_square(act, n, g, xc, sq):
            p, k = groups[g]
            act.wait_ge(s("ln_centred"), NGR * (n - 1) + g + 1)
            nc.scalar.activation(sq[:, p, cols(k)], xc[:, p, cols(k)], ACT.Square).then_inc(s("ln_sq"), 1)

        def ln_log(act, n, g, rs):
            p, k = groups[g]
            act.wait_ge(s("ln_var"), NGR * (n - 1) + g + 1)
            nc.scalar.activation(rs[:, p, cols(k)], PS[:, 2 + g % 2, 0:G], ACT.Ln, bias=EPS5, scale=1.0 / D).then_inc(s("ln_ln"), 1)

        def ln_root(act, n, gs, rs):
            act.wait_ge(s("ln_ln"), NGR * (n - 1) + gs[-1] + 1)
            for g in gs:
                p, k = groups[g]
                nc.scalar.activation(rs[:, p, cols(k)], rs[:, p, cols(k)], ACT.Exp, scale=-0.5).then_inc(s("ln_rs"), 1)

        def ln_centre(dve, n, g, xc):
            p, k = groups[g]
            dve.wait_ge(s("ln_mean"), NGR * (n - 1) + g + 1)
            nc.vector.scalar_tensor_tensor(xc[:, p, cols(k)], PS[:, g % 2, 0:G], -1.0 / D, H[:, p, cols(k)],
                                           ALU.mult, ALU.add).then_inc(s("ln_centred"), 1)

        def ln_scale(dve, n, g, xc, rs):
            p, k = groups[g]
            dve.wait_ge(s("ln_rs"), NGR * (n - 1) + g + 1)
            nc.vector.tensor_tensor(xc[:, p, cols(k)], xc[:, p, cols(k)], rs[:, p, cols(k)], ALU.mult).then_inc(s("ln_out"), 1)

        def ln_pe(pe, n, ready, sq):
            for g in range(NGR + 1):
                if g < NGR:
                    ready(g)
                    ln_mean(pe, n, g)
                if g >= 1:
                    ln_var(pe, n, g - 1, sq)

        def ln_act(act, n, xc, sq, rs):
            for g in range(NGR + 1):
                if g < NGR:
                    ln_square(act, n, g, xc, sq)
                if g >= 1:
                    ln_log(act, n, g - 1, rs)
            ln_root(act, n, range(NGR), rs)

        def ln_dve(dve, n, xc, rs):
            for g in range(NGR):
                ln_centre(dve, n, g, xc)
            for g in range(NGR):
                ln_scale(dve, n, g, xc, rs)

        block = ctx.enter_context(nc.Block())

        @block.sync
        def _(sp):
            sp.dma_start(P1.rearrange("p a t -> p (a t)")[:, 0:NOG * 128 + OG * PATCH], wdft).then_inc(s("w_dft_in"), 16)
            xv = x.rearrange("b c (m h r) v -> b h c m (r v)", h=2, r=RH)
            for b in range(B):
                for hh in range(2):
                    sp.dma_start(xs[half(hh), b, 0:NP_].rearrange("c m r v -> c m (r v)"), xv[b, hh]).then_inc(s(f"x_in{b}"), 16)
                if b == 0:
                    sp.dma_start(W_[:, :], wts).then_inc(s("w_in"), 16)
                    sp.dma_start(txt_sb[:, :].rearrange("t (b d) -> t b d", b=B),
                                 txt.rearrange("b t d -> t b d")).then_inc(s("txt_in"), 16)
            sp.dma_start(bnw[:, :, :].rearrange("p a b -> p (a b)"), bn).then_inc(s("bn_in"), 16)
            sp.wait_ge(s("dend_ready"), 1)
            for p in range(NPAIR):
                sp.dma_start(dram_decay[p].rearrange("b (i c) -> (b i) c", i=D),
                             dend[:, p, :]).then_inc(s("dend_out"), 16)
            sp.wait_ge(s("dend_out"), 16 * NPAIR)
            sp.wait_ge(s("tok_ps"), 4)
            for p in range(NPAIR):
                for b2 in range(2):
                    sp.dma_start(DBC[64 * b2:64 * b2 + 64, p, :],
                                 dram_decay[p, b2:b2 + 1, :].to_broadcast([64, D * NC])).then_inc(s("decay_in"), 16)
            sp.wait_ge(s("states"), NPAIR)
            sp.dma_start(EW, wexp).then_inc(s("experts_in"), 16)
            for x_, (n, members) in enumerate(ROWS):
                b, j = members[0]
                sp.wait_ge(s("rows_ready"), x_ + 1)
                if n == 128:
                    sp.dma_start(out[b, 128 * j:128 * (j + 4), :].rearrange("(j p) d -> p j d", p=128),
                                 RES[:, b, j:j + 4, :]).then_inc(s("out_done"), 16)
                else:
                    sp.dma_start(out[:, 128 * j:S, :].rearrange("b p d -> p b d"), RES[0:n, :, j, :]).then_inc(s("out_done"), 16)
            sp.wait_ge(s("out_done"), 16 * len(ROWS))

        @block.tensor
        def _(pe):
            pe.wait_ge(s("w_dft_in"), 16)
            for g in range(NOG):
                last = nc.tensor.matmul(PS[:, 4 + g // 4, (g % 4) * OG * PATCH:(g % 4 + 1) * OG * PATCH],
                                        wd[:, g * 128:(g + 1) * 128], dft, start=True, stop=True)
            last.then_inc(s("wtok_ps"), 1)
            pe.wait_ge(s("wtok_sb"), 6)

            def tokens_pe(b):
                pe.wait_ge(s(f"x_in{b}"), 32)
                for i, (m0, nm) in enumerate(((0, 8), (8, 8), (NP_, 1))):
                    if nm == 1:
                        pe.wait_ge(s("x_pad"), b + 1)
                    for q in range(RH):
                        last = nc.tensor.matmul(PS[:, TOK_BANKS[b][i], 0:nm * V], Wtok[:, q].rearrange("p h o -> p (h o)"),
                                                xs[:, b, m0:m0 + nm, q, :], start=(q == 0), stop=(q == RH - 1))
                last.then_inc(s("tok_ps"), 1)

            def project(p):
                for r, (wa, wv) in enumerate((("Wi", "Wq"), ("Wf", "Wk"), ("Wo", "Wv"))):
                    for k in range(NG):
                        m = (p * 3 + r) * NG + k
                        pe.wait_ge(s("ln_out"), p * NG + k + 1)
                        if m >= 2:
                            pe.wait_ge(s("gates_ev"), m - 1)
                        nc.tensor.matmul(PS[:, 4 + m % 2, 0:G], w(wa), P1[:, p, cols(k)],
                                         start=True, stop=True).then_inc(s("gates_ps"), 1)
                        if m >= 2:
                            pe.wait_ge(s("qkv_ev"), m - 1)
                        nc.tensor.matmul(PS[:, 6 + m % 2, 0:G], w(wv), P1[:, p, cols(k)],
                                         start=True, stop=True).then_inc(s("qkv_ps"), 1)

            tokens_pe(0)
            pe.wait_ge(s("w_in"), 16)
            pe.wait_ge(s("txt_in"), 16)
            for i in range(NPAIR):
                last = nc.tensor.transpose(PS[:, 4, i * TXT:(i + 1) * TXT], txt_sb[:, i * 128:(i + 1) * 128],
                                           w("ident")[0:TXT, 0:TXT])
            last.then_inc(s("txt_ps"), 1)
            tokens_pe(1)
            pe.wait_ge(s("tokens"), 2)
            pe.wait_ge(s("txt_ev"), 2)
            for g in range(NG):
                ln_mean(pe, 1, g)
            tokens_pe(2)
            for g in range(NG):
                ln_var(pe, 1, g, P2)
            pe.wait_ge(s("ln_centred"), NG)
            tokens_pe(3)
            pe.wait_ge(s("tokens"), 4)
            for g in range(NG, NGR):
                ln_mean(pe, 1, g)
            project(0)
            for g in range(NG, NGR):
                ln_var(pe, 1, g, P2)
            project(1)
            pe.wait_ge(s("qkv_ev"), 3 * NGR)
            for g, (p, k) in enumerate(groups):
                pe.wait_ge(s("nq_ready"), p + 1)
                if g >= 2:
                    pe.wait_ge(s("den_ev"), g - 1)
                nc.tensor.matmul(PS[:, 6 + g % 2, 0:G], w("ones"), ik[:, p, cols(k)],
                                 start=True, stop=True).then_inc(s("den_ps"), 1)
            pe.wait_ge(s("gates_ev"), 3 * NGR)
            for n in range(NL):
                lag, p = n // NPAIR, n % NPAIR
                size = CG * (L - lag)
                pe.wait_ge(s("lag_prod"), n + 1)
                if n >= NPAIR:
                    pe.wait_ge(s("lag_read"), n - 1)
                for k in range(NG):
                    last = nc.tensor.matmul(PS[:, NG * p + k, 0:size], w("ones"), prod[n % 4][:, k * size:(k + 1) * size],
                                            start=True, stop=True)
                last.then_inc(s("lag_ps"), 1)
            pe.wait_ge(s("lag_ve"), NL)
            pe.wait_ge(s("den_ev"), NGR)
            pe.wait_ge(s("lag_read"), NL)

            def turn(u):
                p, (t0, n) = u // NT, seq_of(u % NT)
                if u >= 2:
                    pe.wait_ge(s("rows_ev"), u - 1)
                nc.tensor.transpose(PS[0:n, 6 + u % 2, 0:128], ve[:, p, t0:t0 + n], w("ident"))
                nc.tensor.transpose(PS[0:n, 6 + u % 2, 128:256], k_[:, p, t0:t0 + n], w("ident")).then_inc(s("rows_ps"), 1)

            def chunks_of(x_):
                i = x_ % IB
                return range(1 + i * CB, min(1 + (i + 1) * CB, NC))

            def inter(x_, c):
                p, i = x_ // IB, x_ % IB
                first = c == chunks_of(x_)[0]
                if first:
                    pe.wait_ge(s("states"), p + 1)
                    pe.wait_ge(s("qdiag_ready"), p + 1)
                    if x_ >= 6:
                        pe.wait_ge(s("inter_moved"), x_ - 5)
                a = (c - 1 - i * CB) * 2 * L
                last = nc.tensor.matmul(PS[0:64, INTER_BANKS[x_ % 6], a:a + 2 * L], UMc[:, p, :, c - 1],
                                        qdiag[p][:, c].rearrange("p b r -> p (b r)"), start=True, stop=True)
                if c == chunks_of(x_)[-1]:
                    last.then_inc(s("inter_ps"), 1)

            early_chunks = [c for x_ in range(2) for c in chunks_of(x_)]
            early_from, early_steps = NT + 4, NT - 4
            turn(0)
            for u in range(NPAIR * NT):
                n = seq_of(u % NT)[1]
                if u + 1 < NPAIR * NT:
                    turn(u + 1)
                for b2 in range(2):
                    y = 2 * u + b2
                    pe.wait_ge(s("spread_ready"), y + 1)
                    if y >= 4:
                        pe.wait_ge(s("u_ev"), y - 3)
                    pe.wait_ge(s("khalf_ready"), u + 1)
                    nc.tensor.matmul(PS[:, y % 4, 0:HC * D], khalf[u % 2][0:n, b2].rearrange("p h j -> p (h j)"),
                                     spread[y % 4][0:n, :], start=True, stop=True).then_inc(s("u_mm"), 1)
                if u >= early_from:
                    per = -(-len(early_chunks) // early_steps)
                    for c in early_chunks[(u - early_from) * per:(u - early_from + 1) * per]:
                        inter((c - 1) // CB, c)
            pe.wait_ge(s("u_ev"), 4 * NT)
            for x_ in range(NPAIR * IB):
                for c in chunks_of(x_):
                    if x_ >= 2 or c not in early_chunks:
                        inter(x_, c)
            pe.wait_ge(s("inter_moved"), NPAIR * IB)
            for g, (p, k) in enumerate(groups):
                pe.wait_ge(s("msq_in"), p + 1)
                if g >= 2:
                    pe.wait_ge(s("rms_ev"), g - 1)
                nc.tensor.matmul(PS[:, 6 + g % 2, 0:G], w("ones"), WV[1][:, p, cols(k)],
                                 start=True, stop=True).then_inc(s("msq_ps"), 1)

            def ready2(g):
                pe.wait_ge(s("mlstm_out"), g + 1)
            ln_pe(pe, 2, ready2, P2)

            pe.wait_ge(s("ln_out"), 2 * NGR)
            for j in range(NT):
                for p in range(NPAIR):
                    last = nc.tensor.matmul(PS[:, 4, j * E:(j + 1) * E], P1[:, p, tstart[j]:tstart[j] + 128], w("Wr"),
                                            start=(p == 0), stop=(p == NPAIR - 1))
            last.then_inc(s("logit_ps"), 1)
            pe.wait_ge(s("gate_ready"), 1)
            for j in range(NT):
                last = nc.tensor.transpose(PS[0:32, 5 + j // 4, (j % 4) * 128:(j % 4 + 1) * 128], parts[:, j, :], w("ident"))
            last.then_inc(s("gateT_ps"), 1)
            pe.wait_ge(s("experts_in"), 16)
            pe.wait_ge(s("gateT"), 2)
            pe.wait_ge(s("ln_ln"), 2 * NGR)
            NX = NG * E

            def layer1(n):
                if n >= 1:
                    pe.wait_ge(s("h1_ev"), n)
                for p in range(NPAIR):
                    last = nc.tensor.matmul(PS[:, 2 + p, 0:G], ew("E1", n % E), P1[:, p, cols(n // E)],
                                            start=True, stop=True)
                last.then_inc(s("l1_ps"), 1)

            def layer2(n):
                pe.wait_ge(s("h1_ev"), n + 1)
                if n >= 1:
                    pe.wait_ge(s("h2_ev"), n)
                for p in range(NPAIR):
                    last = nc.tensor.matmul(PS[:, 4 + p, 0:G], ew("E2", n % E), twin(h1b, n % 2)[:, p, :],
                                            start=True, stop=True)
                last.then_inc(s("l2_ps"), 1)

            def spread_weight(n):
                if n >= 2:
                    pe.wait_ge(s("hw_ready"), n - 1)
                nc.tensor.matmul(PS[:, 6 + n % 2, 0:G], pick8[:, (n % E) * 128:(n % E + 1) * 128], wTb[:, cols(n // E)],
                                 start=True, stop=True).then_inc(s("spread_w"), 1)

            def layer3(n):
                k, e = n // E, n % E
                pe.wait_ge(s("hw_ready"), n + 1)
                if e == 0 and k >= 1:
                    pe.wait_ge(s("ffn_out"), k)
                for p in range(NPAIR):
                    last = nc.tensor.matmul(PS[:, p, 0:G], ew("E3", e), twin(hwb, n % 2)[:, p, :],
                                            start=(e == 0), stop=False)
                    if e == E - 1:
                        pe.wait_ge(s("bias_weights"), 1)
                        last = nc.tensor.matmul(PS[:, p, 0:G], w("ebias"), wT[:, cols(k)], start=False, stop=True)
                last.then_inc(s("l3_ps"), 1)

            layer1(0)
            spread_weight(0)
            for n in range(NX):
                layer2(n)
                if n + 1 < NX:
                    layer1(n + 1)
                    spread_weight(n + 1)
                if n >= 1:
                    layer3(n - 1)
            layer3(NX - 1)

            def ready3(g):
                pe.wait_ge(s("ffn_out"), g % NG + 1)
                if g == 0:
                    pe.wait_ge(s("ffn_out"), NG)
            ln_pe(pe, 3, ready3, P2)

            pe.wait_ge(s("ln_out"), 3 * NGR)
            for m in range(B * NG):
                b, k = m // NG, m % NG
                xin = P1[:, b // 2, cols(k)]
                win = w("Win")[:, (b % 2) * 2 * DI:(b % 2 + 1) * 2 * DI]
                if m >= 2:
                    pe.wait_ge(s("xc_ev"), m - 1)
                nc.tensor.matmul(PS[:, m % 2, 0:G], win[:, 0:DI], xin, start=True, stop=True).then_inc(s("xc_ps"), 1)
                if m >= 2:
                    pe.wait_ge(s("z_ev"), m - 1)
                nc.tensor.matmul(PS[:, 2 + m % 2, 0:G], win[:, DI:2 * DI], xin,
                                 start=True, stop=True).then_inc(s("z_ps"), 1)
            pe.wait_ge(s("xc_ev"), B * NG)
            pe.wait_ge(s("z_ev"), B * NG)
            for m in range(B * NG + 1):
                if m < B * NG:
                    b, k = m // NG, m % NG
                    u = batch_array(0, b)[:, cols(k)]
                    pe.wait_ge(s("u_ready"), b + 1)
                    if m >= 2:
                        pe.wait_ge(s("bc_left"), m - 1)
                        pe.wait_ge(s("dlo_ev"), m - 1)
                    nc.tensor.matmul(PS[:, 4 + m % 2, 0:G], w("XD"), u, start=True, stop=True).then_inc(s("dlo_ps"), 1)
                    nc.tensor.matmul(PS[:, 2 * (m % 2), 0:G], w("XB"), u, start=True, stop=True)
                    nc.tensor.matmul(PS[:, 2 * (m % 2) + 1, 0:G], w("XC"), u, start=True, stop=True).then_inc(s("bc_ps"), 1)
                if m >= 1:
                    pe.wait_ge(s("dlo_ev"), m)
                    if m >= 3:
                        pe.wait_ge(s("dt_abs"), m - 2)
                        pe.wait_ge(s("dt_relu"), m - 2)
                    nc.tensor.matmul(PS[:, 6 + (m - 1) % 2, 0:G], w("WdtT"), dlo[(m - 1) % 2],
                                     start=True, stop=True).then_inc(s("dt_ps"), 1)
            pe.wait_ge(s("pick_ready"), 1)
            pe.wait_ge(s("bc_ready"), B)
            pe.wait_ge(s("dt_abs"), B * NG)
            pe.wait_ge(s("dt_relu"), B * NG)
            pe.wait_ge(s("diag_ready"), 1)

            def spread_pair(kind, seg, n, c):
                bank = 4 if kind else B_BANKS[c % 2]
                for h in range(2):
                    last = nc.tensor.matmul(PS[:, bank + h, 0:G], pick[:, bass.ds((n * (2 * NPS) + (2 * c + h)) * 128, 128)],
                                            SBC[:, kind, seg * G:(seg + 1) * G], start=True, stop=True)
                return last

            def add_y(seg, n, c, h, stop):
                if h == 0:
                    pe.wait_ge(s("hc_ready"), n * NPS + (NPS * NS * seg + c + 1))
                last = nc.tensor.matmul(PS[:, seg % 2, 0:G], w("ident"), hcbuf[c][:, h, :],
                                        start=False, stop=stop, skip_group_check=True)
                if h:
                    last.then_inc(s("y_added"), 1)

            def step_pe(seg, n, add):
                first = seg == 0 and add is None
                for c in range(NPS):
                    if not (first and c < 2):
                        pe.wait_ge(s("b_used"), n * NPS + (NPS * NS * seg + c - 1))
                    spread_pair(0, seg, n, c).then_inc(s("b_spread"), 1)
                    if add is not None:
                        add_y(*add, c, 0, False)
                    if not (first and c == 0):
                        pe.wait_ge(s("c_copied"), n * NPS + (NPS * NS * seg + c))
                    spread_pair(1, seg, n, c).then_inc(s("c_spread"), 1)
                    if add is not None:
                        add_y(*add, c, 1, add[0] < seg and c == NPS - 1)

            for seg in range(NSEG):
                step_pe(seg, 0, (seg - 1, NS - 1) if seg else None)
                if seg >= 2:
                    pe.wait_ge(s("ys_ready"), seg - 1)
                nc.tensor.matmul(PS[:, seg % 2, 0:G], diagD[:, :], at(0, seg), start=True, stop=False,
                                 skip_group_check=True)
                with pe.Fori(1, NS) as n:
                    step_pe(seg, n, (seg, n - 1))
            for c in range(NPS):
                for h in range(2):
                    add_y(NSEG - 1, NS - 1, c, h, c == NPS - 1 and h == 1)
            pe.wait_ge(s("ys_ready"), NSEG)
            for g in range(NGR + 2):
                if g < NGR:
                    p, k = groups[g]
                    if g >= 2:
                        pe.wait_ge(s("mo_ev"), g - 1)
                    for b2 in range(2):
                        last = nc.tensor.matmul(PS[:, g % 2, 0:G], w("WoutT")[:, b2 * 128:(b2 + 1) * 128],
                                                batch_array(3, 2 * p + b2)[:, cols(k)], start=(b2 == 0), stop=(b2 == 1))
                    last.then_inc(s("mo_ps"), 1)
                if 1 <= g <= NGR:
                    p, k = groups[g - 1]
                    pe.wait_ge(s("mo_ev"), g)
                    if g >= 3:
                        pe.wait_ge(s("ff1_ev"), g - 2)
                    nc.tensor.matmul(PS[:, 2 + (g - 1) % 2, 0:G], w("FF1"), P1[:, p, cols(k)],
                                     start=True, stop=True).then_inc(s("ff1_ps"), 1)
                if g >= 2:
                    p, k = groups[g - 2]
                    pe.wait_ge(s("ff1_out"), g - 1)
                    if g >= 4:
                        pe.wait_ge(s("ff2_ev"), g - 3)
                    nc.tensor.matmul(PS[:, 4 + g % 2, 0:G], w("FF2"), P3[:, p, cols(k)],
                                     start=True, stop=True).then_inc(s("ff2_ps"), 1)

            def ready4(g):
                pe.wait_ge(s("mamba_out"), g + 1)
            ln_pe(pe, 4, ready4, P2)

            pe.wait_ge(s("ln_out"), 4 * NGR)

            def weight_rows(b):
                for k in range(NG):
                    m = b * NG + k
                    if m >= 2:
                        pe.wait_ge(s("wrow_ev"), m - 1)
                    nc.tensor.matmul(PS[:, m % 2, 0:G], w("wr")[:, (b % 2) * 128:(b % 2 + 1) * 128], P1[:, b // 2, cols(k)],
                                     start=True, stop=True).then_inc(s("wrow_ps"), 1)

            def weight_columns(b):
                pe.wait_ge(s("wrow_ev"), NG * (b + 1))
                if b:
                    pe.wait_ge(s("wcol_ev"), b)
                for j in range(NT):
                    t0, n = j * 128, (128 if j < NT - 1 else LAST)
                    last = nc.tensor.transpose(PS[0:n, 2, b * NT + j:b * NT + j + 1], wrow[b][0:1, t0:t0 + n],
                                               w("ident")[0:1, 0:1])
                last.then_inc(s("wcol_ps"), 1)

            weight_rows(0)
            for b in range(1, B):
                weight_rows(b)
                weight_columns(b - 1)
            weight_columns(B - 1)

            def fill(b):
                steps = [[] for _ in range(NT)]
                for y in range(2 * NG):
                    steps[y].append((hidden, (b, y)))
                if b == 0:
                    for i in range(len(RESID)):
                        steps[i + 1].append((residual_rows, (i,)))
                else:
                    steps[1].append((rows_out, (2 * (b - 1),)))
                    steps[4].append((rows_out, (2 * (b - 1) + 1,)))
                return steps

            def hidden(b, y):
                m = b * 2 * NG + y
                if m >= 2:
                    pe.wait_ge(s("hid_ready"), m - 1)
                nc.tensor.matmul(PS[:, 4 + m % 2, 0:G], w("w1")[:, (b % 2) * HF + (y // NG) * 128:(b % 2) * HF + (y // NG + 1) * 128],
                                 P1[:, b // 2, cols(y % NG)], start=True, stop=True).then_inc(s("hid_ps"), 1)

            def residual_rows(i):
                pr, j0, nj, n = RESID[i]
                pe.wait_ge(s("residual"), 1)
                pe.wait_ge(s("wrow_ev"), B * NG)
                if i >= 2:
                    pe.wait_ge(s("resid_ev"), i - 1)
                for j in range(nj):
                    last = nc.tensor.transpose(PS[0:n, i % 2, j * 128:(j + 1) * 128],
                                               P4[:, pr, (j0 + j) * 128:(j0 + j) * 128 + n], w("ident"))
                last.then_inc(s("resid_ps"), 1)

            def rows_out(x_):
                n, members = ROWS[x_]
                pe.wait_ge(s("hid_ready"), (members[-1][0] + 1) * 2 * NG)
                if x_ < 2:
                    pe.wait_ge(s("wcol_ev"), B)
                    pe.wait_ge(s("resid_ev"), len(RESID))
                if x_ >= 2:
                    pe.wait_ge(s("rows_ready"), x_ - 1)
                for i, (b, j) in enumerate(members):
                    t0 = j * 128
                    for hh in range(2):
                        last = nc.tensor.matmul(PS[0:n, 2 * ((x_ + 1) % 2), i * D:(i + 1) * D], hid[b][:, hh, t0:t0 + n],
                                                w("w2")[:, hh * D:(hh + 1) * D], start=(hh == 0), stop=(hh == 1))
                last.then_inc(s("rows_out_ps"), 1)

            for b in range(B):
                if b >= 2:
                    pe.wait_ge(s("sel_ready"), b - 1)
                steps = fill(b)
                for j in range(NT):
                    x_ = b * NT + j
                    n = 128 if j < NT - 1 else LAST
                    pe.wait_ge(s("beats_ready"), x_ + 1)
                    for i in range(j, NT):
                        ni = 128 if i < NT - 1 else LAST
                        last = nc.tensor.matmul(PS[0:ni, RANK_BANKS[b % 2], i:i + 1], beats[x_ % 3][0:n, 128 * i:128 * i + ni],
                                                one_bf[0:n, :], start=(j == 0 and i == 0), stop=(j == i), skip_group_check=True)
                    last.then_inc(s("rank_ps"), 1)
                    for work, args in steps[j]:
                        work(*args)
            for x_ in range(2 * (B - 1), len(ROWS)):
                rows_out(x_)

        @block.scalar
        def _(act):
            step = stepper(act, "act_step")

            def f(o, i, fn, **kw):
                return nc.scalar.activation(o, i, fn, **kw)

            act.wait_ge(s("const_ready"), 1)

            def pad(b):
                act.wait_ge(s(f"x_in{b}"), 32)
                for hh in range(2):
                    ins = f(xs[half(hh), b, NP_], xs[64:128, b, NP_ - 1, RH - 1:RH, :].to_broadcast([64, RH, V]), ACT.Copy)
                ins.then_inc(s("x_pad"), 1)

            def shift_block(b):
                act.wait_ge(s("tok_ps"), b + 1)
                for bank, m, n, nm in block_pieces(b, 1 - b % 2):
                    ins = f(shifted[half(b), b // 2, n * V:(n + nm) * V], PS[half(1 - b), bank, m * V:(m + nm) * V], ACT.Copy)
                ins.then_inc(s("tok_shift"), 1)

            def gates(p):
                for k in range(NG):
                    m = p * 3 * NG + k
                    act.wait_ge(s("gates_ps"), m + 1)
                    f(li[:, p, cols(k)], PS[:, 4 + m % 2, 0:G], ACT.Tanh, bias=gbias[:, 0:1], scale=0.1).then_inc(s("gates_ev"), 1)
                for k in range(NG):
                    m = (p * 3 + 1) * NG + k
                    act.wait_ge(s("gates_ps"), m + 1)
                    f(fs[:, p, cols(k)], PS[:, 4 + m % 2, 0:G], ACT.Abs, bias=col("bf"))
                    f(r_[:, p, cols(k)], PS[:, 4 + m % 2, 0:G], ACT.Relu, bias=col("bf")).then_inc(s("gates_ev"), 1)
                if p == NPAIR - 1:
                    act.wait_ge(s("gates_ev"), (p * 3 + 2) * NG)
                    step(f(fs, fs, ACT.Exp, scale=-1.0))
                    f(lf, fs, ACT.Ln, bias=ONE).then_inc(s("softplus"), 1)
                for k in range(NG):
                    m = (p * 3 + 2) * NG + k
                    act.wait_ge(s("gates_ps"), m + 1)
                    f(so[:, p, cols(k)], PS[:, 4 + m % 2, 0:G], ACT.Sigmoid, bias=col("bo")).then_inc(s("gates_ev"), 1)

            pad(0)
            pad(1)
            shift_block(0)
            pad(2)
            shift_block(1)
            for g in range(NG):
                ln_square(act, 1, g, P1, P2)
            pad(3)
            shift_block(2)
            for g in range(NG):
                ln_log(act, 1, g, P3)
            ln_root(act, 1, range(NG), P3)
            shift_block(3)
            for g in range(NG, NGR):
                ln_square(act, 1, g, P1, P2)
            act.wait_ge(s("gbias_ready"), 1)
            gates(0)
            for g in range(NG, NGR):
                ln_log(act, 1, g, P3)
            ln_root(act, 1, range(NG, NGR), P3)
            gates(1)
            act.wait_ge(s("exponents"), 1)
            f(fs, fs, ACT.Exp).then_inc(s("factors"), 1)
            act.wait_ge(s("exponents"), 2)
            f(li, li, ACT.Exp).then_inc(s("factors"), 1)
            for g, (p, k) in enumerate(groups):
                act.wait_ge(s("den_ps"), g + 1)
                f(rden[:, p, cols(k)], PS[:, 6 + g % 2, 0:G], ACT.Abs).then_inc(s("den_ev"), 1)
            act.wait_ge(s("den_max"), 1)
            step(f(rden, rden, ACT.Ln))
            f(rden, rden, ACT.Exp, scale=-1.0).then_inc(s("rden_ready"), 1)
            act.wait_ge(s("iv_ready"), 1)
            for n in range(NL):
                lag, p = n // NPAIR, n % NPAIR
                if lag:
                    act.wait_ge(s("lag_w"), n - 1)
                f(chunks(ve[:, p, :])[:, :, L - 1 - lag], chunks(WV[lag % 2][:, p, :])[:, :, L - 1],
                  ACT.Copy).then_inc(s("lag_ve"), 1)
            act.wait_ge(s("lag_sum"), NL - NPAIR)
            act.wait_ge(s("lag_ps"), NL)
            for u in range(NPAIR * NT + 1):
                if u < NPAIR * NT:
                    n = seq_of(u % NT)[1]
                    act.wait_ge(s("rows_ps"), u + 1)
                    if u >= 2:
                        act.wait_ge(s("spread_ready"), 2 * (u - 1))
                        act.wait_ge(s("khalf_ready"), u - 1)
                    f(rows_t[u % 2][0:n, :], PS[0:n, 6 + u % 2, 0:256], ACT.Copy).then_inc(s("rows_ev"), 1)
                if u >= 1:
                    p, j = (u - 1) // NT, (u - 1) % NT
                    ncs = seq_of(j)[1] // L
                    for b2 in range(2):
                        y = 2 * (u - 1) + b2
                        act.wait_ge(s("u_mm"), y + 1)
                        for hh in range(2):
                            nch = min(HC, ncs - hh * HC)
                            c0 = 8 * j + hh * HC
                            ins = f(UMc[half(b2), p, :, c0:c0 + nch],
                                    PS[half(hh), y % 4, 0:nch * D].rearrange("q (c i) -> q i c", i=D), ACT.Copy)
                        ins.then_inc(s("u_ev"), 1)
            for p in range(NPAIR):
                for i in range(IB):
                    c0, c1 = 1 + i * CB, min(1 + (i + 1) * CB, NC)
                    act.wait_ge(s("inter_ps"), p * IB + i + 1)
                    for b2 in range(2):
                        ins = f(WV[0][half(b2), p, c0 * L:c1 * L].rearrange("q (c r) -> q c r", r=L),
                                PS[0:64, INTER_BANKS[(p * IB + i) % 6], 0:(c1 - c0) * 2 * L].rearrange("q (c b r) -> q c b r", b=2, r=L)[:, :, b2],
                                ACT.Copy)
                    ins.then_inc(s("inter_moved"), 1)
            for p in range(NPAIR):
                act.wait_ge(s("gated"), p + 1)
                f(WV[1][:, p, :], hr[:, p, :], ACT.Square).then_inc(s("msq_in"), 1)
            for g, (p, k) in enumerate(groups):
                act.wait_ge(s("msq_ps"), g + 1)
                f(fs[:, p, cols(k)], PS[:, 6 + g % 2, 0:G], ACT.Ln, bias=EPS8, scale=RMS_SCALE / D).then_inc(s("rms_ev"), 1)
            act.wait_ge(s("rms_ev"), NGR)
            for p, k in groups:
                f(fs[:, p, cols(k)], fs[:, p, cols(k)], ACT.Exp, bias=HALF_LN, scale=-0.5).then_inc(s("rms_ready"), 1)
            ln_act(act, 2, P1, P2, P3)
            act.wait_ge(s("bn_in"), 16)
            f(bns[:, :, :], bnw[:, 8:10, :], ACT.Sqrt, bias=EPS3).then_inc(s("bn_sd"), 1)
            act.wait_ge(s("logits"), 1)
            f(lg, lg, ACT.Exp).then_inc(s("gate_exp"), 1)
            act.wait_ge(s("bn_ready"), 1)
            act.wait_ge(s("ln_out"), 2 * NGR)

            def hidden1(n):
                act.wait_ge(s("l1_ps"), n + 1)
                if n >= 2:
                    act.wait_ge(s("l2_ps"), n - 1)
                e = n % E
                f(twin(h1b, n % 2), PS[:, 2:4, 0:G], ACT.Relu, bias=bnb[:, 0, e:e + 1],
                  scale=bns[:, 0, e:e + 1]).then_inc(s("h1_ev"), 1)

            def hidden2(n):
                act.wait_ge(s("l2_ps"), n + 1)
                if n >= 2:
                    act.wait_ge(s("hw_ready"), n - 1)
                e = n % E
                f(twin(h2b, n % 2), PS[:, 4:6, 0:G], ACT.Relu, bias=bnb[:, 1, e:e + 1],
                  scale=bns[:, 1, e:e + 1]).then_inc(s("h2_ev"), 1)

            hidden1(0)
            for n in range(NG * E):
                hidden2(n)
                if n + 1 < NG * E:
                    hidden1(n + 1)
            f(aneg[:, :], w("A_log"), ACT.Exp).then_inc(s("a_exp"), 1)
            ln_act(act, 3, P1, P2, P3)
            for b in range(B):
                for k in range(NG):
                    m = b * NG + k
                    act.wait_ge(s("z_ps"), m + 1)
                    f(batch_array(3, b)[:, cols(k)], PS[:, 2 + m % 2, 0:G], ACT.Silu).then_inc(s("z_ev"), 1)
                act.wait_ge(s("conv_ready"), b + 1)
                f(batch_array(0, b), conv[b % 2], ACT.Silu, bias=col("conv_b")).then_inc(s("u_ready"), 1)

            def mid_part(b):
                act.wait_ge(s("bc_left"), NG * (b + 1))
                f(bc(b)[64:128], resid[b % 2][64:128], ACT.Copy).then_inc(s("bc_mid"), 1)

            def logarithms(p):
                act.wait_ge(s("dt_abs"), 2 * NG * (p + 1))
                f(expo[p], expo[p], ACT.Exp, scale=-1.0).then_inc(s("dt_exp"), 1)
                act.wait_ge(s("dt_exp"), p + 1)
                f(logs[p], expo[p], ACT.Ln, bias=ONE).then_inc(s("dt_log"), 1)

            for m in range(B * NG + 1):
                if m < B * NG:
                    b, k = m // NG, m % NG
                    act.wait_ge(s("dlo_ps"), m + 1)
                    if m >= 2:
                        act.wait_ge(s("dt_ps"), m - 1)
                    f(dlo[m % 2], PS[:, 4 + m % 2, 0:G], ACT.Copy).then_inc(s("dlo_ev"), 1)
                    act.wait_ge(s("bc_ps"), m + 1)
                    f(bc(b)[:, :, cols(k)], PS[:, 2 * (m % 2):2 * (m % 2) + 2, 0:G], ACT.Copy).then_inc(s("bc_high"), 1)
                if m >= 1:
                    b, k = (m - 1) // NG, (m - 1) % NG
                    act.wait_ge(s("dt_ps"), m)
                    f(expo[b // 2][:, b % 2, cols(k)], PS[:, 6 + (m - 1) % 2, 0:G], ACT.Abs,
                      bias=col("b_dt")).then_inc(s("dt_abs"), 1)
                if m >= NG and m % NG == 1:
                    mid_part((m - 1) // NG - 1)
                if m == 2 * NG:
                    logarithms(0)
            mid_part(B - 1)
            logarithms(1)
            act.wait_ge(s("a_ready"), 1)
            act.wait_ge(s("dt_ready"), NPAIR)
            act.wait_ge(s("bc_ready"), B)

            def step_act(seg, n, first):
                early = first and seg == 0
                for c in range(NPS):
                    for h in range(2):
                        act.wait_ge(s("a_ready"), 1)
                        if not early:
                            act.wait_ge(s("scanned"), n * 2 * NPS + (2 * NPS * (NS * seg - 1) + 2 * c + h + 1))
                        f(decays[c][:, h, :], at(1, seg), ACT.Exp,
                          scale=aneg[:, bass.ds(n * (2 * NPS) + (2 * c + h), 1)]).then_inc(s("decay"), 1)
                    if not early:
                        act.wait_ge(s("hc_ready"), n * NPS + (NPS * (NS * seg - 1) + c + 1))
                    act.wait_ge(s("c_spread"), n * NPS + (NPS * NS * seg + c + 1))
                    f(cbuf[c], PS[:, 4:6, 0:G], ACT.Copy).then_inc(s("c_copied"), 1)

            for seg in range(NSEG):
                step_act(seg, 0, True)
                with act.Fori(1, NS) as n:
                    step_act(seg, n, False)
            for g in range(NGR + 2):
                if g < NGR:
                    p, k = groups[g]
                    act.wait_ge(s("mo_ps"), g + 1)
                    f(P1[:, p, cols(k)], PS[:, g % 2, 0:G], ACT.Copy).then_inc(s("mo_ev"), 1)
                if g >= 2:
                    p, k = groups[g - 2]
                    act.wait_ge(s("ff2_ps"), g - 1)
                    f(P4[:, p, cols(k)], PS[:, 4 + g % 2, 0:G], ACT.Sigmoid, bias=col("ff2b")).then_inc(s("ff2_ev"), 1)
            ln_act(act, 4, P1, P2, P3)

            def weight_columns(b):
                act.wait_ge(s("wcol_ps"), b + 1)
                f(wcol[:, b, 0:NT - 1], PS[:, 2, b * NT:b * NT + NT - 1], ACT.Copy)
                f(wcol[0:LAST, b, NT - 1:NT], PS[0:LAST, 2, b * NT + NT - 1:b * NT + NT], ACT.Copy).then_inc(s("wcol_ev"), 1)

            for b in range(B):
                for k in range(NG):
                    m = b * NG + k
                    act.wait_ge(s("wrow_ps"), m + 1)
                    f(wrow[b][:, cols(k)], PS[:, m % 2, 0:G], ACT.Identity, bias=col("br")).then_inc(s("wrow_ev"), 1)
                if b:
                    weight_columns(b - 1)
            weight_columns(B - 1)

            def residual_part(i):
                pr, j0, nj, n = RESID[i]
                act.wait_ge(s("resid_ps"), i + 1)
                f(RES[0:n, 2 * pr:2 * pr + 2, j0:j0 + nj, :].rearrange("q b j d -> q j b d"),
                  PS[0:n, i % 2, 0:nj * 128].rearrange("q (j b d) -> q j b d", j=nj, b=2), ACT.Copy).then_inc(s("resid_ev"), 1)

            for b in range(B):
                for y in range(2 * NG):
                    m = b * 2 * NG + y
                    act.wait_ge(s("hid_ps"), m + 1)
                    f(hid[b][:, y // NG, cols(y % NG)], PS[:, 4 + m % 2, 0:G], ACT.Gelu_apprx_tanh,
                      bias=col("b1a" if y < NG else "b1b")).then_inc(s("hid_ready"), 1)
                    if b == 0 and y:
                        residual_part(y - 1)
                if b == 0:
                    residual_part(len(RESID) - 1)

        @block.gpsimd
        def _(pool):
            step = stepper(pool, "pool_step")

            def forward_decays():
                pool.wait_ge(s("ik_ready"), 1)
                pool.wait_ge(s("iv_ready"), 1)
                pool.wait_ge(s("lag_prod"), NL // 2 + 1)
                fc, dc = (a.rearrange("p a (c r) -> p a c r", r=L) for a in (fs, dfw))
                step(nc.gpsimd.tensor_copy(dc[:, :, :, 0], fc[:, :, :, 0]))
                for r in range(1, L):
                    step(nc.gpsimd.tensor_tensor(dc[:, :, :, r], dc[:, :, :, r - 1], fc[:, :, :, r], ALU.mult))
                step(nc.gpsimd.tensor_copy(dend[:, :, :], dc[:, :, :, L - 1]))
                nc.gpsimd.memset(dend[:, :, 0:1], 0.0).then_inc(s("dend_ready"), 1)
                pool.wait_ge(s("dend_ready"), 1)

            pool.wait_ge(s("qkv_ev"), 3 * NGR)
            pool.wait_ge(s("tok_ps"), 4)
            for n in range(NL):
                lag, p = n // NPAIR, n % NPAIR
                if n >= 4:
                    pool.wait_ge(s("lag_ps"), n - 3)
                nc.gpsimd.tensor_tensor(prod[n % 4][:, 0:NC * (L - lag)].rearrange("p (c r) -> p c r", r=L - lag),
                                        chunks(q_[:, p, :])[:, :, lag:L], chunks(k_[:, p, :])[:, :, 0:L - lag],
                                        ALU.mult).then_inc(s("lag_prod"), 1)
                if n == 3:
                    pool.wait_ge(s("factors"), 2)
                    nc.gpsimd.tensor_tensor(v_, v_, li, ALU.mult).then_inc(s("iv_ready"), 1)
                if n == NL // 2:
                    forward_decays()
            pool.wait_ge(s("lag_read"), NL)
            pool.wait_ge(s("lag_ve"), NL)
            for p in range(NPAIR):
                step(nc.gpsimd.memset((P8, P10)[p], 0.0))
                for b2 in range(2):
                    ins = nc.gpsimd.tensor_copy(qdiag[p][half(b2), :, b2], chunks(q_[half(b2), p, :]))
                ins.then_inc(s("qdiag_ready"), 1)
                pool.wait_ge(s("qdiag_ready"), p + 1)
            pool.wait_ge(s("states"), NPAIR)
            nc.gpsimd.tensor_copy(pick8.rearrange("p (e m) -> p e m", e=E),
                                  w("eyes8").unsqueeze(2).to_broadcast([128, E, 128])).then_inc(s("experts_zero"), 1)
            pool.wait_ge(s("gated"), NPAIR)
            pool.wait_ge(s("experts_zero"), 1)
            nc.gpsimd.memset(P5, 0.0).then_inc(s("experts_zero"), 1)
            pool.wait_ge(s("u_mm"), 4 * NT)
            pool.wait_ge(s("experts_zero"), 2)
            nc.gpsimd.tensor_copy(pick.rearrange("p (e m) -> p e m", e=DS),
                                  w("eyes").unsqueeze(2).to_broadcast([128, DS, 128])).then_inc(s("pick_ready"), 1)
            pool.wait_ge(s("gateT"), 2)
            nc.gpsimd.tensor_copy(wT[0:32], wTb[0:32]).then_inc(s("bias_weights"), 1)
            for p in range(NPAIR):
                pool.wait_ge(s("series"), p + 1)
                nc.gpsimd.tensor_tensor(pair_of(1, p), pair_of(1, p), pair_of(2, p), ALU.mult).then_inc(s("series_mid"), 1)
                pool.wait_ge(s("dt_sum"), p + 1)
                bs = slice(0, 2 - p)
                nc.gpsimd.tensor_tensor(pair_of(2, p)[:, bs], pair_of(1, p)[:, bs], pair_of(0, p)[:, bs],
                                        ALU.mult).then_inc(s("dt_ready"), 1)

            def step_pool(seg, n, first):
                early = first and seg == 0
                for c in range(NPS):
                    pool.wait_ge(s("scanned"), n * 2 * NPS + (2 * NPS * NS * seg + 2 * c + 2))
                    if seg % NG < NG - 1:
                        nc.gpsimd.tensor_copy(carry[:, bass.ds(n * (2 * NPS) + 2 * c, 2)], hbuf[c][:, :, G - 1]).then_inc(s("carried"), 1)
                    pool.wait_ge(s("c_copied"), n * NPS + (NPS * NS * seg + c + 1))
                    if not early:
                        pool.wait_ge(s("y_added"), n * NPS + (NPS * (NS * seg - 1) + c + 1))
                    nc.gpsimd.tensor_tensor(hcbuf[c], hbuf[c], cbuf[c], ALU.mult).then_inc(s("hc_ready"), 1)

            for seg in range(NSEG):
                step_pool(seg, 0, True)
                with pool.Fori(1, NS) as n:
                    step_pool(seg, n, False)
            pool.wait_ge(s("b_spread"), NPS * NS * NSEG)
            pool.wait_ge(s("c_spread"), NPS * NS * NSEG)
            nc.gpsimd.memset(later[:, 128:SP], 1.0)
            nc.gpsimd.tensor_copy(later[:, 0:128], w("after")).then_inc(s("later_ready"), 1)
            pool.wait_ge(s("ln_out"), 4 * NGR)
            nc.gpsimd.tensor_tensor(P4, H[:, :, :], P1, ALU.add).then_inc(s("residual"), 1)

        @block.vector
        def _(dve):
            step = stepper(dve, "dve_step")
            tt = nc.vector.tensor_tensor
            stt = nc.vector.scalar_tensor_tensor
            ts = nc.vector.tensor_scalar

            for c_, v in zip((EPS5, EPS8, ONE, HALF_LN),
                             (1e-5, 1e-8 * RMS_SCALE, 1.0, 0.5 * math.log(RMS_SCALE))):
                nc.vector.memset(c_, v)
            nc.vector.memset(one_bf[:, :], 1.0)
            nc.vector.memset(EPS3, 1e-3).then_inc(s("const_ready"), 1)
            nc.vector.memset(H[:, :, S:SP], 0.0).then_inc(s("txt_ev"), 1)
            dve.wait_ge(s("wtok_ps"), 1)
            for hh in range(2):
                for bank in range(-(-NOG // 4)):
                    o0 = bank * 4 * OG
                    no = min(4 * OG, D - o0)
                    nc.vector.tensor_copy(Wtok[half(hh)].rearrange("p r h o -> p o h r")[:, o0:o0 + no],
                                          PS[half(hh), 4 + bank, 0:no * PATCH].rearrange("p (o h k r) -> p k o h r", h=2, k=2, r=RH)[:, hh]
                                          ).then_inc(s("wtok_sb"), 1)

            def tokens_dve(b):
                dve.wait_ge(s("tok_shift"), b + 1)
                Hp = H[half(b), b // 2, 0:TOK].rearrange("q (v n) -> q n v", n=NP_)
                for bank, m, n, nm in block_pieces(b, b % 2):
                    ins = tt(Hp[:, n:n + nm], PS[half(b), bank, m * V:(m + nm) * V].rearrange("q (n v) -> q n v", v=V),
                             shifted[half(b), b // 2, n * V:(n + nm) * V].rearrange("q (n v) -> q n v", v=V), ALU.add)
                ins.then_inc(s("tokens"), 1)

            tokens_dve(0)
            dve.wait_ge(s("w_in"), 16)
            step(tt(gbias[:, 0:1], col("bi"), col("ib"), ALU.add))
            ts(gbias[:, 0:1], gbias[:, 0:1], 0.1, None, ALU.mult).then_inc(s("gbias_ready"), 1)
            dve.wait_ge(s("txt_ps"), 1)
            nc.vector.tensor_copy(H[:, :, TOK:S], PS[:, 4, 0:NPAIR * TXT].rearrange("q (a t) -> q a t", a=NPAIR)
                                  ).then_inc(s("txt_ev"), 1)
            def qkv(p):
                dve.wait_ge(s("ln_out"), (p + 1) * NG)
                dve.wait_ge(s("ln_var"), (p + 1) * NG)
                for r, (dst, bias, scale) in enumerate(((q_, "bq", 1.0), (k_, "bk", float(D) ** -0.5), (v_, "bv", 1.0))):
                    for k in range(NG):
                        m = (p * 3 + r) * NG + k
                        dve.wait_ge(s("qkv_ps"), m + 1)
                        ts(dst[:, p, cols(k)], PS[:, 6 + m % 2, 0:G], col(bias), scale, ALU.add, ALU.mult).then_inc(s("qkv_ev"), 1)

            dve.wait_ge(s("txt_ev"), 2)
            tokens_dve(1)
            dve.wait_ge(s("tokens"), 2)
            for g in range(NG):
                ln_centre(dve, 1, g, P1)
            tokens_dve(2)
            for g in range(NG):
                ln_scale(dve, 1, g, P1, P3)
            tokens_dve(3)
            dve.wait_ge(s("tokens"), 4)
            for g in range(NG, NGR):
                ln_centre(dve, 1, g, P1)
            qkv(0)
            for g in range(NG, NGR):
                ln_scale(dve, 1, g, P1, P3)
            qkv(1)
            dve.wait_ge(s("gates_ev"), 3 * NGR - NG)
            step(ts(li, li, 10.0, None, ALU.mult))
            dve.wait_ge(s("softplus"), 1)
            step(stt(lf, lf, -1.0, r_, ALU.mult, ALU.subtract))
            for p in range(NPAIR):
                step(nc.vector.tensor_tensor_scan(m_[:, p, :], lf[:, p, :], li[:, p, :], 0.0, ALU.add, ALU.max))
            nc.vector.tensor_copy(fs[:, :, 0:1], lf[:, :, 0:1])
            step(tt(fs[:, :, 1:], lf[:, :, 1:], m_[:, :, 0:SP - 1], ALU.add))
            tt(fs, fs, m_, ALU.subtract).then_inc(s("exponents"), 1)
            tt(li, li, m_, ALU.subtract).then_inc(s("exponents"), 1)
            dve.wait_ge(s("factors"), 2)
            tt(ik, li, k_, ALU.mult).then_inc(s("ik_ready"), 1)
            dve.wait_ge(s("ik_ready"), 1)
            for p in range(NPAIR):
                step(nc.vector.tensor_tensor_scan(n_[:, p, :], fs[:, p, :], ik[:, p, :], 0.0, ALU.mult, ALU.add))
                tt(ik[:, p, :], n_[:, p, :], q_[:, p, :], ALU.mult).then_inc(s("nq_ready"), 1)
            dve.wait_ge(s("den_ev"), NGR)
            ts(rden, rden, 1e-6, None, ALU.max).then_inc(s("den_max"), 1)
            dve.wait_ge(s("iv_ready"), 1)
            for n in range(NL):
                lag, p = n // NPAIR, n % NPAIR
                now, was = (chunks(WV[(lag + d) % 2][:, p, :]) for d in (0, 1))
                if lag:
                    if lag >= 2:
                        dve.wait_ge(s("lag_ve"), n - 3)
                    tt(now[:, :, lag:L], was[:, :, lag - 1:L - 1], chunks(fs[:, p, :])[:, :, lag:L],
                       ALU.mult).then_inc(s("lag_w"), 1)
                    dve.wait_ge(s("lag_w"), n - 1)
                dve.wait_ge(s("lag_ps"), n + 1)
                qk = PS[:, NG * p:NG * p + NG, 0:CG * (L - lag)].rearrange("q k (c r) -> q k c r", r=L - lag)
                wv = now[:, :, lag:L].rearrange("q (k c) r -> q k c r", k=NG)
                if lag == 0:
                    tt(chunks(hr[:, p, :]).rearrange("q (k c) r -> q k c r", k=NG), wv, qk, ALU.mult).then_inc(s("lag_read"), 1)
                    dve.wait_ge(s("lag_read"), n + 1)
                    continue
                tm = term[n % 2][:, 0:NC * (L - lag)]
                tt(tm.rearrange("q (k c r) -> q k c r", k=NG, r=L - lag), wv, qk, ALU.mult).then_inc(s("lag_read"), 1)
                dve.wait_ge(s("lag_read"), n + 1)
                if n >= 2 * NPAIR:
                    dve.wait_ge(s("lag_sum"), n - 2 * NPAIR + 1)
                tt(chunks(hr[:, p, :])[:, :, lag:L], chunks(hr[:, p, :])[:, :, lag:L],
                   tm.rearrange("q (c r) -> q c r", r=L - lag), ALU.add).then_inc(s("lag_sum"), 1)

            def state_scan(p):
                dve.wait_ge(s("decay_in"), 64)
                dve.wait_ge(s("u_ev"), 2 * NT * (p + 1))
                nc.vector.tensor_tensor_scan(UM[:, p, :], DBC[:, p, :], UM[:, p, :], 0.0, ALU.mult,
                                             ALU.add).then_inc(s("states"), 1)

            for u in range(NPAIR * NT):
                n = seq_of(u % NT)[1]
                dve.wait_ge(s("rows_ev"), u + 1)
                if u >= 2:
                    dve.wait_ge(s("u_mm"), 2 * (u - 1))
                tt(khalf[u % 2][0:n], rows_t[u % 2][0:n, 128:256].rearrange("q (b j) -> q b j", b=2).unsqueeze(2).to_broadcast([n, 2, 2, 64]),
                   w("hmask")[0:n].unsqueeze(1).unsqueeze(3).to_broadcast([n, 2, 2, 64]), ALU.mult).then_inc(s("khalf_ready"), 1)
                for b2 in range(2):
                    y = 2 * u + b2
                    if y >= 4:
                        dve.wait_ge(s("u_mm"), y - 3)
                    shape = [n, HC, D]
                    tt(spread[y % 4][0:n].rearrange("q (c i) -> q c i", i=D),
                       rows_t[u % 2][0:n, 64 * b2:64 * b2 + 64].unsqueeze(1).to_broadcast(shape),
                       w("cmask")[0:n].unsqueeze(2).to_broadcast(shape), ALU.mult).then_inc(s("spread_ready"), 1)
                if u == NT + 2:
                    state_scan(0)
            state_scan(1)
            dve.wait_ge(s("lag_sum"), NL - NPAIR)
            dve.wait_ge(s("rden_ready"), 1)
            for p in range(NPAIR):
                dve.wait_ge(s("inter_moved"), (p + 1) * IB)
                step(tt(WV[0][:, p, L:], WV[0][:, p, L:], dfw[:, p, L:], ALU.mult))
                step(tt(hr[:, p, L:], hr[:, p, L:], WV[0][:, p, L:], ALU.add))
                step(tt(hr[:, p, :], hr[:, p, :], rden[:, p, :], ALU.mult))
                tt(hr[:, p, :], hr[:, p, :], so[:, p, :], ALU.mult).then_inc(s("gated"), 1)
            dve.wait_ge(s("gated"), NPAIR)
            for g, (p, k) in enumerate(groups):
                dve.wait_ge(s("rms_ready"), g + 1)
                step(tt(hr[:, p, cols(k)], hr[:, p, cols(k)], fs[:, p, cols(k)], ALU.mult))
                stt(H[:, p, cols(k)], hr[:, p, cols(k)], col("ns"), H[:, p, cols(k)], ALU.mult, ALU.add
                    ).then_inc(s("mlstm_out"), 1)
            dve.wait_ge(s("mlstm_out"), NGR)
            ln_dve(dve, 2, P1, P3)
            dve.wait_ge(s("bn_sd"), 1)
            step(nc.vector.reciprocal(bns[:, :, :], bns[:, :, :]))
            step(tt(bns[:, :, :], bns[:, :, :], bnw[:, 2:4, :], ALU.mult))
            step(tt(bnb[:, :, :], bnw[:, 0:2, :], bnw[:, 6:8, :], ALU.subtract))
            step(tt(bnb[:, :, :], bnb[:, :, :], bns[:, :, :], ALU.mult))
            tt(bnb[:, :, :], bnb[:, :, :], bnw[:, 4:6, :], ALU.add).then_inc(s("bn_ready"), 1)
            wide = [128, NT, E]
            step(nc.vector.memset(gate[:, 256:256 + NT * 32], 0.0))
            dve.wait_ge(s("logit_ps"), 1)
            step(stt(lg, PS[:, 4, 0:NT * E].rearrange("q (j e) -> q j e", e=E), 1.0 / B,
                     w("brow").unsqueeze(1).to_broadcast(wide), ALU.mult, ALU.add))
            step(nc.vector.tensor_reduce(gmax, lg, AX_X, ALU.max))
            tt(lg, lg, gmax.unsqueeze(2).to_broadcast(wide), ALU.subtract).then_inc(s("logits"), 1)
            dve.wait_ge(s("gate_exp"), 1)
            step(nc.vector.tensor_reduce(gsum, lg, AX_X, ALU.add))
            step(nc.vector.reciprocal(gsum, gsum))
            step(tt(lg, lg, gsum.unsqueeze(2).to_broadcast(wide), ALU.mult))
            step(nc.vector.tensor_copy(part_bf[0], lg))
            step(tt(lg, lg, part_bf[0], ALU.subtract))
            nc.vector.tensor_copy(parts[:, :, 0:E], part_bf[0])
            step(nc.vector.tensor_copy(part_bf[1], lg))
            tt(parts[:, :, 2 * E:3 * E], lg, part_bf[1], ALU.subtract)
            nc.vector.tensor_copy(parts[:, :, E:2 * E], part_bf[1]).then_inc(s("gate_ready"), 1)
            dve.wait_ge(s("gateT_ps"), 1)
            dve.wait_ge(s("experts_zero"), 2)
            nc.vector.tensor_copy(wTb[0:32, 0:1024].rearrange("q (a t) -> q a t", a=2), PS[0:32, 5:7, :]).then_inc(s("gateT"), 1)
            dve.wait_ge(s("gateT"), 1)
            nc.vector.tensor_copy(wTb[0:32, SP - 128:SP], PS[0:32, 7, 0:128]).then_inc(s("gateT"), 1)
            dve.wait_ge(s("ln_out"), 2 * NGR)
            for n in range(NG * E + 1):
                if n < NG * E:
                    dve.wait_ge(s("h2_ev"), n + 1)
                    dve.wait_ge(s("spread_w"), n + 1)
                    if n >= 2:
                        dve.wait_ge(s("l3_ps"), n - 1)
                    tt(twin(hwb, n % 2), twin(h2b, n % 2), PS[:, 6 + n % 2:7 + n % 2, 0:G].to_broadcast([128, NPAIR, G]),
                       ALU.mult).then_inc(s("hw_ready"), 1)
                if n and n % E == 0:
                    k = n // E - 1
                    dve.wait_ge(s("l3_ps"), n)
                    tt(H[:, :, cols(k)], PS[:, 0:2, 0:G], H[:, :, cols(k)], ALU.add).then_inc(s("ffn_out"), 1)
            dve.wait_ge(s("ffn_out"), NG)
            ln_dve(dve, 3, P1, P3)
            dve.wait_ge(s("a_exp"), 1)
            ts(aneg[:, :], aneg[:, :], -1.0, None, ALU.mult).then_inc(s("a_ready"), 1)
            dve.wait_ge(s("ln_out"), 3 * NGR)
            ts(diagD[:, :], w("ident"), col("Dm"), None, ALU.mult).then_inc(s("diag_ready"), 1)
            for i in range(2):
                step(nc.vector.memset(xcp[i][:, 0:KC - 1], 0.0))
            for b in range(B):
                xp = xcp[b % 2]
                for k in range(NG):
                    m = b * NG + k
                    dve.wait_ge(s("xc_ps"), m + 1)
                    nc.vector.tensor_copy(xp[:, KC - 1 + k * G:KC - 1 + (k + 1) * G], PS[:, m % 2, 0:G]).then_inc(s("xc_ev"), 1)
                dve.wait_ge(s("xc_ev"), NG * (b + 1))
                if b >= 2:
                    dve.wait_ge(s("u_ready"), b - 1)
                cw = w("conv_w")
                step(ts(conv[b % 2], xp[:, 0:SP], cw[:, 0:1], None, ALU.mult))
                for j in range(1, KC):
                    ins = stt(conv[b % 2], xp[:, j:j + SP], cw[:, j:j + 1], conv[b % 2], ALU.mult, ALU.add)
                    if j < KC - 1:
                        step(ins)
                ins.then_inc(s("conv_ready"), 1)
            dve.wait_ge(s("z_ps"), B * NG)
            dve.wait_ge(s("u_ready"), B)

            def softplus(p, part):
                dt, low = pair_of(1, p), pair_of(2, p)
                if part == 0:
                    dve.wait_ge(s("dt_exp"), p + 1)
                    step(ts(low, expo[p], EDGE, None, ALU.min))
                    ts(dt, low, 1.0 / 3.0, -0.5, ALU.mult, ALU.add).then_inc(s("series"), 1)
                    if p:
                        low_part(B - 1)
                    dve.wait_ge(s("dt_log"), p + 1)
                    step(ts(logs[p], logs[p], -math.log1p(EDGE), 0.0, ALU.add, ALU.max))
                    tt(frelu[p], frelu[p], logs[p], ALU.add).then_inc(s("dt_large"), 1)
                else:
                    dve.wait_ge(s("series_mid"), p + 1)
                    step(stt(dt, dt, 1.0, low, ALU.add, ALU.mult))
                    dve.wait_ge(s("dt_large"), p + 1)
                    tt(dt, dt, frelu[p], ALU.add).then_inc(s("dt_sum"), 1)
                    if p:
                        dve.wait_ge(s("dt_sum"), p + 1)
                        tt(low[:, 1], dt[:, 1], pair_of(0, p)[:, 1], ALU.mult).then_inc(s("dt_u_last"), 1)

            def low_part(b):
                dve.wait_ge(s("bc_mid"), b + 1)
                tt(bc(b)[96:128], resid[b % 2][96:128], bc(b)[96:128], ALU.subtract).then_inc(s("bc_ready"), 1)

            for m in range(B * NG + 1):
                if m < B * NG:
                    b, k = m // NG, m % NG
                    if b >= 2 and k == 0:
                        dve.wait_ge(s("bc_ready"), b - 1)
                    dve.wait_ge(s("bc_high"), m + 1)
                    tt(resid[b % 2][:, :, cols(k)], PS[:, 2 * (m % 2):2 * (m % 2) + 2, 0:G], bc(b)[:, :, cols(k)],
                       ALU.subtract).then_inc(s("bc_left"), 1)
                if m >= 1:
                    b, k = (m - 1) // NG, (m - 1) % NG
                    dve.wait_ge(s("dt_abs"), m)
                    ts(frelu[b // 2][:, b % 2, cols(k)], PS[:, 6 + (m - 1) % 2, 0:G], col("b_dt"), 0.0,
                       ALU.add, ALU.max).then_inc(s("dt_relu"), 1)
                if m >= NG + 2 and m % NG == 2:
                    low_part(m // NG - 1)
                if m == 2 * NG + 2:
                    softplus(0, 0)
                if m == 3 * NG + 2:
                    softplus(0, 1)
            softplus(1, 0)
            softplus(1, 1)
            dve.wait_ge(s("bc_ready"), B)
            dve.wait_ge(s("dt_ready"), NPAIR)
            dve.wait_ge(s("dt_u_last"), 1)

            def input_term(seg, n, c, early):
                if not early:
                    dve.wait_ge(s("scanned"), n * 2 * NPS + (2 * NPS * (NS * seg - 1) + 2 * c + 2))
                dve.wait_ge(s("b_spread"), n * NPS + (NPS * NS * seg + c + 1))
                bank = B_BANKS[c % 2]
                tt(bx[c], at(2, seg).unsqueeze(1).to_broadcast([128, 2, G]), PS[:, bank:bank + 2, 0:G],
                   ALU.mult).then_inc(s("b_used"), 1)

            def scan_pair(seg, n, c, early):
                b, k = seg // NG, seg % NG
                dve.wait_ge(s("b_used"), n * NPS + (NPS * NS * seg + c + 1))
                if not early:
                    dve.wait_ge(s("hc_ready"), n * NPS + (NPS * (NS * seg - 1) + c + 1))
                if k:
                    dve.wait_ge(s("carried"), n * NPS + (NPS * NS * ((NG - 1) * b + k - 1) + c + 1))
                for h in range(2):
                    dve.wait_ge(s("decay"), n * 2 * NPS + (2 * NPS * NS * seg + 2 * c + h + 1))
                    nc.vector.tensor_tensor_scan(hbuf[c][:, h, :], decays[c][:, h, :], bx[c][:, h, :],
                                                 carry[:, bass.ds(n * (2 * NPS) + (2 * c + h), 1)] if k else 0.0, ALU.mult,
                                                 ALU.add).then_inc(s("scanned"), 1)

            def step_dve(seg, n, before, number=None):
                early = number == 0 and seg == 0
                for c in range(NPS):
                    input_term(seg, n, c, early)
                    if c:
                        scan_pair(seg, n, c - 1, early)
                    elif before is not None:
                        scan_pair(*before, NPS - 1, number == 1 and seg == 0)

            def finish_y(seg):
                dve.wait_ge(s("y_added"), NPS * NS * (seg + 1))
                tt(at(3, seg), at(3, seg), PS[:, seg % 2, 0:G], ALU.mult).then_inc(s("ys_ready"), 1)

            for seg in range(NSEG):
                step_dve(seg, 0, (seg - 1, NS - 1) if seg else None, 0)
                step_dve(seg, 1, (seg, 0), 1)
                if seg:
                    finish_y(seg - 1)
                with dve.Fori(2, NS) as n:
                    step_dve(seg, n, (seg, n - 1))
            scan_pair(NSEG - 1, NS - 1, NPS - 1, False)
            finish_y(NSEG - 1)
            for g in range(NGR + 2):
                if 1 <= g <= NGR:
                    p, k = groups[g - 1]
                    dve.wait_ge(s("ff1_ps"), g)
                    ts(P2[:, p, cols(k)], PS[:, 2 + (g - 1) % 2, 0:G], col("ff1b"), None,
                       ALU.add).then_inc(s("ff1_ev"), 1)
                    dve.wait_ge(s("ff1_ev"), g)
                    stt(P3[:, p, cols(k)], P2[:, p, cols(k)], 0.01, P2[:, p, cols(k)],
                        ALU.mult, ALU.max).then_inc(s("ff1_out"), 1)
                if g >= 2:
                    p, k = groups[g - 2]
                    dve.wait_ge(s("ff2_ev"), g - 1)
                    tt(H[:, p, cols(k)], H[:, p, cols(k)], P4[:, p, cols(k)], ALU.add).then_inc(s("mamba_out"), 1)
            dve.wait_ge(s("mamba_out"), NGR)
            dve.wait_ge(s("mo_ev"), NGR)
            dve.wait_ge(s("ff1_ps"), NGR)
            dve.wait_ge(s("ff2_ps"), NGR)
            ln_dve(dve, 4, P1, P3)
            dve.wait_ge(s("ln_out"), 4 * NGR)
            dve.wait_ge(s("later_ready"), 1)
            sel3, lost3 = (a[:, :].rearrange("q (b j) -> q b j", b=B) for a in (sel, lost))

            def select(b):
                dve.wait_ge(s("rank_ps"), NT * (b + 1))
                dve.wait_ge(s("beats_ready"), NT * (b + 1))
                for a, n in ((slice(0, NT - 1), 128), (slice(NT - 1, NT), LAST)):
                    sv = sel3[0:n, b, a]
                    step(tt(sv, PS[0:n, RANK_BANKS[b % 2], a], lost3[0:n, b, a], ALU.subtract))
                    step(tt(sv, sv, w("order")[0:n, a], ALU.is_lt))
                    last = tt(sv, sv, wcol[0:n, b, a], ALU.mult)
                    if n == 128:
                        step(last)
                last.then_inc(s("sel_ready"), 1)

            def rows_of(x_):
                n, members = ROWS[x_]
                b, j = members[0]
                if n == 128:
                    weight, rows = sel3[:, b, j:j + 4], RES[:, b, j:j + 4, :]
                else:
                    weight, rows = sel3[0:n, :, NT - 1], RES[0:n, :, NT - 1, :]
                y = ytmp[0:n, x_ % 2]
                dve.wait_ge(s("rows_out_ps"), x_ + 1)
                step(tt(y, PS[0:n, 2 * ((x_ + 1) % 2), 0:4 * D].rearrange("q (i d) -> q i d", i=4),
                        w("b2row")[0:n, :].unsqueeze(1).to_broadcast([n, 4, D]), ALU.add))
                dve.wait_ge(s("sel_ready"), members[-1][0] + 1)
                step(tt(y, y, weight.unsqueeze(2).to_broadcast([n, 4, D]), ALU.mult))
                dve.wait_ge(s("resid_ev"), len(RESID))
                tt(rows, y, rows, ALU.add).then_inc(s("rows_ready"), 1)

            for b in range(B):
                dve.wait_ge(s("wcol_ev"), b + 1)
                dve.wait_ge(s("wrow_ev"), NG * (b + 1))
                for j in range(NT):
                    t0, n = j * 128, (128 if j < NT - 1 else LAST)
                    x_ = b * NT + j
                    if x_ >= 3:
                        dve.wait_ge(s("rank_ps"), x_ - 2)
                    stt(beats[x_ % 3][0:n, t0:S], wrow[b][0:n, t0:S], wcol[0:n, b, j:j + 1], later[0:n, 0:S - t0], ALU.is_le,
                        ALU.mult, accum_out=lost[0:n, x_:x_ + 1]).then_inc(s("beats_ready"), 1)
                    if b and j == 1:
                        select(b - 1)
                    if b and j == 4:
                        rows_of(2 * (b - 1))
                    if b and j == 7:
                        rows_of(2 * (b - 1) + 1)
            select(B - 1)
            for x_ in range(2 * (B - 1), len(ROWS)):
                rows_of(x_)


def pack(inputs):
    f = {k: np.asarray(v) for k, v in inputs.items()}
    z = np.float32

    def diag2(a):
        o = np.zeros((2 * a.shape[0], 2 * a.shape[1]), z)
        o[:a.shape[0], :a.shape[1]] = a
        o[a.shape[0]:, a.shape[1]:] = a
        return o

    def twice(a):
        return np.concatenate([a, a], 0)

    def rows(a):
        o = np.zeros((128, a.shape[1]), z)
        o[:a.shape[0]] = a
        return o

    def wide(a):
        return np.ascontiguousarray(rows(a.T).T)

    def column(v):
        return rows(v.reshape(-1, 1))

    wg, bg = f["L0_attn_Wg"], f["L0_attn_bg"]
    xp = f["L1_attn_W_xproj"]
    xB, xC = xp[DTR:DTR + DS].T, xp[DTR + DS:].T
    wout = np.zeros((128, 2, 2, 64), z)
    wr = np.zeros((2, 64, 2, 128), z)
    for i in range(2):
        wout[:, i, i, :] = f["L1_attn_W_out"].T
        wr[i, :, i, :] = f["L1_ffn_wr"]
    idx = np.arange(128)
    w2 = f["L1_ffn_w2"]
    parts = {
        "Wq": diag2(f["L0_attn_Wq"]), "Wk": diag2(f["L0_attn_Wk"]), "Wv": diag2(f["L0_attn_Wv"]),
        "Wi": diag2(wg[:, 0:D]), "Wf": diag2(wg[:, D:2 * D]), "Wo": diag2(wg[:, 2 * D:]),
        "Wr": twice(f["L0_ffn_Wr"]), "ebias": rows(np.tile(f["L0_ffn_bo"], (3, 2))),
        "Win": diag2(f["L1_attn_W_in"].T), "XB": np.concatenate([xB] * 4, 1), "XC": np.concatenate([xC] * 4, 1),
        "XD": wide(xp[0:DTR].T), "WdtT": rows(f["L1_attn_W_dt"].T), "WoutT": wout.reshape(128, 256),
        "FF1": wide(diag2(f["L1_attn_W_ff1"].T)), "FF2": rows(diag2(f["L1_attn_W_ff2"].T)),
        "wr": wr.reshape(128, 256), "w1": diag2(f["L1_ffn_w1"]), "w2": np.concatenate([w2[0:128], w2[128:]], 1),
        "ident": np.eye(128, dtype=z), "ones": diag2(np.ones((64, 64), z)),
        "cmask": (idx[:, None] // L % HC == np.arange(HC)[None]).astype(z),
        "hmask": (idx[:, None] // 64 == np.arange(2)[None]).astype(z),
        "eyes": np.concatenate([np.eye(DS, dtype=z) * (i != 1) for i in range(4)], 0),
        "eyes8": ((idx[:, None] % E == np.arange(E)[None]) & (idx[:, None] < 3 * E)).astype(z),
        "after": (idx[None] > idx[:, None]).astype(z),
        "order": (KEEP - (S - 1 - (idx[:, None] + 128 * np.arange(NT)[None]))).astype(z),
        "b2row": np.tile(f["L1_ffn_b2"], (128, 1)), "brow": np.tile(f["L0_ffn_br"], (128, 1)),
        "A_log": f["L1_attn_A_log"], "conv_w": f["L1_attn_conv_w"],
    }
    two = {"bq": f["L0_attn_bq"], "bk": f["L0_attn_bk"], "bv": f["L0_attn_bv"], "bi": bg[0:D], "bf": bg[D:2 * D],
           "bo": bg[2 * D:], "ib": f["L0_attn_input_bias"], "ns": f["L0_attn_norm_scale"],
           "ff1b": f["L1_attn_b_ff1"], "ff2b": f["L1_attn_b_ff2"], "br": np.tile(f["L1_ffn_br"], 64)}
    one = {"conv_b": f["L1_attn_conv_b"], "b_dt": f["L1_attn_b_dt"], "Dm": f["L1_attn_D"],
           "b1a": f["L1_ffn_b1"][0:128], "b1b": f["L1_ffn_b1"][128:]}
    parts["cols"] = np.concatenate([column(np.concatenate([two[n]] * 2) if n in two else one[n]) for n in COLS], 1)
    wts = np.concatenate([parts[n] for n, _ in WEIGHTS], 1)
    wexp = np.concatenate([diag2(f[f"L0_ffn_{n}"][e]) for n in ("W1", "W2", "Wo") for e in range(E)], 1)
    bn = np.concatenate([twice(f[f"L0_ffn_{n}"].T) for n in BN], 1)
    t, fr = np.arange(PATCH), np.arange(NF)
    ang = 2 * np.pi * np.outer(fr, t) / PATCH
    dft = (np.concatenate([np.cos(ang), -np.sin(ang)], 0) / np.sqrt(PATCH)).astype(z)
    wo = np.zeros((NOG * OG, 2 * NF, 2, C), z)
    wo[0:D] = f["L0_tok_W"].reshape(D, 2 * NF, 1, C)
    wd = np.zeros((128, NOG * 128 + OG * PATCH), z)
    wd[0:OG * 2 * NF, 0:NOG * 128] = wo.reshape(NOG, OG * 2 * NF, 128).transpose(1, 0, 2).reshape(OG * 2 * NF, NOG * 128)
    for i in range(OG):
        wd[i * 2 * NF:(i + 1) * 2 * NF, NOG * 128 + i * PATCH:NOG * 128 + (i + 1) * PATCH] = dft
    return {"x": f["x"], "txt": f["txt"], "wdft": wd, "wts": wts, "wexp": wexp, "bn": bn}


def kernel(**inputs):
    import concourse.bacc as bacc
    from concourse.bass_utils import run_bass_kernel_spmd

    nc = bacc.Bacc("TRN2", target_bir_lowering=False, num_devices=1)
    arrays = {k: np.ascontiguousarray(v) for k, v in pack(inputs).items()}
    args = {k: nc.dram_tensor(f"in_{k}", a.shape, mybir.dt.from_np(a.dtype), kind="ExternalInput").ap()
            for k, a in arrays.items()}
    out = nc.dram_tensor("out_h", (B, S, D), F32, kind="ExternalOutput").ap()
    build(nc, out=out, **args)
    r = run_bass_kernel_spmd(nc, [{f"in_{k}": a for k, a in arrays.items()}], core_ids=[0])
    return r.results[0]["out_h"]
```
